# Optimizing a Trainium2 kernel written in Bass

```python
import numpy as np
import jax
import jax.numpy as jnp

def _softmax(x, axis=-1):
    return jax.nn.softmax(x, axis=axis)

def _gelu(x):
    return jax.nn.gelu(x, approximate=True)

def _silu(x):
    return jax.nn.silu(x)

def _sigmoid(x):
    return jax.nn.sigmoid(x)

def _layernorm(x, axis=-1, eps=1e-05):
    m = jnp.mean(x, axis=axis, keepdims=True)
    v = jnp.var(x, axis=axis, keepdims=True)
    return (x - m) / jnp.sqrt(v + eps)

def _scatter_add(tgt, idx, src, axis=0):
    return tgt.at[idx].add(src)

def _segment_sum(src, seg, n):
    return jax.ops.segment_sum(src, seg, n)
kernel_name = 'mk_seq_postln_d4_jaxref_r8_effabf'

def setup_inputs(seed: int=0):
    np.random.seed(seed)
    _w = jnp.asarray

    def _L0_attn_setup():
        import jax, jax.numpy as jnp
        import numpy as np
        B, S, D, H, L = (4, 512, 128, 128, 2)
        LOG_HALF = float(np.log(0.5))

        def _xavier(key, out_f, in_f):
            lim = np.sqrt(6.0 / (in_f + out_f))
            return jax.random.uniform(key, (out_f, in_f), jnp.float32, -lim, lim)

        def _log_g(x):
            return jnp.where(x >= 0, jnp.log(jax.nn.relu(x) + 0.5), -jax.nn.softplus(-x))

        def _mingru_train(x, Wz, bz, Wh, bh):
            k = jnp.einsum('bsi,hi->bsh', x, Wz) + bz
            log_z = -jax.nn.softplus(-k)
            log_coeffs = -jax.nn.softplus(k)
            log_tilde_h = _log_g(jnp.einsum('bsi,hi->bsh', x, Wh) + bh)
            b = x.shape[0]
            log_h0 = jnp.full((b, 1, log_z.shape[-1]), LOG_HALF, log_z.dtype)
            log_values = jnp.concatenate([log_h0, log_z + log_tilde_h], axis=1)
            a_star = jnp.pad(jnp.cumsum(log_coeffs, axis=1), ((0, 0), (1, 0), (0, 0)))
            log_h = a_star + jax.lax.cumlogsumexp(log_values - a_star, axis=1)
            return jnp.exp(log_h)[:, 1:]

        def _reference_tuple_inner(x, Wz0, bz0, Wh0, bh0, Wz1, bz1, Wh1, bh1):
            h1 = _mingru_train(x, Wz0, bz0, Wh0, bh0)
            h2 = _mingru_train(h1, Wz1, bz1, Wh1, bh1)
            h_n = jnp.stack([h1[:, -1, :], h2[:, -1, :]], axis=0)
            return (h2, h_n)
        key = jax.random.key(seed)
        ks = jax.random.split(key, 5)
        x = jax.random.normal(ks[0], (B, S, D), jnp.float32)
        return {'x': x, 'Wz0': _xavier(ks[1], H, D), 'bz0': jnp.zeros((H,), jnp.float32), 'Wh0': _xavier(ks[2], H, D), 'bh0': jnp.zeros((H,), jnp.float32), 'Wz1': _xavier(ks[3], H, H), 'bz1': jnp.zeros((H,), jnp.float32), 'Wh1': _xavier(ks[4], H, H), 'bh1': jnp.zeros((H,), jnp.float32)}
    _L0_attn_in = _L0_attn_setup()

    def _L0_ffn_setup():
        import jax, jax.numpy as jnp
        import numpy as np
        B, T, D = (8, 512, 128)
        NUM_SLOTS = 64
        TOP_K = 8
        DQ = D // 4
        DH = D // 2

        def _forward(x, slot_init, w1, b1, w2, b2, tau, Wih, Whh, bih, bhh, wq, bq, wk, bk, wv, bv, ln_g, ln_b, wvp, bvp, wo, bo):
            Bx, Tx, Dx = x.shape
            S = jnp.broadcast_to(slot_init[None], (Bx, NUM_SLOTS, Dx)).astype(x.dtype)
            slot_mean = jnp.broadcast_to(S.mean(axis=1, keepdims=True), (Bx, Tx, Dx))
            ctx = jnp.concatenate([x, slot_mean], axis=-1)
            h = jax.nn.gelu(ctx @ w1 + b1, approximate=False)
            route_logits = (h @ w2 + b2) / (jnp.abs(tau) + 0.1)
            topk_vals, topk_idx = jax.lax.top_k(route_logits, TOP_K)
            topk_w = jax.nn.softmax(topk_vals, axis=-1)
            alpha = (jax.nn.one_hot(topk_idx, NUM_SLOTS, dtype=x.dtype) * topk_w[..., None]).sum(axis=-2)
            slot_input = jnp.einsum('bts,btd->bsd', alpha, x)
            denom = alpha.sum(axis=1) + 1e-08
            si = slot_input / denom[..., None]
            gi = si @ Wih.T + bih
            gh = S @ Whh.T + bhh
            i_r, i_z, i_n = jnp.split(gi, 3, axis=-1)
            h_r, h_z, h_n = jnp.split(gh, 3, axis=-1)
            r = jax.nn.sigmoid(i_r + h_r)
            z = jax.nn.sigmoid(i_z + h_z)
            n = jnp.tanh(i_n + r * h_n)
            S_new = (1.0 - z) * n + z * S
            q = S_new @ wq + bq
            k = S_new @ wk + bk
            v = S_new @ wv + bv
            scale = DQ ** (-0.5)
            attn = jax.nn.softmax(jnp.einsum('bsq,btq->bst', q, k) * scale, axis=-1)
            S_comm = jnp.einsum('bst,btd->bsd', attn, v)
            y = S_new + S_comm
            mu = y.mean(axis=-1, keepdims=True)
            var = y.var(axis=-1, keepdims=True)
            y = (y - mu) * jax.lax.rsqrt(var + 1e-05) * ln_g + ln_b
            slot_values = y @ wvp + bvp
            out = jnp.einsum('bts,bsd->btd', alpha, slot_values)
            return out @ wo + bo
        key = jax.random.key(seed)
        ks = jax.random.split(key, 24)
        n = lambda k, shp, s=0.02: jax.random.normal(k, shp, dtype=jnp.float32) * s
        return {'x': jax.random.normal(ks[0], (B, T, D), dtype=jnp.float32), 'slot_init': n(ks[1], (NUM_SLOTS, D)), 'w1': n(ks[2], (2 * D, DH)), 'b1': jnp.zeros((DH,)), 'w2': n(ks[3], (DH, NUM_SLOTS)), 'b2': jnp.zeros((NUM_SLOTS,)), 'tau': jnp.ones((1,)), 'Wih': n(ks[4], (3 * D, D)), 'Whh': n(ks[5], (3 * D, D)), 'bih': jnp.zeros((3 * D,)), 'bhh': jnp.zeros((3 * D,)), 'wq': n(ks[6], (D, DQ)), 'bq': jnp.zeros((DQ,)), 'wk': n(ks[7], (D, DQ)), 'bk': jnp.zeros((DQ,)), 'wv': n(ks[8], (D, D)), 'bv': jnp.zeros((D,)), 'ln_g': jnp.ones((D,)), 'ln_b': jnp.zeros((D,)), 'wvp': n(ks[9], (D, D)), 'bvp': jnp.zeros((D,)), 'wo': n(ks[10], (D, D)), 'bo': jnp.zeros((D,))}
    _L0_ffn_in = _L0_ffn_setup()

    def _L1_attn_setup():
        import jax, jax.numpy as jnp
        import numpy as np
        import math
        D_MODEL = 128
        N_HEADS = 16
        HEAD_DIM = D_MODEL // N_HEADS
        FACTOR = 5
        B, L = (4, 512)
        key = jax.random.key(seed)
        ks = jax.random.split(key, 10)
        s = 1.0 / math.sqrt(D_MODEL)
        U = min(FACTOR * int(math.ceil(math.log(L))), L)
        return {'x': jax.random.normal(ks[0], (B, L, D_MODEL), dtype=jnp.float32), 'Wq': jax.random.normal(ks[1], (D_MODEL, D_MODEL), dtype=jnp.float32) * s, 'bq': jnp.zeros((D_MODEL,), jnp.float32), 'Wk': jax.random.normal(ks[2], (D_MODEL, D_MODEL), dtype=jnp.float32) * s, 'bk': jnp.zeros((D_MODEL,), jnp.float32), 'Wv': jax.random.normal(ks[3], (D_MODEL, D_MODEL), dtype=jnp.float32) * s, 'bv': jnp.zeros((D_MODEL,), jnp.float32), 'Wo': jax.random.normal(ks[4], (D_MODEL, D_MODEL), dtype=jnp.float32) * s, 'bo': jnp.zeros((D_MODEL,), jnp.float32), 'sample_idx': jax.random.permutation(ks[5], L)[:U].astype(jnp.int32)}
    _L1_attn_in = _L1_attn_setup()

    def _L1_ffn_setup():
        import jax, jax.numpy as jnp
        import numpy as np
        D_MODEL = 128
        HIDDEN = 512
        N_ROUTING = 2
        key = jax.random.key(seed)
        ks = jax.random.split(key, 10)
        s = 0.02
        x = jax.random.normal(ks[0], (4, 512, D_MODEL), dtype=jnp.float32)
        gate_w = jax.random.normal(ks[1], (N_ROUTING, D_MODEL), dtype=jnp.float32) * s
        w1 = jax.random.normal(ks[2], (N_ROUTING, D_MODEL, HIDDEN), dtype=jnp.float32) * s
        b1 = jax.random.normal(ks[3], (N_ROUTING, HIDDEN), dtype=jnp.float32) * s
        w2 = jax.random.normal(ks[4], (N_ROUTING, HIDDEN, D_MODEL), dtype=jnp.float32) * s
        b2 = jax.random.normal(ks[5], (N_ROUTING, D_MODEL), dtype=jnp.float32) * s
        sw1 = jax.random.normal(ks[6], (D_MODEL, HIDDEN), dtype=jnp.float32) * s
        sb1 = jax.random.normal(ks[7], (HIDDEN,), dtype=jnp.float32) * s
        sw2 = jax.random.normal(ks[8], (HIDDEN, D_MODEL), dtype=jnp.float32) * s
        sb2 = jax.random.normal(ks[9], (D_MODEL,), dtype=jnp.float32) * s
        return {'x': x, 'gate_w': gate_w, 'w1': w1, 'b1': b1, 'w2': w2, 'b2': b2, 'sw1': sw1, 'sb1': sb1, 'sw2': sw2, 'sb2': sb2}
    _L1_ffn_in = _L1_ffn_setup()

    def _L2_attn_setup():
        import math
        import jax, jax.numpy as jnp
        import numpy as np
        NHEAD = 16
        HEAD_DIM = 64
        D_MODEL = 128
        B, T = (2, 512)

        def _cosformer(x, Wq, bq, Wk, bk, Wv, bv, Wo, bo):
            Bsz, Tlen, _ = x.shape
            H, dh = (NHEAD, HEAD_DIM)
            Q = (x @ Wq + bq).reshape(Bsz, Tlen, H, dh)
            K = (x @ Wk + bk).reshape(Bsz, Tlen, H, dh)
            V = (x @ Wv + bv).reshape(Bsz, Tlen, H, dh)
            Qp = jax.nn.relu(Q)
            Kp = jax.nn.relu(K)
            angles = math.pi / (2.0 * Tlen) * jnp.arange(Tlen, dtype=jnp.float32)
            cosw = jnp.cos(angles)[None, :, None, None]
            sinw = jnp.sin(angles)[None, :, None, None]
            Qc, Qs = (Qp * cosw, Qp * sinw)
            Kc, Ks = (Kp * cosw, Kp * sinw)
            tm = lambda a: jnp.moveaxis(a, 1, 0)
            Qc, Qs, Kc, Ks, Vt = (tm(Qc), tm(Qs), tm(Kc), tm(Ks), tm(V))
            S0 = jnp.zeros((Bsz, H, dh, dh), dtype=x.dtype)
            z0 = jnp.zeros((Bsz, H, dh), dtype=x.dtype)

            def step(carry, inp):
                S_cos, S_sin, z_cos, z_sin = carry
                qc, qs, kc, ks_, v = inp
                S_cos = S_cos + kc[..., :, None] * v[..., None, :]
                S_sin = S_sin + ks_[..., :, None] * v[..., None, :]
                z_cos = z_cos + kc
                z_sin = z_sin + ks_
                num = jnp.einsum('bhi,bhij->bhj', qc, S_cos) + jnp.einsum('bhi,bhij->bhj', qs, S_sin)
                den = jnp.sum(qc * z_cos + qs * z_sin, axis=-1)
                den = jnp.maximum(den, 1e-06)[..., None]
                return ((S_cos, S_sin, z_cos, z_sin), num / den)
            _, out = jax.lax.scan(step, (S0, S0, z0, z0), (Qc, Qs, Kc, Ks, Vt))
            out = jnp.moveaxis(out, 0, 1).reshape(Bsz, Tlen, H * dh)
            return out @ Wo + bo
        key = jax.random.key(seed)
        ks = jax.random.split(key, 9)
        HD = NHEAD * HEAD_DIM
        s_in = 1.0 / math.sqrt(D_MODEL)
        s_out = 1.0 / math.sqrt(HD)
        return {'x': jax.random.normal(ks[0], (B, T, D_MODEL), dtype=jnp.float32), 'Wq': jax.random.normal(ks[1], (D_MODEL, HD), dtype=jnp.float32) * s_in, 'bq': jnp.zeros((HD,), dtype=jnp.float32), 'Wk': jax.random.normal(ks[2], (D_MODEL, HD), dtype=jnp.float32) * s_in, 'bk': jnp.zeros((HD,), dtype=jnp.float32), 'Wv': jax.random.normal(ks[3], (D_MODEL, HD), dtype=jnp.float32) * s_in, 'bv': jnp.zeros((HD,), dtype=jnp.float32), 'Wo': jax.random.normal(ks[4], (HD, D_MODEL), dtype=jnp.float32) * s_out, 'bo': jnp.zeros((D_MODEL,), dtype=jnp.float32)}
    _L2_attn_in = _L2_attn_setup()

    def _L2_ffn_setup():
        import jax, jax.numpy as jnp
        import numpy as np
        E, H, I, K = (8, 128, 256, 2)
        B, S = (4, 256)
        key = jax.random.key(seed)
        k1, k2, k3, k4 = jax.random.split(key, 4)
        x = jax.random.normal(k1, (B, S, H), dtype=jnp.float32)
        router_w = jax.random.uniform(k2, (E, H), dtype=jnp.float32, minval=-1.0, maxval=1.0) / np.sqrt(H).astype(np.float32)
        w13 = jax.random.normal(k3, (E, H, 2 * I), dtype=jnp.float32) * 0.02
        w2 = jax.random.normal(k4, (E, I, H), dtype=jnp.float32) * 0.02
        return {'x': x, 'router_w': router_w, 'w13': w13, 'w2': w2}
    _L2_ffn_in = _L2_ffn_setup()

    def _L3_attn_setup():
        import jax, jax.numpy as jnp
        import numpy as np
        from jax import lax
        B, L, D = (2, 256, 128)
        E, N, D_DELTA, D_CONV = (256, 16, 64, 4)
        EPS = 1e-05
        key = jax.random.key(seed)
        ks = jax.random.split(key, 16)
        s = lambda fan_in: 1.0 / np.sqrt(fan_in)
        return {'resid': jax.random.normal(ks[0], (B, L, D), jnp.float32), 'norm_w': jnp.ones((D,), jnp.float32), 'skip_w': jax.random.normal(ks[1], (E, D), jnp.float32) * s(D), 'in_w': jax.random.normal(ks[2], (E, D), jnp.float32) * s(D), 'conv_w': jax.random.normal(ks[3], (E, 1, D_CONV), jnp.float32) * s(D_CONV), 'conv_b': jnp.zeros((E,), jnp.float32), 'wd1': jax.random.normal(ks[4], (D_DELTA, E), jnp.float32) * s(E), 'wd2': jax.random.normal(ks[5], (E, D_DELTA), jnp.float32) * s(D_DELTA), 'wd2_b': jnp.zeros((E,), jnp.float32), 'wb': jax.random.normal(ks[6], (N, E), jnp.float32) * s(E), 'wc': jax.random.normal(ks[7], (N, E), jnp.float32) * s(E), 'A_log': jnp.log(jax.random.uniform(ks[8], (E, N), jnp.float32, 0.5, 1.5)), 'W_D': jnp.ones((E,), jnp.float32), 'out_w': jax.random.normal(ks[9], (D, E), jnp.float32) * s(E)}
    _L3_attn_in = _L3_attn_setup()

    def _L3_ffn_setup():
        import jax, jax.numpy as jnp
        import numpy as np
        TOP_P = 0.8
        B, T, H, F, E = (2, 256, 128, 512, 8)
        key = jax.random.key(seed)
        k0, k1, k2, k3 = jax.random.split(key, 4)
        x = jax.random.normal(k0, (B, T, H), jnp.float32)
        Wr = jax.random.normal(k1, (H, E), jnp.float32) * 0.02
        br = jnp.zeros((E,), jnp.float32)
        W1 = jax.random.normal(k2, (E, H, F), jnp.float32) * 0.02
        b1 = jnp.zeros((E, F), jnp.float32)
        W2 = jax.random.normal(k3, (E, F, H), jnp.float32) * 0.02
        b2 = jnp.zeros((E, H), jnp.float32)
        return {'x': x, 'Wr': Wr, 'br': br, 'W1': W1, 'b1': b1, 'W2': W2, 'b2': b2}
    _L3_ffn_in = _L3_ffn_setup()
    _d = {'L0_attn_x': _L0_attn_in['x'], 'L0_attn_Wz0': _L0_attn_in['Wz0'], 'L0_attn_bz0': _L0_attn_in['bz0'], 'L0_attn_Wh0': _L0_attn_in['Wh0'], 'L0_attn_bh0': _L0_attn_in['bh0'], 'L0_attn_Wz1': _L0_attn_in['Wz1'], 'L0_attn_bz1': _L0_attn_in['bz1'], 'L0_attn_Wh1': _L0_attn_in['Wh1'], 'L0_attn_bh1': _L0_attn_in['bh1'], 'L0_ffn_slot_init': _L0_ffn_in['slot_init'], 'L0_ffn_w1': _L0_ffn_in['w1'], 'L0_ffn_b1': _L0_ffn_in['b1'], 'L0_ffn_w2': _L0_ffn_in['w2'], 'L0_ffn_b2': _L0_ffn_in['b2'], 'L0_ffn_tau': _L0_ffn_in['tau'], 'L0_ffn_Wih': _L0_ffn_in['Wih'], 'L0_ffn_Whh': _L0_ffn_in['Whh'], 'L0_ffn_bih': _L0_ffn_in['bih'], 'L0_ffn_bhh': _L0_ffn_in['bhh'], 'L0_ffn_wq': _L0_ffn_in['wq'], 'L0_ffn_bq': _L0_ffn_in['bq'], 'L0_ffn_wk': _L0_ffn_in['wk'], 'L0_ffn_bk': _L0_ffn_in['bk'], 'L0_ffn_wv': _L0_ffn_in['wv'], 'L0_ffn_bv': _L0_ffn_in['bv'], 'L0_ffn_ln_g': _L0_ffn_in['ln_g'], 'L0_ffn_ln_b': _L0_ffn_in['ln_b'], 'L0_ffn_wvp': _L0_ffn_in['wvp'], 'L0_ffn_bvp': _L0_ffn_in['bvp'], 'L0_ffn_wo': _L0_ffn_in['wo'], 'L0_ffn_bo': _L0_ffn_in['bo'], 'L1_attn_Wq': _L1_attn_in['Wq'], 'L1_attn_bq': _L1_attn_in['bq'], 'L1_attn_Wk': _L1_attn_in['Wk'], 'L1_attn_bk': _L1_attn_in['bk'], 'L1_attn_Wv': _L1_attn_in['Wv'], 'L1_attn_bv': _L1_attn_in['bv'], 'L1_attn_Wo': _L1_attn_in['Wo'], 'L1_attn_bo': _L1_attn_in['bo'], 'L1_attn_sample_idx': _L1_attn_in['sample_idx'], 'L1_ffn_gate_w': _L1_ffn_in['gate_w'], 'L1_ffn_w1': _L1_ffn_in['w1'], 'L1_ffn_b1': _L1_ffn_in['b1'], 'L1_ffn_w2': _L1_ffn_in['w2'], 'L1_ffn_b2': _L1_ffn_in['b2'], 'L1_ffn_sw1': _L1_ffn_in['sw1'], 'L1_ffn_sb1': _L1_ffn_in['sb1'], 'L1_ffn_sw2': _L1_ffn_in['sw2'], 'L1_ffn_sb2': _L1_ffn_in['sb2'], 'L2_attn_Wq': _L2_attn_in['Wq'], 'L2_attn_bq': _L2_attn_in['bq'], 'L2_attn_Wk': _L2_attn_in['Wk'], 'L2_attn_bk': _L2_attn_in['bk'], 'L2_attn_Wv': _L2_attn_in['Wv'], 'L2_attn_bv': _L2_attn_in['bv'], 'L2_attn_Wo': _L2_attn_in['Wo'], 'L2_attn_bo': _L2_attn_in['bo'], 'L2_ffn_router_w': _L2_ffn_in['router_w'], 'L2_ffn_w13': _L2_ffn_in['w13'], 'L2_ffn_w2': _L2_ffn_in['w2'], 'L3_attn_norm_w': _L3_attn_in['norm_w'], 'L3_attn_skip_w': _L3_attn_in['skip_w'], 'L3_attn_in_w': _L3_attn_in['in_w'], 'L3_attn_conv_w': _L3_attn_in['conv_w'], 'L3_attn_conv_b': _L3_attn_in['conv_b'], 'L3_attn_wd1': _L3_attn_in['wd1'], 'L3_attn_wd2': _L3_attn_in['wd2'], 'L3_attn_wd2_b': _L3_attn_in['wd2_b'], 'L3_attn_wb': _L3_attn_in['wb'], 'L3_attn_wc': _L3_attn_in['wc'], 'L3_attn_A_log': _L3_attn_in['A_log'], 'L3_attn_W_D': _L3_attn_in['W_D'], 'L3_attn_out_w': _L3_attn_in['out_w'], 'L3_ffn_Wr': _L3_ffn_in['Wr'], 'L3_ffn_br': _L3_ffn_in['br'], 'L3_ffn_W1': _L3_ffn_in['W1'], 'L3_ffn_b1': _L3_ffn_in['b1'], 'L3_ffn_W2': _L3_ffn_in['W2'], 'L3_ffn_b2': _L3_ffn_in['b2']}
    _x0 = _d['L0_attn_x']
    _d['L0_attn_x'] = jax.random.normal(jax.random.fold_in(jax.random.key(seed), 1), (4, 1024, 128), dtype=_x0.dtype)
    del _x0
    return _d

def reference(L0_attn_x, L0_attn_Wz0, L0_attn_bz0, L0_attn_Wh0, L0_attn_bh0, L0_attn_Wz1, L0_attn_bz1, L0_attn_Wh1, L0_attn_bh1, L0_ffn_slot_init, L0_ffn_w1, L0_ffn_b1, L0_ffn_w2, L0_ffn_b2, L0_ffn_tau, L0_ffn_Wih, L0_ffn_Whh, L0_ffn_bih, L0_ffn_bhh, L0_ffn_wq, L0_ffn_bq, L0_ffn_wk, L0_ffn_bk, L0_ffn_wv, L0_ffn_bv, L0_ffn_ln_g, L0_ffn_ln_b, L0_ffn_wvp, L0_ffn_bvp, L0_ffn_wo, L0_ffn_bo, L1_attn_Wq, L1_attn_bq, L1_attn_Wk, L1_attn_bk, L1_attn_Wv, L1_attn_bv, L1_attn_Wo, L1_attn_bo, L1_attn_sample_idx, L1_ffn_gate_w, L1_ffn_w1, L1_ffn_b1, L1_ffn_w2, L1_ffn_b2, L1_ffn_sw1, L1_ffn_sb1, L1_ffn_sw2, L1_ffn_sb2, L2_attn_Wq, L2_attn_bq, L2_attn_Wk, L2_attn_bk, L2_attn_Wv, L2_attn_bv, L2_attn_Wo, L2_attn_bo, L2_ffn_router_w, L2_ffn_w13, L2_ffn_w2, L3_attn_norm_w, L3_attn_skip_w, L3_attn_in_w, L3_attn_conv_w, L3_attn_conv_b, L3_attn_wd1, L3_attn_wd2, L3_attn_wd2_b, L3_attn_wb, L3_attn_wc, L3_attn_A_log, L3_attn_W_D, L3_attn_out_w, L3_ffn_Wr, L3_ffn_br, L3_ffn_W1, L3_ffn_b1, L3_ffn_W2, L3_ffn_b2):

    def _L0_attn_ref(x, Wz0, bz0, Wh0, bh0, Wz1, bz1, Wh1, bh1):
        import jax, jax.numpy as jnp
        import numpy as np
        B, S, D, H, L = (4, 512, 128, 128, 2)
        LOG_HALF = float(np.log(0.5))

        def _xavier(key, out_f, in_f):
            lim = np.sqrt(6.0 / (in_f + out_f))
            return jax.random.uniform(key, (out_f, in_f), jnp.float32, -lim, lim)

        def _log_g(x):
            return jnp.where(x >= 0, jnp.log(jax.nn.relu(x) + 0.5), -jax.nn.softplus(-x))

        def _mingru_train(x, Wz, bz, Wh, bh):
            k = jnp.einsum('bsi,hi->bsh', x, Wz) + bz
            log_z = -jax.nn.softplus(-k)
            log_coeffs = -jax.nn.softplus(k)
            log_tilde_h = _log_g(jnp.einsum('bsi,hi->bsh', x, Wh) + bh)
            b = x.shape[0]
            log_h0 = jnp.full((b, 1, log_z.shape[-1]), LOG_HALF, log_z.dtype)
            log_values = jnp.concatenate([log_h0, log_z + log_tilde_h], axis=1)
            a_star = jnp.pad(jnp.cumsum(log_coeffs, axis=1), ((0, 0), (1, 0), (0, 0)))
            log_h = a_star + jax.lax.cumlogsumexp(log_values - a_star, axis=1)
            return jnp.exp(log_h)[:, 1:]

        def _reference_tuple_inner(x, Wz0, bz0, Wh0, bh0, Wz1, bz1, Wh1, bh1):
            h1 = _mingru_train(x, Wz0, bz0, Wh0, bh0)
            h2 = _mingru_train(h1, Wz1, bz1, Wh1, bh1)
            h_n = jnp.stack([h1[:, -1, :], h2[:, -1, :]], axis=0)
            return (h2, h_n)
        return _reference_tuple_inner(x, Wz0, bz0, Wh0, bh0, Wz1, bz1, Wh1, bh1)[0]

    def _L0_ffn_ref(x, slot_init, w1, b1, w2, b2, tau, Wih, Whh, bih, bhh, wq, bq, wk, bk, wv, bv, ln_g, ln_b, wvp, bvp, wo, bo):
        import jax, jax.numpy as jnp
        import numpy as np
        B, T, D = (8, 512, 128)
        NUM_SLOTS = 64
        TOP_K = 8
        DQ = D // 4
        DH = D // 2

        def _forward(x, slot_init, w1, b1, w2, b2, tau, Wih, Whh, bih, bhh, wq, bq, wk, bk, wv, bv, ln_g, ln_b, wvp, bvp, wo, bo):
            Bx, Tx, Dx = x.shape
            S = jnp.broadcast_to(slot_init[None], (Bx, NUM_SLOTS, Dx)).astype(x.dtype)
            slot_mean = jnp.broadcast_to(S.mean(axis=1, keepdims=True), (Bx, Tx, Dx))
            ctx = jnp.concatenate([x, slot_mean], axis=-1)
            h = jax.nn.gelu(ctx @ w1 + b1, approximate=False)
            route_logits = (h @ w2 + b2) / (jnp.abs(tau) + 0.1)
            topk_vals, topk_idx = jax.lax.top_k(route_logits, TOP_K)
            topk_w = jax.nn.softmax(topk_vals, axis=-1)
            alpha = (jax.nn.one_hot(topk_idx, NUM_SLOTS, dtype=x.dtype) * topk_w[..., None]).sum(axis=-2)
            slot_input = jnp.einsum('bts,btd->bsd', alpha, x)
            denom = alpha.sum(axis=1) + 1e-08
            si = slot_input / denom[..., None]
            gi = si @ Wih.T + bih
            gh = S @ Whh.T + bhh
            i_r, i_z, i_n = jnp.split(gi, 3, axis=-1)
            h_r, h_z, h_n = jnp.split(gh, 3, axis=-1)
            r = jax.nn.sigmoid(i_r + h_r)
            z = jax.nn.sigmoid(i_z + h_z)
            n = jnp.tanh(i_n + r * h_n)
            S_new = (1.0 - z) * n + z * S
            q = S_new @ wq + bq
            k = S_new @ wk + bk
            v = S_new @ wv + bv
            scale = DQ ** (-0.5)
            attn = jax.nn.softmax(jnp.einsum('bsq,btq->bst', q, k) * scale, axis=-1)
            S_comm = jnp.einsum('bst,btd->bsd', attn, v)
            y = S_new + S_comm
            mu = y.mean(axis=-1, keepdims=True)
            var = y.var(axis=-1, keepdims=True)
            y = (y - mu) * jax.lax.rsqrt(var + 1e-05) * ln_g + ln_b
            slot_values = y @ wvp + bvp
            out = jnp.einsum('bts,bsd->btd', alpha, slot_values)
            return out @ wo + bo
        return _forward(x, slot_init, w1, b1, w2, b2, tau, Wih, Whh, bih, bhh, wq, bq, wk, bk, wv, bv, ln_g, ln_b, wvp, bvp, wo, bo)

    def _L1_attn_ref(x, Wq, bq, Wk, bk, Wv, bv, Wo, bo, sample_idx):
        import jax, jax.numpy as jnp
        import numpy as np
        import math
        D_MODEL = 128
        N_HEADS = 16
        HEAD_DIM = D_MODEL // N_HEADS
        FACTOR = 5
        B, L = (4, 512)
        Bv, Lv, _ = x.shape
        scale = HEAD_DIM ** (-0.5)
        U = min(FACTOR * int(math.ceil(math.log(Lv))), Lv)

        def proj(W, b):
            y = jnp.einsum('bld,de->ble', x, W) + b
            return y.reshape(Bv, Lv, N_HEADS, HEAD_DIM).transpose(0, 2, 1, 3)
        Q = proj(Wq, bq)
        K = proj(Wk, bk)
        V = proj(Wv, bv)
        K_sample = K[:, :, sample_idx, :]
        QK_s = jnp.einsum('bhld,bhsd->bhls', Q, K_sample) * scale
        M = QK_s.max(axis=-1) - QK_s.mean(axis=-1)
        _, top_idx = jax.lax.top_k(M, U)
        Q_red = jnp.take_along_axis(Q, top_idx[..., None], axis=2)
        scores = jnp.einsum('bhud,bhld->bhul', Q_red, K) * scale
        attn = jax.nn.softmax(scores, axis=-1)
        out_red = jnp.einsum('bhul,bhld->bhud', attn, V)
        out = jnp.broadcast_to(V.mean(axis=2, keepdims=True), (Bv, N_HEADS, Lv, HEAD_DIM))
        bi = jnp.arange(Bv)[:, None, None]
        hi = jnp.arange(N_HEADS)[None, :, None]
        out = out.at[bi, hi, top_idx].set(out_red)
        out = out.transpose(0, 2, 1, 3).reshape(Bv, Lv, D_MODEL)
        return jnp.einsum('bld,de->ble', out, Wo) + bo

    def _L1_ffn_ref(x, gate_w, w1, b1, w2, b2, sw1, sb1, sw2, sb2):
        import jax, jax.numpy as jnp
        import numpy as np
        D_MODEL = 128
        HIDDEN = 512
        N_ROUTING = 2
        B, S, D = x.shape
        xf = x.reshape(-1, D)
        gate_scores = xf @ gate_w.T
        gate_probs = jax.nn.softmax(gate_scores, axis=-1)
        top1 = jnp.argmax(gate_probs, axis=-1)
        one_hot = jax.nn.one_hot(top1, N_ROUTING, dtype=xf.dtype)
        masked = xf[None, :, :] * one_hot.T[:, :, None]
        h = jax.nn.relu(jnp.einsum('end,edh->enh', masked, w1) + b1[:, None, :])
        expert_out = jnp.einsum('enh,ehd->end', h, w2) + b2[:, None, :]
        routing_output = expert_out.sum(axis=0)
        shared = jax.nn.relu(xf @ sw1 + sb1) @ sw2 + sb2
        return (routing_output + shared).reshape(B, S, D)

    def _L2_attn_ref(x, Wq, bq, Wk, bk, Wv, bv, Wo, bo):
        import math
        import jax, jax.numpy as jnp
        import numpy as np
        NHEAD = 16
        HEAD_DIM = 64
        D_MODEL = 128
        B, T = (2, 512)

        def _cosformer(x, Wq, bq, Wk, bk, Wv, bv, Wo, bo):
            Bsz, Tlen, _ = x.shape
            H, dh = (NHEAD, HEAD_DIM)
            Q = (x @ Wq + bq).reshape(Bsz, Tlen, H, dh)
            K = (x @ Wk + bk).reshape(Bsz, Tlen, H, dh)
            V = (x @ Wv + bv).reshape(Bsz, Tlen, H, dh)
            Qp = jax.nn.relu(Q)
            Kp = jax.nn.relu(K)
            angles = math.pi / (2.0 * Tlen) * jnp.arange(Tlen, dtype=jnp.float32)
            cosw = jnp.cos(angles)[None, :, None, None]
            sinw = jnp.sin(angles)[None, :, None, None]
            Qc, Qs = (Qp * cosw, Qp * sinw)
            Kc, Ks = (Kp * cosw, Kp * sinw)
            tm = lambda a: jnp.moveaxis(a, 1, 0)
            Qc, Qs, Kc, Ks, Vt = (tm(Qc), tm(Qs), tm(Kc), tm(Ks), tm(V))
            S0 = jnp.zeros((Bsz, H, dh, dh), dtype=x.dtype)
            z0 = jnp.zeros((Bsz, H, dh), dtype=x.dtype)

            def step(carry, inp):
                S_cos, S_sin, z_cos, z_sin = carry
                qc, qs, kc, ks_, v = inp
                S_cos = S_cos + kc[..., :, None] * v[..., None, :]
                S_sin = S_sin + ks_[..., :, None] * v[..., None, :]
                z_cos = z_cos + kc
                z_sin = z_sin + ks_
                num = jnp.einsum('bhi,bhij->bhj', qc, S_cos) + jnp.einsum('bhi,bhij->bhj', qs, S_sin)
                den = jnp.sum(qc * z_cos + qs * z_sin, axis=-1)
                den = jnp.maximum(den, 1e-06)[..., None]
                return ((S_cos, S_sin, z_cos, z_sin), num / den)
            _, out = jax.lax.scan(step, (S0, S0, z0, z0), (Qc, Qs, Kc, Ks, Vt))
            out = jnp.moveaxis(out, 0, 1).reshape(Bsz, Tlen, H * dh)
            return out @ Wo + bo
        return _cosformer(x, Wq, bq, Wk, bk, Wv, bv, Wo, bo)

    def _L2_ffn_ref(x, router_w, w13, w2):
        import jax, jax.numpy as jnp
        import numpy as np
        E, H, I, K = (8, 128, 256, 2)
        B, S = (4, 256)
        logits = jnp.einsum('bsh,eh->bse', x, router_w)
        probs = jax.nn.softmax(logits, axis=-1)
        weights, indices = jax.lax.top_k(probs, K)
        weights = weights / (weights.sum(axis=-1, keepdims=True) + 1e-06)
        h13 = jnp.einsum('bsh,ehi->bsei', x, w13)
        gate, up = jnp.split(h13, 2, axis=-1)
        h = jax.nn.silu(gate) * up
        y = jnp.einsum('bsei,eih->bseh', h, w2)
        y_sel = jnp.take_along_axis(y, indices[..., None], axis=2)
        return (y_sel * weights[..., None]).sum(axis=2)

    def _L3_attn_ref(resid, norm_w, skip_w, in_w, conv_w, conv_b, wd1, wd2, wd2_b, wb, wc, A_log, W_D, out_w):
        import jax, jax.numpy as jnp
        import numpy as np
        from jax import lax
        B, L, D = (2, 256, 128)
        E, N, D_DELTA, D_CONV = (256, 16, 64, 4)
        EPS = 1e-05
        Bt, Lt, Dt = resid.shape
        x = resid * lax.rsqrt(jnp.mean(resid * resid, -1, keepdims=True) + EPS) * norm_w
        skip = x @ skip_w.T
        xe = x @ in_w.T
        xt = xe.transpose(0, 2, 1)
        xc = lax.conv_general_dilated(xt, conv_w, window_strides=(1,), padding=[(D_CONV - 1, 0)], feature_group_count=conv_w.shape[0])
        xc = xc + conv_b[None, :, None]
        xs = jax.nn.silu(xc.transpose(0, 2, 1))
        delta = jax.nn.softplus(xs @ wd1.T @ wd2.T + wd2_b)
        A = -jnp.exp(A_log)
        Bm = xs @ wb.T
        Cm = xs @ wc.T

        def step(h, inp):
            d_l, b_l, c_l, x_l = inp
            h = jnp.exp(d_l[:, :, None] * A) * h + (d_l * x_l)[:, :, None] * b_l[:, None, :]
            y_l = jnp.einsum('ben,bn->be', h, c_l)
            return (h, y_l)
        h0 = jnp.zeros((Bt, xs.shape[-1], A.shape[-1]), xs.dtype)
        _, ys = lax.scan(step, h0, (delta.transpose(1, 0, 2), Bm.transpose(1, 0, 2), Cm.transpose(1, 0, 2), xs.transpose(1, 0, 2)))
        y = ys.transpose(1, 0, 2)
        y = y + xs * W_D
        y = y * jax.nn.silu(skip)
        y = y @ out_w.T
        return resid + y

    def _L3_ffn_ref(x, Wr, br, W1, b1, W2, b2):
        import jax, jax.numpy as jnp
        import numpy as np
        TOP_P = 0.8
        B, T, H, F, E = (2, 256, 128, 512, 8)
        probs = jax.nn.softmax(x @ Wr + br, axis=-1)
        sorted_idx = jnp.argsort(-probs, axis=-1)
        sorted_probs = jnp.take_along_axis(probs, sorted_idx, axis=-1)
        cum = jnp.cumsum(sorted_probs, axis=-1)
        mask = cum < TOP_P
        mask = mask.at[..., 0].set(True)
        inv = jnp.argsort(sorted_idx, axis=-1)
        keep = jnp.take_along_axis(mask, inv, axis=-1)
        gate = probs * keep
        h = jax.nn.relu(jnp.einsum('bth,ehf->betf', x, W1) + b1[None, :, None, :])
        y = jnp.einsum('betf,efh->beth', h, W2) + b2[None, :, None, :]
        return jnp.einsum('bte,beth->bth', gate, y)
    x = L0_attn_x
    x = _layernorm(x + _L0_attn_ref(x, L0_attn_Wz0, L0_attn_bz0, L0_attn_Wh0, L0_attn_bh0, L0_attn_Wz1, L0_attn_bz1, L0_attn_Wh1, L0_attn_bh1), axis=-1)
    x = _layernorm(x + _L0_ffn_ref(x, L0_ffn_slot_init, L0_ffn_w1, L0_ffn_b1, L0_ffn_w2, L0_ffn_b2, L0_ffn_tau, L0_ffn_Wih, L0_ffn_Whh, L0_ffn_bih, L0_ffn_bhh, L0_ffn_wq, L0_ffn_bq, L0_ffn_wk, L0_ffn_bk, L0_ffn_wv, L0_ffn_bv, L0_ffn_ln_g, L0_ffn_ln_b, L0_ffn_wvp, L0_ffn_bvp, L0_ffn_wo, L0_ffn_bo), axis=-1)
    x = _layernorm(x + _L1_attn_ref(x, L1_attn_Wq, L1_attn_bq, L1_attn_Wk, L1_attn_bk, L1_attn_Wv, L1_attn_bv, L1_attn_Wo, L1_attn_bo, L1_attn_sample_idx), axis=-1)
    x = _layernorm(x + _L1_ffn_ref(x, L1_ffn_gate_w, L1_ffn_w1, L1_ffn_b1, L1_ffn_w2, L1_ffn_b2, L1_ffn_sw1, L1_ffn_sb1, L1_ffn_sw2, L1_ffn_sb2), axis=-1)
    x = _layernorm(x + _L2_attn_ref(x, L2_attn_Wq, L2_attn_bq, L2_attn_Wk, L2_attn_bk, L2_attn_Wv, L2_attn_bv, L2_attn_Wo, L2_attn_bo), axis=-1)
    x = _layernorm(x + _L2_ffn_ref(x, L2_ffn_router_w, L2_ffn_w13, L2_ffn_w2), axis=-1)
    x = _layernorm(x + _L3_attn_ref(x, L3_attn_norm_w, L3_attn_skip_w, L3_attn_in_w, L3_attn_conv_w, L3_attn_conv_b, L3_attn_wd1, L3_attn_wd2, L3_attn_wd2_b, L3_attn_wb, L3_attn_wc, L3_attn_A_log, L3_attn_W_D, L3_attn_out_w), axis=-1)
    x = _layernorm(x + _L3_ffn_ref(x, L3_ffn_Wr, L3_ffn_br, L3_ffn_W1, L3_ffn_b1, L3_ffn_W2, L3_ffn_b2), axis=-1)
    return x

_drawn_inputs = setup_inputs


def setup_inputs(seed=0):
    import zlib

    import numpy as np

    out = dict(_drawn_inputs(seed))
    spreads = {'L0_attn_bz0': (0.0, 0.8),
     'L0_attn_bh0': (0.0, 0.1),
     'L0_attn_bz1': (0.0, 0.8),
     'L0_attn_bh1': (0.0, 0.1),
     'L0_ffn_b1': (0.0, 0.8),
     'L0_ffn_b2': (0.0, 0.8),
     'L0_ffn_bih': (0.0, 0.1),
     'L0_ffn_bhh': (0.0, 0.448),
     'L0_ffn_bq': (0.0, 2.0),
     'L0_ffn_bk': (0.0, 2.0),
     'L0_ffn_bv': (0.0, 0.1),
     'L0_ffn_ln_g': (1.0, 0.6),
     'L0_ffn_ln_b': (0.0, 0.8),
     'L0_ffn_bvp': (0.0, 0.1),
     'L0_ffn_bo': (0.0, 0.1),
     'L1_attn_bq': (0.0, 0.8),
     'L1_attn_bk': (0.0, 2.0),
     'L1_attn_bv': (0.0, 0.1),
     'L1_attn_bo': (0.0, 0.1),
     'L2_attn_bq': (0.0, 2.0),
     'L2_attn_bk': (0.0, 0.8),
     'L2_attn_bv': (0.0, 0.1),
     'L2_attn_bo': (0.0, 0.1),
     'L3_attn_norm_w': (1.0, 0.2),
     'L3_attn_conv_b': (0.0, 0.1),
     'L3_attn_wd2_b': (0.0, 0.652),
     'L3_attn_W_D': (1.0, 0.2),
     'L3_ffn_br': (0.0, 0.567),
     'L3_ffn_b1': (0.0, 0.773),
     'L3_ffn_b2': (0.0, 0.1)}
    factors = {'L0_ffn_slot_init': 8.0,
     'L0_ffn_w1': 8.0,
     'L0_ffn_w2': 8.0,
     'L0_ffn_Whh': 8.0,
     'L0_ffn_wq': 64.0,
     'L0_ffn_wk': 41.609,
     'L0_ffn_wv': 4.581,
     'L1_attn_Wq': 2.835,
     'L1_ffn_b1': 5.989,
     'L1_ffn_sb1': 7.896,
     'L2_attn_Wq': 2.728,
     'L2_ffn_router_w': 8.0,
     'L2_ffn_w13': 7.698,
     'L2_ffn_w2': 7.572,
     'L3_ffn_W1': 2.761}
    for name, (base, spread) in spreads.items():
        noise = np.random.default_rng([zlib.crc32(name.encode()), seed]).standard_normal(out[name].shape)
        drawn = base * np.exp(spread * noise) if base else spread * noise
        out[name] = jnp.asarray(drawn.astype(out[name].dtype))
    for name, factor in factors.items():
        out[name] = (out[name] * factor).astype(out[name].dtype)
    return out
```

```python
import numpy as np
import concourse.bass as bass
from concourse import mybir
from contextlib import ExitStack

F32 = mybir.dt.float32
BF16 = mybir.dt.bfloat16
I32 = mybir.dt.int32
ALU = mybir.AluOpType
ACT = mybir.ActivationFunctionType
AX = mybir.AxisListType.X
FILL = -3.0e38

NB, L, D = 4, 1024, 128
T = NB * L
NT = T // 128

START, STOP = 1, 8


class Queue:

    def __init__(self, name, sem):
        self.name, self.sem, self.n, self.items = name, sem, 0, []

    def do(self, fn, *deps):
        self.n += 1
        self.items.append((fn, deps, self.sem, 1))
        return (self.sem, self.n)

    def dma(self, fn, sem, *deps):
        self.items.append((fn, deps, sem, 16))

    def emit(self, eng):
        seen = {}

        def wait(d):
            if d is None:
                return
            if isinstance(d, list):
                for x in d:
                    wait(x)
                return
            sem, v = d
            if v > 0 and seen.get(id(sem), 0) < v:
                eng.wait_ge(sem, v)
                seen[id(sem)] = v

        for fn, deps, sem, k in self.items:
            for d in deps:
                wait(d)
            if fn is not None:
                fn().then_inc(sem, k)


class Ring:

    def __init__(self, bufs, first=None):
        self.bufs, self.i = bufs, -1
        self.free = [first or [] for _ in bufs]

    def take(self):
        self.i = (self.i + 1) % len(self.bufs)
        return self.i, self.bufs[self.i], self.free[self.i]


GROUPS = [
    [("ident", 128, 128), ("cen", 128, 128), ("ones", 128, 128), ("one64", 64, 1), ("hm", 128, 16),
     ("hmT", 112, 128), ("E64", 64, 4 * 112), ("ucol", 112, 5), ("tokid", 128, 8), ("iotau", 128, 560),
     ("sel8", 8, 8 * 128),
     ("Wz0", 128, 128), ("Wh0", 128, 128), ("Wz1", 128, 128), ("Wh1", 128, 128), ("b_l0a", 128, 4)],
    [("slotT", 128, 64), ("slot", 64, 128), ("w1", 128, 128), ("w2", 64, 64), ("WihT", 128, 384), ("WhhT", 128, 384),
     ("wq", 128, 32), ("wk", 128, 32), ("wv", 128, 128), ("wvp", 128, 128), ("wo", 128, 128),
     ("b1", 64, 1), ("b2r", 128, 64), ("tau", 128, 1), ("bih", 128, 3), ("bhh", 128, 3), ("bq", 32, 1), ("bk", 32, 1),
     ("bvr", 64, 128), ("lng", 128, 1), ("lnb", 128, 1), ("bvp", 128, 1), ("bo", 128, 1)],
    [("aWq", 128, 128), ("aWk", 128, 128), ("aWv", 128, 128), ("aWo", 128, 128), ("abq", 128, 1), ("abk", 128, 1),
     ("abvr", 128, 128), ("abo", 128, 1),
     ("gate0", 128, 128), ("gate1", 128, 128), ("fw1", 128, 1024), ("fb1", 128, 8), ("fw2", 128, 1024), ("fb2", 128, 2),
     ("sw1", 128, 512), ("sb1", 128, 4), ("sw2", 128, 512), ("sb2", 128, 1)],
    [("cWq", 128, 1024), ("cWk", 128, 1024), ("cWv", 128, 1024), ("cWo", 128, 1024),
     ("cbq2", 128, 16), ("cbk", 128, 8), ("cbo", 128, 1), ("dmask", 128, 128), ("coss", 128, 16),
     ("rwT", 128, 8)],
    [("w13", 128, 4096), ("w2e", 128, 2048)],
    [("normw", 128, 1), ("skT", 128, 256), ("inT", 128, 256), ("convw", 128, 8), ("convb", 128, 2), ("wd1T", 128, 128),
     ("wd2T", 64, 256), ("wd2b", 128, 2), ("wbcT", 128, 64), ("Alog", 128, 32), ("WD", 128, 2), ("outT", 128, 256)],
    [("Wr", 128, 8), ("brr", 128, 8), ("W1", 128, 4096), ("B1", 128, 32), ("W2", 128, 4096), ("B2", 128, 8)],
]


def place():
    off, at, spans = 0, {}, []
    for g in GROUPS:
        a = off
        for name, r, c in g:
            at[name] = (r, off, c)
            off += c
        spans.append((a, off))
    return at, spans, off


def build(nc, wp, xT_d, xK_d, sidx_d, cs_d, bkv_d, out_d):
    at, spans, WN = place()
    names = ["pe", "dve", "act", "pool", "sp"]
    ctx = ExitStack()
    sem = lambda n: ctx.enter_context(nc.semaphore(n))
    PE, V, A, G, S = (Queue(n, sem("q_" + n)) for n in names)
    engines = (PE, V, A, G)
    s_w = [sem(f"s_w{i}") for i in range(len(GROUPS))]
    s_x, s_si, s_cs, s_kv, s_out, s_cs2 = (sem(n) for n in ("s_x", "s_si", "s_cs", "s_kv", "s_out", "s_cs2"))

    W = nc.alloc_sbuf_tensor("W", [128, WN], F32)
    XTt = nc.alloc_sbuf_tensor("XT", [128, T], F32)
    XKt = nc.alloc_sbuf_tensor("XK", [128, T], F32)
    SMN = 512
    SMt = nc.alloc_sbuf_tensor("SM", [128, SMN], F32)
    TN = (212863 - 4 * (WN + 2 * T + SMN)) // 4 - 64
    TMP = nc.alloc_sbuf_tensor("TMP", [128, TN], F32)
    XT, XK, SM = XTt[:, :], XKt[:, :], SMt[:, :]
    PSALL = nc.alloc_psum_tensor("ps", [128, 4096], F32)[:, :]
    PS = [PSALL[:, i * 512:(i + 1) * 512] for i in range(8)]

    def w(name):
        r, o, c = at[name]
        return W[0:r, o:o + c]

    wtok = lambda g: (s_w[g], 16)

    class Arena:
        def __init__(self):
            self.o = 0

        def __call__(self, cols, rows=128, dt=F32):
            n = cols if dt == F32 or dt == I32 else (cols + 1) // 2
            assert self.o + n <= TN, ("arena", self.o + n, TN)
            v = TMP[:, self.o:self.o + n]
            self.o += n
            if dt != F32:
                v = v.bitcast(dt)
            return v[0:rows, 0:cols]

    def now():
        return [(q.sem, q.n) for q in engines]

    def barrier():
        t = now()
        for q in engines:
            q.items.append((None, t, None, 0))

    def mm(out, lhsT, rhs, start=True, stop=True, **k):
        return nc.tensor.matmul(out, lhsT, rhs, start=start, stop=stop, **k)

    def act(out, in_, f, bias=0.0, scale=1.0, acc=None):
        if acc is None:
            return nc.scalar.activation(out, in_, f, bias=bias, scale=scale)
        return nc.scalar.activation(out, in_, f, bias=bias, scale=scale, accum_out=acc)

    tt = lambda o, a, b, op: nc.vector.tensor_tensor(o, a, b, op)
    ts = lambda o, a, s1, s2, op0, op1=None: (nc.vector.tensor_scalar(o, a, s1, s2, op0, op1) if op1 is not None
                                             else nc.vector.tensor_scalar(o, a, s1, None, op0))
    stt = lambda o, a, s, b, op0, op1: nc.vector.scalar_tensor_tensor(out=o, in0=a, scalar=s, in1=b, op0=op0, op1=op1)

    def g3(ap, n):
        return ap.rearrange("p (n k) -> p n k", n=n)

    def bin_(ap, n, k):
        return ap.unsqueeze(2).to_broadcast([ap.shape[0], n, k])

    def bout(ap, n):
        return ap.unsqueeze(1).to_broadcast([ap.shape[0], n, ap.shape[1]])

    CH = 512
    NCH = T // CH
    ch = lambda ap, i, k=CH: ap[:, i * k:(i + 1) * k]
    tile = lambda ap, i: ap[:, i * 128:(i + 1) * 128]

    t_eps = V.do(lambda: nc.vector.memset(SM[:, 479:480], 1e-5))

    def layernorm(last=False, src=None):
        src = XT if src is None else src
        ar = Arena()
        Rj = Ring([ar(512) for _ in range(2)])
        ss, rs, sd, eps = SM[:, 0:32], SM[:, 32:64], SM[:, 480:512], SM[:, 479:480]
        Rp, Rt = Ring([PS[0], PS[1], PS[2], PS[3]]), Ring([PS[4], PS[5], PS[6], PS[7]])
        pend = []

        def back(i, t_xk):
            k, pt, fr = Rt.take()

            def f():
                for j in range(4):
                    r = nc.tensor.transpose(pt[:, j * 128:(j + 1) * 128], tile(XK, 4 * i + j), w("ident"))
                return r
            t = PE.do(f, fr, t_xk)
            t = A.do(lambda: nc.scalar.copy(ch(XT, i), pt), t)
            Rt.free[k] = [t]

        for i in range(NCH):
            k, p, fr = Rp.take()

            def f(i=i, p=p):
                for j in range(4):
                    r = mm(p[:, j * 128:(j + 1) * 128], tile(src, 4 * i + j), w("cen"))
                return r
            t0 = PE.do(f, fr)

            kj, jk, fj = Rj.take()

            def f(i=i, p=p, jk=jk):
                for j in range(4):
                    c = 4 * i + j
                    r = act(jk[:, j * 128:(j + 1) * 128], p[:, j * 128:(j + 1) * 128], ACT.Square, scale=128 ** -0.5, acc=ss[:, c:c + 1])
                return r
            t1 = A.do(f, t0, fj)
            Rj.free[kj] = [t1]
            t2 = A.do(lambda i=i: act(sd[:, 4 * i:4 * i + 4], ss[:, 4 * i:4 * i + 4], ACT.Sqrt, bias=eps), t1, t_eps)
            t2 = V.do(lambda i=i: nc.vector.reciprocal(rs[:, 4 * i:4 * i + 4], sd[:, 4 * i:4 * i + 4]), t2)
            t3 = V.do(lambda i=i, p=p: tt(g3(ch(XK, i), 4), g3(p, 4), bin_(rs[:, 4 * i:4 * i + 4], 4, 128), ALU.mult), t2)
            Rp.free[k] = [t3]
            if last:
                S.dma(lambda i=i: nc.sync.dma_start(
                    out_d.rearrange("b (n p) d -> p (b n) d", p=128)[:, 4 * i:4 * i + 4, :], g3(ch(XK, i), 4)), s_out, t3)
            else:
                pend.append((i, t3))
                if len(pend) > 1:
                    back(*pend.pop(0))
        for x in pend:
            back(*x)
        barrier()

    def stage1():
        ar = Arena()
        H1 = ar(T)
        bufs = [[ar(512) for _ in range(3)] for _ in range(5)]
        Ra, Rz, Rs, Rg, Rh = (Ring(b) for b in bufs)
        Rp = Ring([(PS[2 * i], PS[2 * i + 1]) for i in range(4)])
        nb, bh5 = SM[:, 64:66], SM[:, 66:68]
        b = w("b_l0a")
        t_b = V.do(lambda: ts(nb, b.rearrange("p (l k) -> p k l", k=2)[:, 0, :], -1.0, None, ALU.mult), wtok(0))
        t_b = V.do(lambda: ts(bh5, b.rearrange("p (l k) -> p k l", k=2)[:, 1, :], 0.5, None, ALU.add), wtok(0))
        tH = {}

        def part(l, i):
            src = XT if l == 0 else H1
            k, (pz, ph), fr = Rp.take()

            def f():
                mm(pz, w(f"Wz{l}"), ch(src, i))
                return mm(ph, w(f"Wh{l}"), ch(src, i))
            t0 = PE.do(f, fr, wtok(0), (s_x, 16) if l == 0 else tH[(0, i)])
            ka, a, fa = Ra.take()
            kz, z, fz = Rz.take()
            ks, s, fs = Rs.take()
            kg, g, fg = Rg.take()
            t1 = A.do(lambda: act(a, pz, ACT.Sigmoid, bias=nb[:, l:l + 1], scale=-1.0), t0, t_b, fa)
            t1 = A.do(lambda: act(z, pz, ACT.Sigmoid, bias=b[:, 2 * l:2 * l + 1]), fz)
            t1 = A.do(lambda: act(s, ph, ACT.Sigmoid, bias=b[:, 2 * l + 1:2 * l + 2]), fs)
            t2 = V.do(lambda: stt(g, ph, bh5[:, l:l + 1], s, ALU.add, ALU.max), t1, fg)
            Rp.free[k] = [t1, t2]
            t3 = V.do(lambda: tt(g, g, z, ALU.mult), t2)
            if l == 0:
                h = ch(H1, i)
                hprev = H1[:, i * 512 - 1:i * 512] if i % 2 else 0.5
                fh = None
            else:
                kh, h, fh = Rh.take()
                hprev = Rh.bufs[(kh - 1) % 3][:, 511:512] if i % 2 else 0.5
            t4 = V.do(lambda: nc.vector.tensor_tensor_scan(h, a, g, hprev, ALU.mult, ALU.add), t3, fh, tH.get((l, i - 1)))
            tH[(l, i)] = t4
            Ra.free[ka] = Rz.free[kz] = Rs.free[ks] = Rg.free[kg] = [t4]
            if l == 1:
                t5 = G.do(lambda: nc.gpsimd.tensor_tensor(ch(XT, i), ch(XT, i), h, ALU.add), t4, (s_x, 16))
                Rh.free[kh] = [t5]

        for i in range(NCH + 1):
            if i < NCH:
                part(0, i)
            if i > 0:
                part(1, i - 1)
        barrier()

    def stage2():
        ar = Arena()
        hb = [ar(512, 64) for _ in range(2)]
        Lg, R, E, AL = ar(NT * 64), ar(NT * 64), ar(NT * 64), ar(NT * 64)
        V8, den, rden = ar(NT * 8), ar(NT), ar(NT)
        aT = [ar(512, 64) for _ in range(2)]
        sm1, b1p, itau = SM[:, 68:69], SM[0:64, 69:70], SM[:, 70:71]
        bsum = SM[:, 71:74]
        siT, rd, gr, gz, gn, tn, Sn = (ar(256) for _ in range(7))
        qk, vK = ar(512, 32), ar(512, 64)
        sc, mx, sm = ar(256, 64), SM[0:64, 74:78], SM[0:64, 78:82]
        sT, yT, yN = ar(256, 64), ar(256), ar(512, 64)
        ss, sd = SM[0:64, 82:86], SM[0:64, 86:90]
        eps = SM[:, 479:480]
        jk = hb[0]
        Zt = hb[1]
        w1, w2, slotT, slot = w("w1"), w("w2"), w("slotT"), w("slot")
        W1 = wtok(1)
        t = PE.do(lambda: mm(PS[7][:, 0:1], slot, w("one64")), W1)
        t = V.do(lambda: nc.vector.tensor_copy(sm1, PS[7][:, 0:1]), t, W1)
        t = PE.do(lambda: mm(PS[7][0:64, 8:9], w1[:, 64:128], sm1), t)
        t_b1 = V.do(lambda: tt(b1p, PS[7][0:64, 8:9], w("b1"), ALU.add), t)
        t = V.do(lambda: ts(itau, w("tau"), 0.0, None, ALU.max))
        t2 = V.do(lambda: ts(SM[:, 90:91], w("tau"), -1.0, 0.0, ALU.mult, ALU.max))
        t = V.do(lambda: stt(itau, itau, 0.1, SM[:, 90:91], ALU.add, ALU.add), t2)
        t_tau = V.do(lambda: nc.vector.reciprocal(itau, itau), t)
        t_bs = V.do(lambda: tt(bsum, w("bih"), w("bhh"), ALU.add))
        Rp, Rl, Rh = Ring([PS[0], PS[1]]), Ring([PS[2][:, 0:256], PS[3][:, 0:256]]), Ring(hb)
        last_m = None
        for i in range(NCH):
            k, p, fr = Rp.take()
            t = PE.do(lambda p=p, i=i: mm(p[0:64, :], w1[:, 0:64], ch(XT, i)), fr)
            kh, h, fh = Rh.take()
            t = A.do(lambda p=p, h=h: act(h, p[0:64, :], ACT.Gelu, bias=b1p), t, t_b1, fh)
            Rp.free[k] = [t]
            kl, pl, fl = Rl.take()

            def f(h=h, pl=pl):
                for j in range(4):
                    r = mm(pl[:, j * 64:(j + 1) * 64], tile(h, j), w2)
                return r
            t = PE.do(f, t, fl)
            Rh.free[kh] = [t]
            lg = Lg[:, i * 256:(i + 1) * 256]
            b2 = w("b2r").unsqueeze(1).to_broadcast([128, 4, 64])
            t = V.do(lambda lg=lg, pl=pl, b2=b2: tt(g3(lg, 4), g3(pl, 4), b2, ALU.add), t)
            Rl.free[kl] = [t]
            t = V.do(lambda lg=lg: ts(lg, lg, itau, None, ALU.mult), t, t_tau)

            def f(i=i):
                for c in range(4 * i, 4 * i + 4):
                    r = nc.vector.max(V8[:, c * 8:c * 8 + 8], Lg[:, c * 64:c * 64 + 64])
                return r
            t = V.do(f, t)

            def f(i=i):
                for c in range(4 * i, 4 * i + 4):
                    r = nc.vector.match_replace(R[:, c * 64:c * 64 + 64], V8[:, c * 8:c * 8 + 8], Lg[:, c * 64:c * 64 + 64], FILL)
                return r
            last_m = V.do(f, t)
        Lg3, R3, E3, A3 = g3(Lg, NT), g3(R, NT), g3(E, NT), g3(AL, NT)
        v1 = g3(V8, NT)[:, :, 0:1].to_broadcast([128, NT, 64])
        t = V.do(lambda: tt(E3, Lg3, v1, ALU.subtract), last_m)
        te = A.do(lambda: act(E, E, ACT.Exp), t)
        t = V.do(lambda: tt(R, R, Lg, ALU.not_equal), last_m)
        t = V.do(lambda: tt(E, E, R, ALU.mult), te, t)
        t = V.do(lambda: nc.vector.tensor_reduce(den, E3, AX, ALU.add), t)
        t = V.do(lambda: nc.vector.reciprocal(rden, den), t)
        t_al = V.do(lambda: tt(A3, E3, bin_(rden, NT, 64), ALU.mult), t)

        def f():
            for b in range(NB):
                for c in range(8):
                    mm(PS[4][:, b * 64:(b + 1) * 64], tile(XK, b * 8 + c), A3[:, b * 8 + c, :], c == 0, c == 7)
                for c in range(8):
                    r = mm(PS[5][:, b * 64:(b + 1) * 64], w("ones"), A3[:, b * 8 + c, :], c == 0, c == 7)
            return r
        t0 = PE.do(f, t_al)
        t = V.do(lambda: ts(rd, PS[5][:, 0:256], 1e-8, None, ALU.add), t0)
        t = V.do(lambda: nc.vector.reciprocal(rd, rd), t)
        t = V.do(lambda: tt(siT, PS[4][:, 0:256], rd, ALU.mult), t)
        s4 = slotT.unsqueeze(1).to_broadcast([128, 4, 64])
        Wih, Whh = w("WihT"), w("WhhT")

        def f():
            for g in range(2):
                mm(PS[6][:, g * 256:(g + 1) * 256], tile(Wih, g), siT, True, False)
                mm(g3(PS[6][:, g * 256:(g + 1) * 256], 4), tile(Whh, g), s4, False, True)
            mm(PS[7][:, 0:256], tile(Wih, 2), siT)
            return mm(g3(PS[7][:, 256:512], 4), tile(Whh, 2), s4)
        t0 = PE.do(f, t, t_b1)
        t1 = A.do(lambda: act(gr, PS[6][:, 0:256], ACT.Sigmoid, bias=bsum[:, 0:1]), t0, t_bs)
        tz = A.do(lambda: act(gz, PS[6][:, 256:512], ACT.Sigmoid, bias=bsum[:, 1:2]))
        t = V.do(lambda: stt(tn, PS[7][:, 256:512], w("bhh")[:, 2:3], gr, ALU.add, ALU.mult), t1)
        t = V.do(lambda: stt(tn, PS[7][:, 0:256], w("bih")[:, 2:3], tn, ALU.add, ALU.add), t)
        t = A.do(lambda: act(gn, tn, ACT.Tanh), t)
        t = V.do(lambda: tt(g3(tn, 4), s4, g3(gn, 4), ALU.subtract), t)
        t = V.do(lambda: tt(tn, tn, gz, ALU.mult), t, tz)
        t_S = V.do(lambda: tt(Sn, tn, gn, ALU.add), t)

        def f():
            mm(PS[0][0:32, 0:256], w("wq"), Sn)
            return mm(PS[0][0:32, 256:512], w("wk"), Sn)
        t = PE.do(f, t_S)
        tq = V.do(lambda: ts(qk[:, 0:256], PS[0][0:32, 0:256], w("bq"), None, ALU.add), t)
        tq = V.do(lambda: ts(qk[:, 256:512], PS[0][0:32, 256:512], w("bk"), None, ALU.add), t)

        def f():
            for b in range(NB):
                r = mm(PS[1][0:64, b * 128:(b + 1) * 128], Sn[:, b * 64:(b + 1) * 64], w("wv"))
            return r
        t = PE.do(f, t_S)
        tv = V.do(lambda: tt(g3(vK, 4), g3(PS[1][0:64, :], 4), w("bvr").unsqueeze(1).to_broadcast([64, 4, 128]), ALU.add), t)

        def f():
            for b in range(NB):
                r = mm(PS[2][0:64, b * 64:(b + 1) * 64], qk[:, b * 64:(b + 1) * 64], qk[:, 256 + b * 64:256 + (b + 1) * 64])
            return r
        t = PE.do(f, tq, last_m)
        s3 = g3(sc, 4)
        p3 = g3(PS[2][0:64, 0:256], 4)
        tm = V.do(lambda: nc.vector.tensor_reduce(mx, p3, AX, ALU.max), t)
        t = V.do(lambda: tt(s3, p3, bin_(mx, 4, 64), ALU.subtract), tm)
        t = A.do(lambda: act(sc, sc, ACT.Exp, scale=32 ** -0.5), t)
        t = V.do(lambda: nc.vector.tensor_reduce(sm, s3, AX, ALU.add), t)
        t = V.do(lambda: nc.vector.reciprocal(sm, sm), t)
        t = V.do(lambda: tt(s3, s3, bin_(sm, 4, 64), ALU.mult), t)

        def f():
            for b in range(NB):
                r = nc.tensor.transpose(PS[3][0:64, b * 64:(b + 1) * 64], sc[:, b * 64:(b + 1) * 64], w("ident")[0:64, 0:64])
            return r
        t = PE.do(f, t, last_m)
        t = V.do(lambda: nc.vector.tensor_copy(sT, PS[3][0:64, 0:256]), t)

        def f():
            for b in range(NB):
                r = mm(PS[0][:, b * 64:(b + 1) * 64], vK[:, b * 128:(b + 1) * 128], sT[:, b * 64:(b + 1) * 64])
            return r
        t = PE.do(f, t, tv)
        t = V.do(lambda: tt(yT, PS[0][:, 0:256], Sn, ALU.add), t)

        def f():
            for b in range(NB):
                r = mm(PS[1][0:64, b * 128:(b + 1) * 128], yT[:, b * 64:(b + 1) * 64], w("cen"))
            return r
        t0 = PE.do(f, t)

        def f():
            for b in range(NB):
                r = act(jk[:, b * 128:(b + 1) * 128], PS[1][0:64, b * 128:(b + 1) * 128], ACT.Square, scale=128 ** -0.5, acc=ss[:, b:b + 1])
            return r
        t = A.do(f, t0)
        t = A.do(lambda: act(sd, ss, ACT.Sqrt, bias=eps[0:64, :]), t, t_eps)
        t = V.do(lambda: nc.vector.reciprocal(sd, sd), t)
        t = V.do(lambda: tt(g3(yN, 4), g3(PS[1][0:64, :], 4), bin_(sd, 4, 128), ALU.mult), t)

        def f():
            for b in range(NB):
                r = nc.tensor.transpose(PS[0][:, b * 64:(b + 1) * 64], yN[:, b * 128:(b + 1) * 128], w("ident")[0:64, 0:64])
            return r
        t = PE.do(f, t)
        t = V.do(lambda: ts(yT, PS[0][:, 0:256], w("lng"), w("lnb"), ALU.mult, ALU.add), t)
        t = PE.do(lambda: mm(PS[1][:, 0:256], w("wvp"), yT), t)
        t = V.do(lambda: ts(siT, PS[1][:, 0:256], w("bvp"), None, ALU.add), t)

        def f():
            for b in range(NB):
                r = mm(PS[0][0:64, b * 128:(b + 1) * 128], siT[:, b * 64:(b + 1) * 64], w("wo"))
            return r
        t = PE.do(f, t)
        t_Z = V.do(lambda: nc.vector.tensor_copy(Zt, PS[0][0:64, :]), t)
        Rt, Ra, Ro = Ring([PS[4], PS[5]], [t_Z]), Ring(aT), Ring([PS[6], PS[7]], [t_S])
        for i in range(NCH):
            k, p, fr = Rt.take()

            def f(i=i, p=p):
                for j in range(4):
                    r = nc.tensor.transpose(p[0:64, j * 128:(j + 1) * 128], A3[:, 4 * i + j, :], w("ident"))
                return r
            t = PE.do(f, fr)
            ka, a, fa = Ra.take()
            t = A.do(lambda a=a, p=p: nc.scalar.copy(a, p[0:64, :]), t, fa)
            Rt.free[k] = [t]
            ko, o, fo = Ro.take()
            b = i // 2
            t = PE.do(lambda a=a, o=o, b=b: mm(o, Zt[:, b * 128:(b + 1) * 128], a), t, t_Z, fo)
            Ra.free[ka] = [t]
            t = V.do(lambda i=i, o=o: stt(ch(XT, i), o, w("bo"), ch(XT, i), ALU.add, ALU.add), t)
            Ro.free[ko] = [t]
        barrier()

    def stage3():
        ar = Arena()
        W2 = wtok(2)
        NU = 560
        SO = ar(280)
        sidx, sif = ar(35, dt=I32), ar(35)
        KTb = ar(1024)
        Kbk = [ar(576), ar(576)]
        ks = ar(35)
        MK = ar(512)
        MT = ar(1024, 64)
        cand = SM[0:64, 192:200]
        one64 = ar(1024, 64)
        posT = ar(1024, 64)
        PK = ar(512)
        xs = ar(35)
        rsum = SM[:, 93:94]
        t = G.do(None)if False else None
        G.dma(lambda: nc.gpsimd.dma_start(sidx, sidx_d.partition_broadcast(128)), s_si, now())
        t = V.do(lambda: nc.vector.tensor_copy(sif, sidx), (s_si, 16), W2)
        tid = w("tokid")
        t = V.do(lambda: tt(g3(SO, 8), sif.unsqueeze(1).to_broadcast([128, 8, 35]), bin_(tid, 8, 35), ALU.is_equal), t)
        t_so = t
        Rq, Rk = Ring([ar(512) for _ in range(2)]), Ring(Kbk)
        Rp = Ring([PS[0], PS[1]])
        Rm = Ring([(PS[2], PS[3]), (PS[4], PS[5])])
        hm = w("hm")
        MK4 = MK.rearrange("p (c b h) -> p c b h", c=8, b=4)
        t_mk = None
        t_xs = t_kb = None
        for b in range(NB):
            def f(b=b):
                for c in range(8):
                    r = mm(PS[6][:, 0:35], tile(XK, b * 8 + c), SO[:, c * 35:(c + 1) * 35], c == 0, c == 7)
                return r
            t = PE.do(f, t_so, t_kb)
            t = V.do(lambda: nc.vector.tensor_copy(xs, PS[6][:, 0:35]), t)
            t = PE.do(lambda: mm(PS[7][:, 0:35], w("aWk"), xs), t, W2)
            t = V.do(lambda: ts(ks, PS[7][:, 0:35], w("abk"), None, ALU.add), t)
            kk, kb, fk = Rk.take()
            kv = kb.rearrange("p (g c) -> p g c", g=2)
            ksum = SM[:, 94:95]
            t2 = V.do(lambda: nc.vector.tensor_reduce(ksum, ks, AX, ALU.add), t)
            for g in range(2):
                mk = hm[:, g * 8:g * 8 + 8]
                t_kb = V.do(lambda kv=kv, g=g, mk=mk: tt(kv[:, g, 0:280].rearrange("p (h s) -> p h s", h=8),
                            ks.unsqueeze(1).to_broadcast([128, 8, 35]), bin_(mk, 8, 35), ALU.mult), t, fk)
                t_kb = V.do(lambda kv=kv, g=g, mk=mk: ts(kv[:, g, 280:288], mk, ksum, None, ALU.mult), t2)
            for i in range(2):
                k, p, fr = Rp.take()
                t = PE.do(lambda p=p, b=b, i=i: mm(p, w("aWq"), ch(XT, 2 * b + i)), fr)
                kq, q, fq = Rq.take()
                t = A.do(lambda p=p, q=q: act(q, p, ACT.Identity, bias=w("abq")), t, fq)
                Rp.free[k] = [t]
                for j in range(4):
                    km, pm, fm = Rm.take()

                    def f(q=q, j=j, pm=pm, kv=kv):
                        for g in range(2):
                            r = mm(pm[g][:, 0:288], tile(q, j), kv[:, g, :])
                        return r
                    tq = PE.do(f, t, t_kb, fm)
                    c = 4 * i + j
                    for g in range(2):
                        m = MK4[:, c, b, g * 8:g * 8 + 8]
                        t2 = V.do(lambda pm=pm, g=g, m=m: nc.vector.tensor_reduce(
                            m, pm[g][:, 0:280].rearrange("p (h s) -> p h s", h=8), AX, ALU.max), tq)
                        t_mk = V.do(lambda pm=pm, g=g, m=m: stt(m, pm[g][:, 280:288], -1.0 / 35, m, ALU.mult, ALU.add), t2)
                    Rm.free[km] = [t_mk]
                Rq.free[kq] = [tq]
            Rk.free[kk] = [tq]

        def f():
            for c in range(8):
                r = nc.tensor.transpose(PS[c // 4][0:64, (c % 4) * 128:(c % 4 + 1) * 128], MK[:, c * 64:(c + 1) * 64], w("ident"))
            return r
        t = PE.do(f, t_mk, now())
        for i in range(2):
            t = V.do(lambda i=i: nc.vector.tensor_scalar(ch(MT, i), PS[i][0:64, :], 8 ** -0.5, None, ALU.mult), t)
        for r in range(5):
            t = V.do(lambda: nc.vector.max(cand, MT), t)
            if r == 4:
                t = V.do(lambda: nc.vector.memset(cand[:, 3:8], FILL), t)
            t = V.do(lambda: nc.vector.match_replace(MT, cand, MT, FILL), t)
        t1 = V.do(lambda: nc.vector.memset(one64, 1.0))
        t = V.do(lambda: ts(MT, MT, FILL, None, ALU.is_equal), t)
        t = V.do(lambda: nc.vector.tensor_tensor_scan(posT, one64, MT, 0.0, ALU.mult, ALU.add), t, t1)
        t_pos = V.do(lambda: tt(posT, posT, MT, ALU.mult), t)

        def f():
            for c in range(8):
                r = nc.tensor.transpose(PS[2][:, c * 64:(c + 1) * 64], tile(posT, c), w("ident")[0:64, 0:64])
            return r
        t = PE.do(f, t_pos)
        t_pk = V.do(lambda: nc.vector.tensor_copy(PK, PS[2]), t)
        PK4 = PK.rearrange("p (c b h) -> p c b h", c=8, b=4)

        barrier()
        ar.o = 280 + 70 + 1024 + 1152 + 35 + 512 + 1024 + 1024 + 1024 + 512 + 35
        SO2 = SO
        Roh = Ring([ar(NU), ar(NU)])
        Xs, Qb, VK = ar(NU), ar(NU), ar(1024)
        PR = ar(1024, 112)
        PTt = ar(1024)[:, 0:896]
        Ob = ar(640, 112)
        vmc = SM[:, 95:96]
        vmr = ar(128, 112)
        posB = ar(1024, 112)
        OHT = [ar(512, 112), ar(512, 112)]
        outT = ar(512)
        hmT = w("hmT")
        nmx = SM[:, 200:201]
        iota3 = w("iotau").rearrange("p (u h) -> p u h", h=16)
        Xs3, Qb3 = Xs.rearrange("p (u h) -> p u h", h=16), Qb.rearrange("p (u h) -> p u h", h=16)
        Roo = Ring(OHT)
        for b in range(NB):
            def f(b=b):
                for i in range(2):
                    r = mm(PS[4 + i], w("aWk"), ch(XT, 2 * b + i))
                return r
            t = PE.do(f, now())
            for i in range(2):
                t_k = A.do(lambda i=i: act(ch(KTb, i), PS[4 + i], ACT.Identity, bias=w("abk")), t, now())
            for i in range(2):
                def f(b=b, i=i):
                    for j in range(4):
                        r = mm(PS[6 + i][:, j * 128:(j + 1) * 128], tile(XT, b * 8 + 4 * i + j), w("aWv"))
                    return r
                t = PE.do(f)
                t_v = V.do(lambda i=i: tt(g3(ch(VK, i), 4), g3(PS[6 + i], 4), w("abvr").unsqueeze(1).to_broadcast([128, 4, 128]), ALU.add), t)
            for c in range(8):
                ko, oh, fo = Roh.take()
                t = V.do(lambda oh=oh, c=c, b=b: tt(oh.rearrange("p (u h) -> p u h", h=16),
                         PK4[:, c, b, :].unsqueeze(1).to_broadcast([128, 35, 16]), iota3, ALU.is_equal), fo, t_k)

                def f(oh=oh, c=c, b=b):
                    for g in range(2):
                        r = mm(PS[g][:, 0:280], tile(XK, b * 8 + c), oh[:, g * 280:(g + 1) * 280], c == 0, c == 7)
                    return r
                t = PE.do(f, t)
                Roh.free[ko] = [t]
            for g in range(2):
                t2 = V.do(lambda g=g: nc.vector.tensor_copy(Xs[:, g * 280:(g + 1) * 280], PS[g][:, 0:280]), t)

            def f():
                for g in range(2):
                    r = mm(PS[2 + g][:, 0:280], w("aWq"), Xs[:, g * 280:(g + 1) * 280])
                return r
            t = PE.do(f, t2)
            for g in range(2):
                t2 = V.do(lambda g=g: ts(Xs[:, g * 280:(g + 1) * 280], PS[2 + g][:, 0:280], w("abq"), None, ALU.add), t)
            t_q = V.do(lambda: tt(Qb3, Xs3, hm.unsqueeze(1).to_broadcast([128, 35, 16]), ALU.mult), t2)

            def f():
                for c in range(8):
                    mm(PS[6][:, 0:1], tile(VK, c), w("ones")[:, 0:1], c == 0, c == 7)
                for c in range(8):
                    r = mm(PS[7][0:112, 0:128], w("ones")[:, 0:112], tile(VK, c), c == 0, c == 7)
                return r
            t = PE.do(f, t_v)
            t = V.do(lambda: ts(vmc, PS[6][:, 0:1], 1.0 / 1024, None, ALU.mult), t)
            t_vm = V.do(lambda: ts(vmr, PS[7][0:112, 0:128], 1.0 / 1024, None, ALU.mult))
            for j in range(5):
                def f(j=j):
                    for i in range(2):
                        r = mm(PS[i][0:112, :], Qb[:, j * 112:(j + 1) * 112], ch(KTb, i))
                    return r
                t = PE.do(f, t_q, t_k, now())
                for i in range(2):
                    t1 = V.do(lambda i=i: nc.vector.tensor_reduce(SM[0:112, 201 + i:202 + i], PS[i][0:112, :], AX, ALU.max), t)
                t = V.do(lambda: tt(nmx[0:112, :], SM[0:112, 201:202], SM[0:112, 202:203], ALU.max), t1)
                t = V.do(lambda: ts(nmx[0:112, :], nmx[0:112, :], -8 ** -0.5, None, ALU.mult), t)
                for i in range(2):
                    t1 = A.do(lambda i=i: act(ch(PR, i), PS[i][0:112, :], ACT.Exp, bias=nmx[0:112, :], scale=8 ** -0.5,
                                              acc=SM[0:112, 204 + i:205 + i]), t)
                t = V.do(lambda: tt(rsum[0:112, :], SM[0:112, 204:205], SM[0:112, 205:206], ALU.add), t1)
                t_r = V.do(lambda: nc.vector.reciprocal(rsum[0:112, :], rsum[0:112, :]), t)

                def f():
                    for c in range(8):
                        r = nc.tensor.transpose(PS[2 + c // 4][:, (c % 4) * 112:(c % 4 + 1) * 112], tile(PR, c), w("ident")[0:112, 0:112])
                    return r
                t = PE.do(f, t1)
                t = A.do(lambda: nc.scalar.copy(PTt[:, 0:448], PS[2][:, 0:448]), t)
                t = V.do(lambda: nc.vector.tensor_copy(PTt[:, 448:896], PS[3][:, 0:448]), t)

                def f():
                    for c in range(8):
                        r = mm(PS[6][0:112, 0:128], PTt[:, c * 112:(c + 1) * 112], tile(VK, c), c == 0, c == 7)
                    return r
                t = PE.do(f, t, t_vm)
                ob = Ob[:, j * 128:(j + 1) * 128]
                t = V.do(lambda ob=ob: stt(ob, PS[6][0:112, 0:128], rsum[0:112, :], vmr, ALU.mult, ALU.subtract), t, t_r)
                t = V.do(lambda ob=ob: tt(ob, ob, hmT, ALU.mult), t)
            t_ob = t

            def f(b=b):
                for i in range(2):
                    r = mm(PS[i][0:112, :], w("E64")[:, b * 112:(b + 1) * 112], ch(posT, i))
                return r
            t = PE.do(f)
            for i in range(2):
                t_pb = A.do(lambda i=i: nc.scalar.copy(ch(posB, i), PS[i][0:112, :]), t)
            for i in range(2):
                for j in range(5):
                    ko, oh, fo = Roo.take()
                    t = V.do(lambda oh=oh, i=i, j=j: ts(oh, ch(posB, i), w("ucol")[:, j:j + 1], None, ALU.is_equal), t_pb, fo)
                    t = PE.do(lambda oh=oh, j=j, i=i: mm(PS[4 + i], Ob[:, j * 128:(j + 1) * 128], oh, j == 0, j == 4), t, t_ob)
                    Roo.free[ko] = [t]
                t = A.do(lambda i=i: act(outT, PS[4 + i], ACT.Identity, bias=vmc), t, now())
                t = PE.do(lambda i=i: mm(PS[6 + i], w("aWo"), outT), t)
                t = V.do(lambda i=i, b=b: stt(ch(XT, 2 * b + i), PS[6 + i], w("abo"), ch(XT, 2 * b + i), ALU.add, ALU.add), t)
        barrier()

    def stage4():
        ar = Arena()
        b2 = SM[:, 92:93]
        G = Ggate = ar(128)
        Rx, Rh = Ring([(ar(512), ar(512)) for _ in range(2)]), Ring([ar(512) for _ in range(4)])
        Rp, Ro, Rd = Ring(PS[0:4]), Ring(PS[4:6]), Ring(PS[6:8])
        W2 = wtok(2)
        tg = V.do(lambda: tt(Ggate, w("gate1"), w("gate0"), ALU.subtract), W2)
        t = V.do(lambda: tt(b2, w("fb2")[:, 0:1], w("fb2")[:, 1:2], ALU.add))
        tb = V.do(lambda: tt(b2, b2, w("sb2"), ALU.add), t)
        fw1, fw2, sw1, sw2 = w("fw1"), w("fw2"), w("sw1"), w("sw2")
        for i in range(NCH):
            kd, d, fd = Rd.take()
            kx, (x0, x1), fx = Rx.take()
            x = ch(XT, i)
            t = PE.do(lambda d=d, x=x: mm(d, Ggate, x), tg, fd)
            t = V.do(lambda d=d, x=x, x1=x1: stt(x1, d, 0.0, x, ALU.is_gt, ALU.mult), t, fx)
            Rd.free[kd] = [t]
            tx = V.do(lambda x0=x0, x1=x1, x=x: tt(x0, x, x1, ALU.subtract), t)
            ko, o, fo = Ro.take()
            pend = []

            def down(h, kh, th, n, o=o, fo=fo):
                t = PE.do(lambda: mm(o, fw2[:, n * 128:(n + 1) * 128] if n < 8 else sw2[:, (n - 8) * 128:(n - 7) * 128], h,
                                     n == 8, n == 7), th, fo)
                Rh.free[kh] = [t]
                return t
            for n in (8, 9, 10, 11, 0, 1, 2, 3, 4, 5, 6, 7):
                src = x if n >= 8 else (x0 if n < 4 else x1)
                wt = fw1[:, n * 128:(n + 1) * 128] if n < 8 else sw1[:, (n - 8) * 128:(n - 7) * 128]
                bb = w("fb1")[:, n:n + 1] if n < 8 else w("sb1")[:, n - 8:n - 7]
                k, p, fr = Rp.take()
                t = PE.do(lambda p=p, wt=wt, src=src: mm(p, wt, src), fr, W2, tx if n < 8 else None)
                kh, h, fh = Rh.take()
                if n % 2:
                    t = A.do(lambda h=h, p=p, bb=bb: act(h, p, ACT.Relu, bias=bb), t, fh)
                else:
                    t = V.do(lambda h=h, p=p, bb=bb: ts(h, p, bb, 0.0, ALU.add, ALU.max), t, fh)
                Rp.free[k] = [t]
                pend.append((h, kh, t, n))
                if len(pend) > 2:
                    down(*pend.pop(0))
            for q in pend:
                to = down(*q)
            Rx.free[kx] = [to]
            t = V.do(lambda o=o, x=x: stt(x, o, b2, x, ALU.add, ALU.add), to, tb)
            Ro.free[ko] = [t]
        barrier()

    def stage5():
        ar = Arena()
        W3 = wtok(3)
        CS, bkr, bvr = ar(1024), ar(1024), ar(1024)
        S.dma(lambda: nc.sync.dma_start(CS, cs_d), s_cs2, now())
        S.dma(lambda: nc.sync.dma_start(bkr, bkv_d[0:1, :].partition_broadcast(128)), s_kv)
        S.dma(lambda: nc.sync.dma_start(bvr, bkv_d[1:2, :].partition_broadcast(128)), s_kv)
        Qr, Qe = ar(2048), ar(2048)
        KT, Kr, Ke = ar(1024), ar(1024), ar(2048)
        Vv = ar(4 * 260)
        AM = Ring([ar(512), ar(512)])
        Sb = ar(260)
        Ok, OT = ar(1024), ar(1024)
        den = SM[:, 208:212]
        co = w("coss")
        V5 = Vv.rearrange("p (c h d) -> p c h d", c=4, h=4)
        t_one = V.do(lambda: nc.vector.memset(V5[:, :, :, 64:65], 1.0))
        Ke5 = Ke.rearrange("p (c h s d) -> p c h s d", c=4, h=4, s=2)
        Rp, Ra, Ro = Ring([PS[0], PS[1]]), Ring([PSALL[:, 1024:2048].rearrange("p (e q j t) -> p q e j t", e=2, q=2, j=2)[:, q] for q in range(2)]), Ring([PS[5], PS[6]])
        Sp = PS[4]
        cWq, cWk, cWv, cWo = w("cWq"), w("cWk"), w("cWv"), w("cWo")
        dm = w("dmask").unsqueeze(1).unsqueeze(1).to_broadcast([128, 2, 2, 128])
        a4 = lambda am: am.rearrange("p (e j t) -> p e j t", e=2, j=2)
        CSt = (s_cs2, 16)
        fQr = fQe = fKT = fKe = fV = fOk = fOT = fS = f7 = t_kr = None
        t_cp = None
        for b in range(NB):
            for g in range(4):
                for i in range(2):
                    x = ch(XT, 2 * b + i)
                    tq, tk = [], []
                    for h in range(4):
                        k, p, fr = Rp.take()
                        o = (4 * g + h) * 64

                        def f(p=p, x=x, o=o):
                            mm(p[0:64, :], cWq[:, o:o + 64], x)
                            return mm(p[64:128, :], cWq[:, o:o + 64], x)
                        t = PE.do(f, fr, W3)
                        q = Qr[:, h * 512:(h + 1) * 512]
                        t = A.do(lambda q=q, p=p, h=h, g=g: act(q, p, ACT.Relu, bias=w("cbq2")[:, 4 * g + h:4 * g + h + 1]), t, fQr)
                        Rp.free[k] = [t]
                        t_qr = t
                        t_qe = G.do(lambda h=h, q=q, i=i: nc.gpsimd.tensor_tensor(Qe[:, h * 512:(h + 1) * 512], q, ch(CS, i), ALU.mult),
                                    t, fQe, CSt)
                    for h in range(2):
                        k, p, fr = Rp.take()
                        o = (4 * g + 2 * h) * 64
                        t = PE.do(lambda p=p, x=x, o=o: mm(p, cWk[:, o:o + 128], x), fr)
                        t_kt = A.do(lambda h=h, p=p, g=g: act(KT[:, h * 512:(h + 1) * 512], p, ACT.Relu,
                                                              bias=w("cbk")[:, 2 * g + h:2 * g + h + 1]), t, fKT)
                        Rp.free[k] = [t_kt]
                    for c in range(4):
                        k, p, fr = Rp.take()
                        xt = tile(XT, b * 8 + 4 * i + c)
                        o = g * 256

                        def f(p=p, xt=xt, o=o):
                            mm(p[:, 0:256], xt, cWk[:, o:o + 256])
                            return mm(p[:, 256:512], xt, cWv[:, o:o + 256])
                        t = PE.do(f, fr)
                        kr = Kr[:, c * 256:(c + 1) * 256]
                        t1 = V.do(lambda p=p, kr=kr, o=o: tt(kr, p[:, 0:256], bkr[:, o:o + 256], ALU.add), t, (s_kv, 32), t_kr)
                        t_v = V.do(lambda p=p, c=c, o=o: tt(V5[:, c, :, 0:64], g3(p[:, 256:512], 4), g3(bvr[:, o:o + 256], 4), ALU.add), fV, t_one)
                        Rp.free[k] = [t_v]
                        n = 4 * i + c
                        A.do(lambda c=c, kr=kr, n=n: act(Ke5[:, c, :, 0, :], g3(kr, 4), ACT.Relu, scale=co[:, n:n + 1]), t1, fKe)
                        t_ke = A.do(lambda c=c, kr=kr, n=n: act(Ke5[:, c, :, 1, :], g3(kr, 4), ACT.Relu, scale=co[:, 8 + n:9 + n]))
                    t_kr = t_ke
                    for c in range(4):
                        n = 4 * i + c
                        k, pa, fr = Ra.take()

                        def f(pa=pa, c=c):
                            for h in range(4):
                                r0 = 64 * (h % 2)
                                r = mm(pa[:, h % 2, h // 2, :],
                                       KT[r0:r0 + 64, (h // 2) * 512 + c * 128:(h // 2) * 512 + (c + 1) * 128],
                                       Qr[r0:r0 + 64, h * 512 + c * 128:h * 512 + (c + 1) * 128])
                            return r
                        t = PE.do(f, fr, t_qr, t_kt)
                        ka, am, fa = AM.take()
                        t_am = V.do(lambda am=am, pa=pa: tt(a4(am), pa, dm, ALU.mult), t, fa)
                        Ra.free[k] = [t_am]
                        ko, po, fo = Ro.take()

                        def f(po=po, c=c, am=am, n=n):
                            for h in range(4):
                                r = mm(po[:, h * 65:(h + 1) * 65], a4(am)[:, h % 2, h // 2, :], V5[:, c, h, :], True, n == 0)
                                if n > 0:
                                    r = mm(po[:, h * 65:(h + 1) * 65], Qe[:, h * 512 + c * 128:h * 512 + (c + 1) * 128],
                                           Sb[:, h * 65:(h + 1) * 65], False, True)
                            return r
                        t_o = PE.do(f, t_am, t_v, t_qe, t_cp, fo)
                        AM.free[ka] = [t_o]
                        if n < 7:
                            def f(c=c, n=n):
                                for h in range(4):
                                    r = mm(Sp[:, h * 65:(h + 1) * 65], Ke5[:, c, h, :, :].rearrange("p s d -> p (s d)"),
                                           V5[:, c, h, :], n == 0 and h == 0, n == 6, skip_group_check=True)
                                return r
                            t = PE.do(f, t_ke, t_cp)
                            t_cp = A.do(lambda: nc.scalar.copy(Sb, Sp[:, 0:260]), t, t_o)
                        o4 = po[:, 0:260].rearrange("p (h d) -> p h d", h=4)
                        t = V.do(lambda o4=o4: ts(den, o4[:, :, 64], 1e-6, None, ALU.max), t_o)
                        t = V.do(lambda: nc.vector.reciprocal(den, den), t)
                        t_ok = V.do(lambda o4=o4, c=c: tt(g3(Ok[:, c * 256:(c + 1) * 256], 4), o4[:, :, 0:64], bin_(den, 4, 64), ALU.mult),
                                    t, fOk)
                        Ro.free[ko] = [t_ok]
                    last = PE.n
                    fQr = fQe = fKT = fKe = fV = [(PE.sem, last)]
                    fQr = [(PE.sem, last), t_qe]
                    for h in range(2):
                        def f(h=h):
                            for c in range(4):
                                r = nc.tensor.transpose(PS[7][:, c * 128:(c + 1) * 128], Ok[:, c * 256 + h * 128:c * 256 + (h + 1) * 128], w("ident"))
                            return r
                        t = PE.do(f, t_ok, f7)
                        f7 = t_ot = A.do(lambda h=h: nc.scalar.copy(ch(OT, h), PS[7]), t, fOT)
                        fOk = t
                    k, p, fr = Rp.take()

                    def f(p=p, g=g):
                        for h in range(2):
                            r = mm(p, cWo[:, (2 * g + h) * 128:(2 * g + h + 1) * 128], ch(OT, h), h == 0, h == 1)
                        return r
                    t = fOT = PE.do(f, t_ot, fr)
                    y = ch(XK, 2 * b + i)
                    if g == 0:
                        t = V.do(lambda p=p, y=y, x=x: stt(y, p, w("cbo"), x, ALU.add, ALU.add), t)
                    else:
                        t = V.do(lambda p=p, y=y: tt(y, p, y, ALU.add), t)
                    Rp.free[k] = [t]
        barrier()

    def softmax8(ar, lg, V8, pr):
        m, s = SM[:, 96:128], SM[:, 128:160]
        l3, p3 = g3(lg, NT), g3(pr, NT)
        t = V.do(lambda: nc.vector.tensor_reduce(m, l3, AX, ALU.max), now())
        t = V.do(lambda: tt(l3, l3, bin_(m, NT, 8), ALU.subtract), t)
        t = A.do(lambda: act(lg, lg, ACT.Exp), t)
        t = V.do(lambda: nc.vector.tensor_reduce(s, l3, AX, ALU.add), t)
        t = V.do(lambda: nc.vector.reciprocal(s, s), t)
        t = V.do(lambda: tt(p3[:, :, 0:8], l3, bin_(s, NT, 8), ALU.mult), t)

        def f():
            for c in range(NT):
                r = nc.vector.max(V8[:, c * 8:c * 8 + 8], pr[:, c * 16:c * 16 + 8])
            return r
        return V.do(f, t)

    def router(rw, lg, bias, wt):
        p = PS[0][:, 0:256]

        def f():
            for c in range(NT):
                r = mm(p[:, c * 8:c * 8 + 8], tile(XT, c), rw)
            return r
        t = PE.do(f, wt)
        if bias is None:
            return V.do(lambda: nc.vector.tensor_copy(lg, p), t)
        return V.do(lambda: tt(g3(lg, NT), g3(p, NT), bias.unsqueeze(1).to_broadcast([128, NT, 8]), ALU.add), t)

    def to_rows(WK, WT, tw):
        Rt = Ring(PS[1:3])
        for i in range(NCH):
            k, p, fr = Rt.take()

            def f(i=i, p=p):
                for j in range(4):
                    c = 4 * i + j
                    r = nc.tensor.transpose(p[0:8, j * 128:(j + 1) * 128], WK[:, c * 8:c * 8 + 8], w("ident"))
                return r
            t = PE.do(f, fr, tw)
            t = A.do(lambda i=i, p=p: nc.scalar.copy(ch(WT, i), p[0:8, :]), t)
            Rt.free[k] = [t]
        return t

    def stage6():
        ar = Arena()
        lg, V8, pr, R = ar(256), ar(256), ar(NT * 16), ar(NT * 16)
        WK, WT = ar(256), ar(T, 8)
        rp = ar(NT * 8)
        s2 = SM[:, 160:192]
        router(w("rwT"), lg, None, wtok(3))
        tp = V.do(lambda: nc.vector.memset(pr, FILL))
        tv = softmax8(ar, lg, V8, pr)
        v3 = g3(V8, NT)
        t = V.do(lambda: stt(s2, v3[:, :, 0], 1e-6, v3[:, :, 1], ALU.add, ALU.add), tv)
        t_s = V.do(lambda: nc.vector.reciprocal(s2, s2), t)
        t = V.do(lambda: nc.vector.memset(rp, FILL))
        t = V.do(lambda: nc.vector.tensor_copy(g3(rp, NT)[:, :, 0:2], v3[:, :, 0:2]), t)

        def f():
            for c in range(NT):
                r = nc.vector.match_replace(R[:, c * 16:c * 16 + 16], rp[:, c * 8:c * 8 + 8], pr[:, c * 16:c * 16 + 16], FILL)
            return r
        t = V.do(f, t)
        r3, q3, w3 = g3(R, NT)[:, :, 0:8], g3(pr, NT)[:, :, 0:8], g3(WK, NT)
        t = V.do(lambda: tt(w3, r3, q3, ALU.not_equal), t)
        t = V.do(lambda: tt(w3, w3, q3, ALU.mult), t)
        t = V.do(lambda: tt(w3, w3, bin_(s2, NT, 8), ALU.mult), t, t_s)
        t_w = to_rows(WK, WT, t)
        Rx, Rg, Rh = Ring([ar(512) for _ in range(2)]), Ring([ar(512) for _ in range(2)]), Ring([ar(512) for _ in range(3)])
        Rb, Rp, Ro = Ring(PS[0:2], [t_w]), Ring([(PS[2], PS[3]), (PS[4], PS[5])], [t_w]), Ring(PS[6:8])
        w13, w2e = w("w13"), w("w2e")
        W4 = wtok(4)
        for i in range(NCH):
            x = ch(XT, i)
            ko, o, fo = Ro.take()
            pend = []

            def down(h, kh, th, n, o=o, fo=fo):
                t = PE.do(lambda: mm(o, w2e[:, n * 128:(n + 1) * 128], h, n == 0, n == 15), th, fo)
                Rh.free[kh] = [t]
                return t
            for e in range(8):
                kb, pb, fb = Rb.take()
                kx, xw, fx = Rx.take()
                t = PE.do(lambda e=e, pb=pb, i=i: mm(pb, w("sel8")[:, e * 128:(e + 1) * 128], ch(WT, i)), fb, t_w)
                tx = V.do(lambda pb=pb, xw=xw, x=x: tt(xw, pb, x, ALU.mult), t, fx)
                Rb.free[kb] = [tx]
                for c in range(2):
                    k, (pg, pu), fr = Rp.take()
                    o1 = e * 512 + c * 128
                    t1 = PE.do(lambda pg=pg, x=x, o1=o1: mm(pg, w13[:, o1:o1 + 128], x), fr, W4)
                    kg, g, fg = Rg.take()
                    t1 = A.do(lambda pg=pg, g=g: act(g, pg, ACT.Silu), t1, fg)
                    t2 = PE.do(lambda pu=pu, xw=xw, o1=o1: mm(pu, w13[:, o1 + 256:o1 + 384], xw), tx)
                    kh, h, fh = Rh.take()
                    t = V.do(lambda h=h, pu=pu, g=g: tt(h, pu, g, ALU.mult), t1, t2, fh)
                    Rp.free[k] = Rg.free[kg] = [t]
                    pend.append((h, kh, t, 2 * e + c))
                    if len(pend) > 1:
                        down(*pend.pop(0))
                Rx.free[kx] = [t2]
            for q in pend:
                to = down(*q)
            t = V.do(lambda o=o, x=x: tt(x, o, x, ALU.add), to)
            Ro.free[ko] = [t]
        barrier()

    def stage7():
        W5 = wtok(5)
        ss, rs, sd = SM[:, 0:32], SM[:, 32:64], SM[:, 212:244]
        negA, car, carx = SM[:, 244:276], SM[:, 276:308], SM[:, 308:314]
        eps = SM[:, 479:480]
        ar = Arena()
        Rj = Ring([ar(512) for _ in range(2)])
        Rt = Ring(PS[0:2])
        t_A = A.do(lambda: act(negA, w("Alog"), ACT.Exp), W5)
        t_A = V.do(lambda: ts(negA, negA, -1.0, None, ALU.mult), t_A)
        for i in range(NCH):
            kj, jk, fj = Rj.take()

            def f(i=i, jk=jk):
                for j in range(4):
                    c = 4 * i + j
                    r = act(jk[:, j * 128:(j + 1) * 128], tile(XK, c), ACT.Square, scale=128 ** -0.5, acc=ss[:, c:c + 1])
                return r
            t = A.do(f, fj)
            Rj.free[kj] = [t]
        t = A.do(lambda: act(sd, ss, ACT.Sqrt, bias=eps), t, t_eps)
        t_rs = V.do(lambda: nc.vector.reciprocal(rs, sd), t)
        for i in range(NCH):
            t = V.do(lambda i=i: tt(g3(ch(XK, i), 4), g3(ch(XK, i), 4), bin_(rs[:, 4 * i:4 * i + 4], 4, 128), ALU.mult), t_rs)
            k, p, fr = Rt.take()

            def f(i=i, p=p):
                for j in range(4):
                    r = nc.tensor.transpose(p[:, j * 128:(j + 1) * 128], tile(XK, 4 * i + j), w("ident"))
                return r
            t = PE.do(f, t, fr)
            t_xn = A.do(lambda i=i, p=p: act(ch(XK, i), p, ACT.Copy, scale=w("normw")), t)
            Rt.free[k] = [t_xn]
        barrier()
        ar = Arena()
        sk, xs, dl, dx, ev = ar(1024), ar(1024), ar(1024), ar(1024), ar(1024)
        xe = [ar(515), ar(515)]
        d1, BC = ar(512, 64), ar(512, 32)
        sB = lambda n: w("ident")[0:32, n:n + 1].to_broadcast([32, 128])
        Rb, Ra, Ru, Rh, Rc = (Ring([ar(512) for _ in range(2)]) for _ in range(5))
        Bp, Cp = Ring(PS[0:2]), Ring(PS[2:4])
        Yp = PS[4:6]
        Rp = Ring(PS[6:8])
        skT, inT, cw, cb = w("skT"), w("inT"), w("convw"), w("convb")
        for i in range(NCH):
            b, first = i // 2, i % 2 == 0
            xn = ch(XK, i)
            n0 = now()
            for e in range(2):
                k, p, fr = Rp.take()
                t = PE.do(lambda p=p, e=e, xn=xn: mm(p, tile(skT, e), xn), fr, n0)
                t_sk = A.do(lambda p=p, e=e: act(ch(sk, e), p, ACT.Silu), t, n0)
                Rp.free[k] = [t_sk]
                k, p, fr = Rp.take()
                t = PE.do(lambda p=p, e=e, xn=xn: mm(p, tile(inT, e), xn), fr)
                if first:
                    t2 = V.do(lambda e=e: nc.vector.memset(xe[e][:, 0:3], 0.0), n0)
                else:
                    t2 = V.do(lambda e=e: nc.vector.tensor_copy(xe[e][:, 0:3], carx[:, 3 * e:3 * e + 3]), n0)
                t = V.do(lambda p=p, e=e: nc.vector.tensor_copy(xe[e][:, 3:515], p), t)
                Rp.free[k] = [t]
                t3 = V.do(lambda e=e: nc.vector.tensor_copy(carx[:, 3 * e:3 * e + 3], xe[e][:, 512:515]), t, t2)
                v = ch(ev, e)
                t = V.do(lambda e=e, v=v: ts(v, xe[e][:, 0:512], cw[:, 4 * e:4 * e + 1], cb[:, e:e + 1], ALU.mult, ALU.add), t, t2)
                for j in range(1, 4):
                    t = V.do(lambda e=e, v=v, j=j: stt(v, xe[e][:, j:j + 512], cw[:, 4 * e + j:4 * e + j + 1], v, ALU.mult, ALU.add), t)
                t_xs = A.do(lambda e=e, v=v: act(ch(xs, e), v, ACT.Silu), t)
            k, p, fr = Rp.take()

            def f(p=p):
                for e in range(2):
                    r = mm(p[0:64, :], w("wd1T")[:, e * 64:(e + 1) * 64], ch(xs, e), e == 0, e == 1)
                return r
            t = PE.do(f, t_xs, fr)
            t_d1 = V.do(lambda p=p: nc.vector.tensor_copy(d1, p[0:64, :]), t)
            Rp.free[k] = [t_d1]
            k, p, fr = Rp.take()

            def f(p=p):
                for e in range(2):
                    r = mm(p[0:32, :], w("wbcT")[:, e * 32:(e + 1) * 32], ch(xs, e), e == 0, e == 1)
                return r
            t = PE.do(f, fr)
            t_bc = V.do(lambda p=p: nc.vector.tensor_copy(BC, p[0:32, :]), t)
            Rp.free[k] = [t_bc]
            for e in range(2):
                k, p, fr = Rp.take()
                t = PE.do(lambda p=p, e=e: mm(p, w("wd2T")[:, e * 128:(e + 1) * 128], d1), t_d1, fr)
                t2 = V.do(lambda p=p, e=e: ts(ch(dl, e), p, w("wd2b")[:, e:e + 1], 0.0, ALU.add, ALU.max), t)
                t1 = A.do(lambda p=p, e=e: act(ch(ev, e), p, ACT.Abs, bias=w("wd2b")[:, e:e + 1]), t2)
                Rp.free[k] = [t1, t2]
            t = A.do(lambda: act(ev, ev, ACT.Exp, scale=-1.0), t1)
            t = A.do(lambda: act(ev, ev, ACT.Ln, bias=1.0), t)
            t_dl = V.do(lambda: tt(dl, dl, ev, ALU.add), t, t2)
            t_dx = V.do(lambda: tt(dx, dl, xs, ALU.mult), t_dl)
            for n in range(16):
                kb, pb, fb = Bp.take()
                kc, pc, fc = Cp.take()
                t = PE.do(lambda pb=pb, n=n: mm(pb, sB(n), BC), t_bc, fb)
                t_c = PE.do(lambda pc=pc, n=n: mm(pc, sB(16 + n), BC), fc)
                kB, Bs, fB = Rb.take()
                t_b = A.do(lambda pb=pb, Bs=Bs: nc.scalar.copy(Bs, pb), t, fB)
                Bp.free[kb] = [t_b]
                for e in range(2):
                    q = e * 16 + n
                    ka, a, fa = Ra.take()
                    t_a = A.do(lambda a=a, e=e, q=q: act(a, ch(dl, e), ACT.Exp, scale=negA[:, q:q + 1]), t_dl, fa, t_A)
                    ku, u, fu = Ru.take()
                    t_u = G.do(lambda u=u, e=e, Bs=Bs: nc.gpsimd.tensor_tensor(u, ch(dx, e), Bs, ALU.mult), t_b, t_dx, fu)
                    kh, h, fh = Rh.take()
                    ini = 0.0 if first else car[:, q:q + 1]
                    t_h = V.do(lambda h=h, a=a, u=u, ini=ini: nc.vector.tensor_tensor_scan(h, a, u, ini, ALU.mult, ALU.add), t_a, t_u, fh)
                    Ra.free[ka] = Ru.free[ku] = [t_h]
                    kC, hc, fC = Rc.take()
                    t_hc = V.do(lambda hc=hc, h=h, pc=pc: tt(hc, pc, h, ALU.mult), t_h, t_c, fC)
                    t_cr = G.do(lambda h=h, q=q: nc.gpsimd.tensor_copy(car[:, q:q + 1], h[:, 511:512]), t_h)
                    Rh.free[kh] = [t_hc, t_cr]
                    t_y = PE.do(lambda e=e, hc=hc, n=n: mm(Yp[e], w("ident"), hc, n == 0, n == 15), t_hc)
                    Rc.free[kC] = [t_y]
                Rb.free[kB] = [t_u]
                Cp.free[kc] = [t_hc]
            for e in range(2):
                z = ch(ev, e)
                t = V.do(lambda e=e, z=z: stt(z, ch(xs, e), w("WD")[:, e:e + 1], Yp[e], ALU.mult, ALU.add), t_y)
                t = V.do(lambda e=e, z=z: tt(z, z, ch(sk, e), ALU.mult), t)
            k, p, fr = Rp.take()

            def f(p=p):
                for e in range(2):
                    r = mm(p, w("outT")[:, e * 128:(e + 1) * 128], ch(ev, e), e == 0, e == 1)
                return r
            t = PE.do(f, t, fr)
            t = V.do(lambda i=i, p=p: stt(ch(XT, i), ch(XT, i), 2.0, p, ALU.mult, ALU.add), t)
            Rp.free[k] = [t]
        barrier()

    def stage8():
        ar = Arena()
        lg, V8, pr, R = ar(256), ar(256), ar(NT * 16), ar(NT * 16)
        WK, WT, rp, cum = ar(256), ar(T, 8), ar(256), ar(256)
        router(w("Wr"), lg, w("brr"), wtok(6))
        V.do(lambda: nc.vector.memset(pr, FILL))
        tv = softmax8(ar, lg, V8, pr)
        v3, c3 = g3(V8, NT), g3(cum, NT)
        t = V.do(lambda: nc.vector.tensor_copy(c3[:, :, 0], v3[:, :, 0]), tv)
        for j in range(1, 8):
            t = V.do(lambda j=j: tt(c3[:, :, j], c3[:, :, j - 1], v3[:, :, j], ALU.add), t)
        t = V.do(lambda: ts(cum, cum, 0.8, None, ALU.is_lt), t)
        t = V.do(lambda: nc.vector.memset(c3[:, :, 0:1], 1.0), t)
        t = V.do(lambda: tt(rp, V8, cum, ALU.mult), t)
        t = V.do(lambda: ts(cum, cum, -FILL, FILL, ALU.mult, ALU.add), t)
        t = V.do(lambda: tt(rp, rp, cum, ALU.add), t)

        def f():
            for c in range(NT):
                r = nc.vector.match_replace(R[:, c * 16:c * 16 + 16], rp[:, c * 8:c * 8 + 8], pr[:, c * 16:c * 16 + 16], FILL)
            return r
        t = V.do(f, t)
        r3, q3, w3 = g3(R, NT)[:, :, 0:8], g3(pr, NT)[:, :, 0:8], g3(WK, NT)
        t = V.do(lambda: tt(w3, r3, q3, ALU.not_equal), t)
        t = V.do(lambda: tt(w3, w3, q3, ALU.mult), t)
        t_w = to_rows(WK, WT, t)
        Rh = Ring([ar(512) for _ in range(4)])
        Rw, Rv = Ring([ar(512) for _ in range(2)]), Ring([ar(512) for _ in range(2)])
        Rb, Rp, Ro = Ring(PS[0:2], [t_w]), Ring(PS[2:6], [t_w]), Ring(PS[6:8])
        W1, W2, B1, B2 = w("W1"), w("W2"), w("B1"), w("B2")
        W6 = wtok(6)
        t_acc = None
        for i in range(NCH):
            x = ch(XT, i)
            xr = ch(XK, i)
            tc = G.do(lambda x=x, xr=xr: nc.gpsimd.tensor_copy(xr, x))
            for e in range(8):
                kb, pb, fb = Rb.take()
                kw, wb, fw = Rw.take()
                t = PE.do(lambda e=e, pb=pb, i=i: mm(pb, w("sel8")[:, e * 128:(e + 1) * 128], ch(WT, i)), fb, t_w)
                t_wb = A.do(lambda wb=wb, pb=pb: nc.scalar.copy(wb, pb), t, fw)
                Rb.free[kb] = [t_wb]
                ko, o, fo = Ro.take()
                pend = []

                def down(h, kh, th, n, o=o, fo=fo):
                    t = PE.do(lambda: mm(o, W2[:, n * 128:(n + 1) * 128], h, n % 4 == 0, n % 4 == 3), th, fo)
                    Rh.free[kh] = [t]
                    return t
                for c in range(4):
                    n = 4 * e + c
                    k, p, fr = Rp.take()
                    t = PE.do(lambda p=p, n=n, xr=xr: mm(p, W1[:, n * 128:(n + 1) * 128], xr), fr, W6, tc)
                    kh, h, fh = Rh.take()
                    if c % 2:
                        t = A.do(lambda h=h, p=p, n=n: act(h, p, ACT.Relu, bias=B1[:, n:n + 1]), t, fh)
                    else:
                        t = V.do(lambda h=h, p=p, n=n: ts(h, p, B1[:, n:n + 1], 0.0, ALU.add, ALU.max), t, fh)
                    Rp.free[k] = [t]
                    pend.append((h, kh, t, n))
                    if len(pend) > 2:
                        down(*pend.pop(0))
                for q in pend:
                    to = down(*q)
                kv, v, fv = Rv.take()
                t = V.do(lambda v=v, o=o, e=e, wb=wb: stt(v, o, B2[:, e:e + 1], wb, ALU.add, ALU.mult), to, t_wb, fv)
                Ro.free[ko] = Rw.free[kw] = [t]
                t_acc = G.do(lambda x=x, v=v: nc.gpsimd.tensor_tensor(x, x, v, ALU.add), t, tc, t_acc)
                Rv.free[kv] = [t_acc]
        barrier()


    stages = [stage1, stage2, stage3, stage4, stage5, stage6, stage7, stage8]
    for k in range(START, STOP + 1):
        stages[k - 1]()
        layernorm(last=(k == STOP), src=XK if k == 5 else XT)

    for g, (a, b) in enumerate(spans):
        S.items.insert(g + (1 if g > 0 else 0), (lambda a=a, b=b: nc.sync.dma_start(W[:, a:b], wp[:, a:b]), (), s_w[g], 16))
        if g == 0:
            S.items.insert(1, (lambda: nc.sync.dma_start(XT, xT_d), (), s_x, 16))
    pre = [(lambda: nc.scalar.dma_start(XK, xK_d), (), s_cs, 16)] if START > 1 else []
    A.items[:0] = pre
    if START > 1:
        for q in engines:
            k = 1 if q is A else 0
            q.items.insert(k, (None, [(s_cs, 16), (s_x, 16)] + [(s, 16) for s in s_w], None, 0))
    S.items.append((None, [(s_out, 16 * NCH)], None, 0))

    block = ctx.enter_context(nc.Block())

    @block.tensor
    def _(e):
        PE.emit(e)

    @block.vector
    def _(e):
        V.emit(e)

    @block.scalar
    def _(e):
        A.emit(e)

    @block.gpsimd
    def _(e):
        G.emit(e)

    @block.sync
    def _(e):
        S.emit(e)

    ctx.close()


def constants():
    p = np.arange(128)
    c = {}
    c["ident"] = np.eye(128)
    c["cen"] = np.eye(128) - 1.0 / 128
    c["ones"] = np.ones((128, 128))
    c["one64"] = np.full((64, 1), 1.0 / 64)
    c["hm"] = (p[:, None] // 8 == np.arange(16)[None]) * 1.0
    r = np.arange(112)
    c["hmT"] = (r[:, None] % 16 == p[None] // 8) * 1.0
    e = np.zeros((64, 4, 112))
    for b in range(4):
        for j in range(112):
            e[b * 16 + j % 16, b, j] = 1
    c["E64"] = e.reshape(64, -1)
    c["ucol"] = r[:, None] // 16 + 7.0 * np.arange(5)[None] + 1
    c["tokid"] = p[:, None] + 128.0 * np.arange(8)[None]
    c["iotau"] = np.broadcast_to((np.arange(560) // 16 + 1.0)[None], (128, 560))
    s = np.zeros((8, 8, 128))
    for i in range(8):
        s[i, i] = 1
    c["sel8"] = s.reshape(8, -1)
    th = np.float32(np.pi / 2048) * np.arange(1024, dtype=np.float32)
    co, si = np.cos(th, dtype=np.float32), np.sin(th, dtype=np.float32)
    d = np.pi / 2048 * (p[None, :] - p[:, None])
    c["dmask"] = np.where(p[None, :] >= p[:, None], np.cos(d), 0.0)
    c["coss"] = np.concatenate([co.reshape(8, 128).T, si.reshape(8, 128).T], 1)
    c = {k: np.asarray(v, np.float32) for k, v in c.items()}
    cs = np.concatenate([np.broadcast_to(co, (64, 1024)), np.broadcast_to(si, (64, 1024))], 0).astype(np.float32)
    return c, np.ascontiguousarray(cs)


def kernel(**inputs):
    from concourse import bacc as _bacc
    from concourse.bass_utils import run_bass_kernel_spmd as _run
    I = {k: np.asarray(v) for k, v in inputs.items()}
    c, cs = constants()
    P = dict(c)
    col = lambda a: a.reshape(-1, 128).T
    rep = lambda a, n=128: np.broadcast_to(a.reshape(1, -1), (n, a.size))
    ck = lambda a: a.reshape(-1, 128, a.shape[-1]).transpose(1, 0, 2).reshape(128, -1)
    for l in range(2):
        P[f"Wz{l}"], P[f"Wh{l}"] = I[f"L0_attn_Wz{l}"].T, I[f"L0_attn_Wh{l}"].T
    P["b_l0a"] = np.stack([I["L0_attn_" + n] for n in ("bz0", "bh0", "bz1", "bh1")], 1)
    f = lambda n: I["L0_ffn_" + n]
    P["slot"], P["slotT"] = f("slot_init"), f("slot_init").T
    P["w1"] = ck(f("w1"))
    P["w2"], P["WihT"], P["WhhT"] = f("w2"), f("Wih").T, f("Whh").T
    for n in ("wq", "wk", "wv", "wvp", "wo"):
        P[n] = f(n)
    P["b1"], P["b2r"], P["tau"] = f("b1")[:, None], rep(f("b2")), rep(f("tau"))
    P["bih"], P["bhh"], P["bq"], P["bk"] = col(f("bih")), col(f("bhh")), f("bq")[:, None], f("bk")[:, None]
    P["bvr"], P["lng"], P["lnb"], P["bvp"], P["bo"] = rep(f("bv"), 64), col(f("ln_g")), col(f("ln_b")), col(f("bvp")), col(f("bo"))
    f = lambda n: I["L1_attn_" + n]
    for n in ("Wq", "Wk", "Wv", "Wo"):
        P["a" + n] = f(n)
    P["abq"], P["abk"], P["abvr"], P["abo"] = col(f("bq")), col(f("bk")), rep(f("bv")), col(f("bo"))
    f = lambda n: I["L1_ffn_" + n]
    P["gate0"], P["gate1"] = (np.broadcast_to(f("gate_w")[e][:, None], (128, 128)) for e in range(2))
    P["fw1"] = f("w1").transpose(1, 0, 2).reshape(128, -1)
    P["fb1"], P["fw2"] = col(f("b1")), ck(f("w2").reshape(1024, 128))
    P["fb2"], P["sw1"], P["sb1"], P["sw2"], P["sb2"] = col(f("b2")), f("sw1"), col(f("sb1")), ck(f("sw2")), col(f("sb2"))
    f = lambda n: I["L2_attn_" + n]
    P["cWq"], P["cWk"], P["cWv"], P["cWo"] = f("Wq"), f("Wk"), f("Wv"), ck(f("Wo"))
    bq = f("bq").reshape(16, 64).T
    P["cbq2"], P["cbk"], P["cbo"] = np.concatenate([bq, bq], 0), col(f("bk")), col(f("bo"))
    P["rwT"] = I["L2_ffn_router_w"].T
    P["w13"] = I["L2_ffn_w13"].transpose(1, 0, 2).reshape(128, -1)
    P["w2e"] = ck(I["L2_ffn_w2"].reshape(2048, 128))
    f = lambda n: I["L3_attn_" + n]
    P["normw"], P["skT"], P["inT"] = col(f("norm_w")), f("skip_w").T, f("in_w").T
    P["convw"], P["convb"] = ck(f("conv_w").reshape(256, 4)), col(f("conv_b"))
    P["wd1T"], P["wd2T"], P["wd2b"] = ck(f("wd1").T), f("wd2").T, col(f("wd2_b"))
    P["wbcT"] = ck(np.concatenate([f("wb"), f("wc")], 0).T)
    P["Alog"], P["WD"], P["outT"] = ck(f("A_log")), col(f("W_D")), ck(f("out_w").T)
    f = lambda n: I["L3_ffn_" + n]
    P["Wr"], P["brr"] = f("Wr"), rep(f("br"))
    P["W1"], P["B1"] = f("W1").transpose(1, 0, 2).reshape(128, -1), col(f("b1"))
    P["W2"], P["B2"] = ck(f("W2").reshape(4096, 128)), col(f("b2"))

    cols = []
    for g in GROUPS:
        for name, r, n in g:
            a = P[name]
            assert a.shape == (r, n) and a.dtype == np.float32, (name, a.shape, a.dtype)
            if r < 128:
                a = np.concatenate([a, np.zeros((128 - r, n), np.float32)], 0)
            cols.append(a)
    x = I["L0_attn_x"]
    arrays = {
        "wp": np.ascontiguousarray(np.concatenate(cols, 1)),
        "xT": np.ascontiguousarray(x.reshape(T, D).T),
        "sidx": np.ascontiguousarray(I["L1_attn_sample_idx"].reshape(1, 35)),
        "cs": cs,
        "bkv": np.ascontiguousarray(np.stack([I["L2_attn_bk"], I["L2_attn_bv"]], 0)),
    }
    if START > 1:
        arrays["xK"] = np.ascontiguousarray(x.reshape(NT, 128, D).transpose(1, 0, 2).reshape(128, T))
    nc = _bacc.Bacc("TRN2", target_bir_lowering=False, num_devices=1)
    h = {}
    for k, a in arrays.items():
        h[k] = nc.dram_tensor(k, a.shape, mybir.dt.from_np(a.dtype), kind="ExternalInput").ap()
    out = nc.dram_tensor("out", (NB, L, D), F32, kind="ExternalOutput").ap()
    build(nc, h["wp"], h["xT"], h.get("xK"), h["sidx"], h["cs"], h["bkv"], out)
    r = _run(nc, [arrays], core_ids=[0])
    return r.results[0]["out"]
```

```python
import numpy as np
import concourse.bass as bass
from concourse import mybir
from contextlib import ExitStack

F32 = mybir.dt.float32
BF16 = mybir.dt.bfloat16
I32 = mybir.dt.int32
ALU = mybir.AluOpType
ACT = mybir.ActivationFunctionType
AX = mybir.AxisListType.X
FILL = -3.0e38

NB, L, D = 4, 1024, 128
T = NB * L
NT = T // 128

START, STOP = 1, 8


class Queue:

    def __init__(self, name, sem):
        self.name, self.sem, self.n, self.items = name, sem, 0, []

    def do(self, fn, *deps):
        self.n += 1
        self.items.append((fn, deps, self.sem, 1))
        return (self.sem, self.n)

    def dma(self, fn, sem, *deps):
        self.items.append((fn, deps, sem, 16))

    def emit(self, eng):
        seen = {}

        def wait(d):
            if d is None:
                return
            if isinstance(d, list):
                for x in d:
                    wait(x)
                return
            sem, v = d
            if v > 0 and seen.get(id(sem), 0) < v:
                eng.wait_ge(sem, v)
                seen[id(sem)] = v

        for fn, deps, sem, k in self.items:
            for d in deps:
                wait(d)
            if fn is not None:
                fn().then_inc(sem, k)


class Ring:

    def __init__(self, bufs, first=None):
        self.bufs, self.i = bufs, -1
        self.free = [first or [] for _ in bufs]

    def take(self):
        self.i = (self.i + 1) % len(self.bufs)
        return self.i, self.bufs[self.i], self.free[self.i]


GROUPS = [
    [("ss2", 64, 32), ("ident", 128, 128), ("cen", 128, 128), ("ones", 128, 128), ("one64", 64, 1), ("hm", 128, 16),
     ("hmT", 112, 128), ("E64", 64, 4 * 112), ("ucol", 112, 5), ("tokid", 128, 8), ("iotau", 128, 560),
     ("sel8", 8, 8 * 128),
     ("Wz0", 128, 128), ("Wh0", 128, 128), ("Wz1", 128, 128), ("Wh1", 128, 128), ("b_l0a", 128, 4)],
    [("slotT", 128, 64), ("slot", 64, 128), ("w1", 128, 128), ("w2", 64, 64), ("WihT", 128, 384), ("WhhT", 128, 384),
     ("wq", 128, 32), ("wk", 128, 32), ("wv", 128, 128), ("wvp", 128, 128), ("wo", 128, 128),
     ("b1", 64, 1), ("b2r", 128, 64), ("tau", 128, 1), ("bih", 128, 3), ("bhh", 128, 3), ("bq", 32, 1), ("bk", 32, 1),
     ("bvr", 64, 128), ("lng", 128, 1), ("lnb", 128, 1), ("bvp", 128, 1), ("bo", 128, 1)],
    [("aWq", 128, 128), ("aWk", 128, 128), ("aWv", 128, 128), ("aWo", 128, 128), ("abq", 128, 1), ("abk", 128, 1),
     ("abvr", 128, 128), ("abo", 128, 1),
     ("gate0", 128, 128), ("gate1", 128, 128), ("fw1", 128, 1024), ("fb1", 128, 8), ("fw2", 128, 1024), ("fb2", 128, 2),
     ("sw1", 128, 512), ("sb1", 128, 4), ("sw2", 128, 512), ("sb2", 128, 1)],
    [("cWq", 128, 1024), ("cWk", 128, 1024), ("cWv", 128, 1024), ("cWo", 128, 1024),
     ("cbq2", 128, 16), ("cbk", 128, 8), ("cbo", 128, 1), ("dmask", 128, 128), ("coss", 128, 16),
     ("rwT", 128, 8)],
    [("w13", 128, 4096), ("w2e", 128, 2048)],
    [("normw", 128, 1), ("skT", 128, 256), ("inT", 128, 256), ("convw", 128, 8), ("convb", 128, 2), ("wd1T", 128, 128),
     ("wd2T", 64, 256), ("wd2b", 128, 2), ("wbcT", 128, 64), ("Alog", 128, 32), ("WD", 128, 2), ("outT", 128, 256)],
    [("Wr", 128, 8), ("brr", 128, 8), ("W1", 128, 4096), ("B1", 128, 32), ("W2", 128, 4096), ("B2", 128, 8)],
]


LATE = 6


def place():
    off, at, spans = 0, {}, []
    for k, g in enumerate(GROUPS):
        if k == LATE:
            keep, off = off, spans[1][0]
        a = off
        for name, r, c in g:
            at[name] = (r, off, c)
            off += c
        spans.append((a, off))
        if k == LATE:
            assert off <= spans[3][1]
            off = keep
    return at, spans, off


def build(nc, wp, xT_d, xK_d, sidx_d, cs_d, bkv_d, out_d):
    at, spans, WN = place()
    names = ["pe", "dve", "act", "pool", "sp"]
    ctx = ExitStack()
    sem = lambda n: ctx.enter_context(nc.semaphore(n))
    PE, V, A, G, S = (Queue(n, sem("q_" + n)) for n in names)
    engines = (PE, V, A, G)
    s_w = [sem(f"s_w{i}") for i in range(len(GROUPS))]
    s_x, s_si, s_cs, s_kv, s_out, s_cs2 = (sem(n) for n in ("s_x", "s_si", "s_cs", "s_kv", "s_out", "s_cs2"))

    W = nc.alloc_sbuf_tensor("W", [128, WN], F32)
    XTt = nc.alloc_sbuf_tensor("XT", [128, T], F32)
    XKt = nc.alloc_sbuf_tensor("XK", [128, T], F32)
    SMN = 512
    SMt = nc.alloc_sbuf_tensor("SM", [128, SMN], F32)
    RN = 1056
    RT = nc.alloc_sbuf_tensor("RT", [128, RN], mybir.dt.float32r)
    TN = (212863 - 4 * (WN + 2 * T + SMN + RN)) // 4 - 64
    TMP = nc.alloc_sbuf_tensor("TMP", [128, TN], F32)
    XT, XK, SM = XTt[:, :], XKt[:, :], SMt[:, :]
    PSALL = nc.alloc_psum_tensor("ps", [128, 4096], F32)[:, :]
    PS = [PSALL[:, i * 512:(i + 1) * 512] for i in range(8)]

    def w(name):
        r, o, c = at[name]
        return W[0:r, o:o + c]

    wtok = lambda g: (s_w[g], 16)

    class Arena:
        def __init__(self):
            self.o = 0

        def __call__(self, cols, rows=128, dt=F32):
            n = cols if dt == F32 or dt == I32 else (cols + 1) // 2
            assert self.o + n <= TN, ("arena", self.o + n, TN)
            v = TMP[:, self.o:self.o + n]
            self.o += n
            if dt != F32:
                v = v.bitcast(dt)
            return v[0:rows, 0:cols]

    def now():
        return [(q.sem, q.n) for q in engines]

    def barrier():
        t = now()
        for q in engines:
            q.items.append((None, t, None, 0))

    def mm(out, lhsT, rhs, start=True, stop=True, **k):
        return nc.tensor.matmul(out, lhsT, rhs, start=start, stop=stop, **k)

    def act(out, in_, f, bias=0.0, scale=1.0, acc=None):
        if acc is None:
            return nc.scalar.activation(out, in_, f, bias=bias, scale=scale)
        return nc.scalar.activation(out, in_, f, bias=bias, scale=scale, accum_out=acc)

    tt = lambda o, a, b, op: nc.vector.tensor_tensor(o, a, b, op)
    ts = lambda o, a, s1, s2, op0, op1=None: (nc.vector.tensor_scalar(o, a, s1, s2, op0, op1) if op1 is not None
                                             else nc.vector.tensor_scalar(o, a, s1, None, op0))
    stt = lambda o, a, s, b, op0, op1: nc.vector.scalar_tensor_tensor(out=o, in0=a, scalar=s, in1=b, op0=op0, op1=op1)

    def g3(ap, n):
        return ap.rearrange("p (n k) -> p n k", n=n)

    def bin_(ap, n, k):
        return ap.unsqueeze(2).to_broadcast([ap.shape[0], n, k])

    def bout(ap, n):
        return ap.unsqueeze(1).to_broadcast([ap.shape[0], n, ap.shape[1]])

    CH = 512
    NCH = T // CH
    ch = lambda ap, i, k=CH: ap[:, i * k:(i + 1) * k]
    tile = lambda ap, i: ap[:, i * 128:(i + 1) * 128]

    t_eps = V.do(lambda: nc.vector.memset(SM[:, 479:480], 1e-5))

    def layernorm(last=False, src=None):
        src = XT if src is None else src
        ar = Arena()
        Rj = Ring([ar(512) for _ in range(2)])
        ss, rs, sd, eps = SM[:, 0:32], SM[:, 32:64], SM[:, 480:512], SM[:, 479:480]
        Rp, Rt = Ring([PS[0], PS[1], PS[2], PS[3]]), Ring([PS[4], PS[5], PS[6], PS[7]])
        pend = []

        def back(i, t_xk):
            k, pt, fr = Rt.take()

            def f(i=i, pt=pt):
                for j in range(4):
                    r = nc.tensor.transpose(pt[:, j * 128:(j + 1) * 128], tile(XK, 4 * i + j), w("ident"))
                return r
            t = PE.do(f, fr, t_xk)
            t = A.do(lambda i=i, pt=pt: nc.scalar.copy(ch(XT, i), pt), t)
            Rt.free[k] = [t]

        for i in range(NCH):
            k, p, fr = Rp.take()

            def f(src=src, i=i, p=p):
                for j in range(4):
                    r = mm(p[:, j * 128:(j + 1) * 128], tile(src, 4 * i + j), w("cen"))
                return r
            t0 = PE.do(f, fr)

            kj, jk, fj = Rj.take()

            def f(ss=ss, i=i, p=p, jk=jk):
                for j in range(4):
                    c = 4 * i + j
                    r = act(jk[:, j * 128:(j + 1) * 128], p[:, j * 128:(j + 1) * 128], ACT.Square, scale=128 ** -0.5, acc=ss[:, c:c + 1])
                return r
            t1 = A.do(f, t0, fj)
            Rj.free[kj] = [t1]
            t2 = A.do(lambda eps=eps, sd=sd, ss=ss, i=i: act(sd[:, 4 * i:4 * i + 4], ss[:, 4 * i:4 * i + 4], ACT.Sqrt, bias=eps), t1, t_eps)
            t2 = V.do(lambda rs=rs, sd=sd, i=i: nc.vector.reciprocal(rs[:, 4 * i:4 * i + 4], sd[:, 4 * i:4 * i + 4]), t2)
            t3 = V.do(lambda rs=rs, i=i, p=p: tt(g3(ch(XK, i), 4), g3(p, 4), bin_(rs[:, 4 * i:4 * i + 4], 4, 128), ALU.mult), t2)
            Rp.free[k] = [t3]
            if last:
                S.dma(lambda i=i: nc.sync.dma_start(
                    out_d.rearrange("b (n p) d -> p (b n) d", p=128)[:, 4 * i:4 * i + 4, :], g3(ch(XK, i), 4)), s_out, t3)
            else:
                pend.append((i, t3))
                if len(pend) > 1:
                    back(*pend.pop(0))
        for x in pend:
            back(*x)
        barrier()

    def stage1():
        ar = Arena()
        H1 = ar(T)
        bufs = [[ar(512) for _ in range(3)] for _ in range(5)]
        Ra, Rz, Rs, Rg, Rh = (Ring(b) for b in bufs)
        Rp = Ring([(PS[2 * i], PS[2 * i + 1]) for i in range(4)])
        nb, bh5 = SM[:, 64:66], SM[:, 66:68]
        b = w("b_l0a")
        t_b = V.do(lambda b=b, nb=nb: ts(nb, b.rearrange("p (l k) -> p k l", k=2)[:, 0, :], -1.0, None, ALU.mult), wtok(0))
        t_b = V.do(lambda b=b, bh5=bh5: ts(bh5, b.rearrange("p (l k) -> p k l", k=2)[:, 1, :], 0.5, None, ALU.add), wtok(0))
        tH = {}

        def part(l, i):
            src = XT if l == 0 else H1
            k, (pz, ph), fr = Rp.take()

            def f(i=i, l=l, ph=ph, pz=pz, src=src):
                mm(pz, w(f"Wz{l}"), ch(src, i))
                return mm(ph, w(f"Wh{l}"), ch(src, i))
            t0 = PE.do(f, fr, wtok(0), (s_x, 16) if l == 0 else tH[(0, i)])
            ka, a, fa = Ra.take()
            kz, z, fz = Rz.take()
            ks, s, fs = Rs.take()
            kg, g, fg = Rg.take()
            t1 = A.do(lambda a=a, l=l, pz=pz: act(a, pz, ACT.Sigmoid, bias=nb[:, l:l + 1], scale=-1.0), t0, t_b, fa)
            t1 = A.do(lambda l=l, pz=pz, z=z: act(z, pz, ACT.Sigmoid, bias=b[:, 2 * l:2 * l + 1]), fz)
            t1 = A.do(lambda l=l, ph=ph, s=s: act(s, ph, ACT.Sigmoid, bias=b[:, 2 * l + 1:2 * l + 2]), fs)
            t2 = V.do(lambda g=g, l=l, ph=ph, s=s: stt(g, ph, bh5[:, l:l + 1], s, ALU.add, ALU.max), t1, fg)
            Rp.free[k] = [t1, t2]
            t3 = V.do(lambda g=g, z=z: tt(g, g, z, ALU.mult), t2)
            if l == 0:
                h = ch(H1, i)
                hprev = H1[:, i * 512 - 1:i * 512] if i % 2 else 0.5
                fh = None
            else:
                kh, h, fh = Rh.take()
                hprev = Rh.bufs[(kh - 1) % 3][:, 511:512] if i % 2 else 0.5
            t4 = V.do(lambda a=a, g=g, h=h, hprev=hprev: nc.vector.tensor_tensor_scan(h, a, g, hprev, ALU.mult, ALU.add), t3, fh, tH.get((l, i - 1)))
            tH[(l, i)] = t4
            Ra.free[ka] = Rz.free[kz] = Rs.free[ks] = Rg.free[kg] = [t4]
            if l == 1:
                t5 = G.do(lambda h=h, i=i: nc.gpsimd.tensor_tensor(ch(XT, i), ch(XT, i), h, ALU.add), t4, (s_x, 16))
                Rh.free[kh] = [t5]

        for i in range(NCH + 1):
            if i < NCH:
                part(0, i)
            if i > 0:
                part(1, i - 1)
        barrier()

    def stage2():
        ar = Arena()
        hb = [ar(512, 64) for _ in range(2)]
        Lg, R, E, AL = ar(NT * 64), ar(NT * 64), ar(NT * 64), ar(NT * 64)
        V8, den, rden = ar(NT * 8), ar(NT), ar(NT)
        aT = [ar(512, 64) for _ in range(2)]
        sm1, b1p, itau = SM[:, 68:69], SM[0:64, 69:70], SM[:, 70:71]
        bsum = SM[:, 71:74]
        siT, rd, gr, gz, gn, tn, Sn = (ar(256) for _ in range(7))
        qk, vK = ar(512, 32), ar(512, 64)
        sc, mx, sm = ar(256, 64), SM[0:64, 74:78], SM[0:64, 78:82]
        sT, yT, yN = ar(256, 64), ar(256), ar(512, 64)
        ss, sd = SM[0:64, 82:86], SM[0:64, 86:90]
        eps = SM[:, 479:480]
        jk = hb[0]
        Zt = hb[1]
        w1, w2, slotT, slot = w("w1"), w("w2"), w("slotT"), w("slot")
        W1 = wtok(1)
        t = PE.do(lambda slot=slot: mm(PS[7][:, 0:1], slot, w("one64")), W1)
        t = V.do(lambda sm1=sm1: nc.vector.tensor_copy(sm1, PS[7][:, 0:1]), t, W1)
        t = PE.do(lambda sm1=sm1, w1=w1: mm(PS[7][0:64, 8:9], w1[:, 64:128], sm1), t)
        t_b1 = V.do(lambda b1p=b1p: tt(b1p, PS[7][0:64, 8:9], w("b1"), ALU.add), t)
        t = V.do(lambda itau=itau: ts(itau, w("tau"), 0.0, None, ALU.max))
        t2 = V.do(lambda: ts(SM[:, 90:91], w("tau"), -1.0, 0.0, ALU.mult, ALU.max))
        t = V.do(lambda itau=itau: stt(itau, itau, 0.1, SM[:, 90:91], ALU.add, ALU.add), t2)
        t_tau = V.do(lambda itau=itau: nc.vector.reciprocal(itau, itau), t)
        t_bs = V.do(lambda bsum=bsum: tt(bsum, w("bih"), w("bhh"), ALU.add))
        Rp, Rl, Rh = Ring([PS[0], PS[1]]), Ring([PS[2][:, 0:256], PS[3][:, 0:256]]), Ring(hb)
        last_m = None
        for i in range(NCH):
            k, p, fr = Rp.take()
            t = PE.do(lambda w1=w1, p=p, i=i: mm(p[0:64, :], w1[:, 0:64], ch(XT, i)), fr)
            kh, h, fh = Rh.take()
            t = A.do(lambda b1p=b1p, p=p, h=h: act(h, p[0:64, :], ACT.Gelu, bias=b1p), t, t_b1, fh)
            Rp.free[k] = [t]
            kl, pl, fl = Rl.take()

            def f(w2=w2, h=h, pl=pl):
                for j in range(4):
                    r = mm(pl[:, j * 64:(j + 1) * 64], tile(h, j), w2)
                return r
            t = PE.do(f, t, fl)
            Rh.free[kh] = [t]
            lg = Lg[:, i * 256:(i + 1) * 256]
            b2 = w("b2r").unsqueeze(1).to_broadcast([128, 4, 64])
            t = V.do(lambda lg=lg, pl=pl, b2=b2: tt(g3(lg, 4), g3(pl, 4), b2, ALU.add), t)
            Rl.free[kl] = [t]
            t = V.do(lambda itau=itau, lg=lg: ts(lg, lg, itau, None, ALU.mult), t, t_tau)

            def f(Lg=Lg, V8=V8, i=i):
                for c in range(4 * i, 4 * i + 4):
                    r = nc.vector.max(V8[:, c * 8:c * 8 + 8], Lg[:, c * 64:c * 64 + 64])
                return r
            t = V.do(f, t)

            def f(Lg=Lg, R=R, V8=V8, i=i):
                for c in range(4 * i, 4 * i + 4):
                    r = nc.vector.match_replace(R[:, c * 64:c * 64 + 64], V8[:, c * 8:c * 8 + 8], Lg[:, c * 64:c * 64 + 64], FILL)
                return r
            last_m = V.do(f, t)
        Lg3, R3, E3, A3 = g3(Lg, NT), g3(R, NT), g3(E, NT), g3(AL, NT)
        v1 = g3(V8, NT)[:, :, 0:1].to_broadcast([128, NT, 64])
        t = V.do(lambda E3=E3, Lg3=Lg3, v1=v1: tt(E3, Lg3, v1, ALU.subtract), last_m)
        te = A.do(lambda E=E: act(E, E, ACT.Exp), t)
        t = V.do(lambda Lg=Lg, R=R: tt(R, R, Lg, ALU.not_equal), last_m)
        t = V.do(lambda E=E, R=R: tt(E, E, R, ALU.mult), te, t)
        t = V.do(lambda E3=E3, den=den: nc.vector.tensor_reduce(den, E3, AX, ALU.add), t)
        t = V.do(lambda den=den, rden=rden: nc.vector.reciprocal(rden, den), t)
        t_al = V.do(lambda A3=A3, E3=E3, rden=rden: tt(A3, E3, bin_(rden, NT, 64), ALU.mult), t)

        def f(A3=A3):
            for b in range(NB):
                for c in range(8):
                    mm(PS[4][:, b * 64:(b + 1) * 64], tile(XK, b * 8 + c), A3[:, b * 8 + c, :], c == 0, c == 7)
                for c in range(8):
                    r = mm(PS[5][:, b * 64:(b + 1) * 64], w("ones"), A3[:, b * 8 + c, :], c == 0, c == 7)
            return r
        t0 = PE.do(f, t_al)
        t = V.do(lambda rd=rd: ts(rd, PS[5][:, 0:256], 1e-8, None, ALU.add), t0)
        t = V.do(lambda rd=rd: nc.vector.reciprocal(rd, rd), t)
        t = V.do(lambda rd=rd, siT=siT: tt(siT, PS[4][:, 0:256], rd, ALU.mult), t)
        s4 = slotT.unsqueeze(1).to_broadcast([128, 4, 64])
        Wih, Whh = w("WihT"), w("WhhT")

        def f(Whh=Whh, Wih=Wih, s4=s4, siT=siT):
            for g in range(2):
                mm(PS[6][:, g * 256:(g + 1) * 256], tile(Wih, g), siT, True, False)
                mm(g3(PS[6][:, g * 256:(g + 1) * 256], 4), tile(Whh, g), s4, False, True)
            mm(PS[7][:, 0:256], tile(Wih, 2), siT)
            return mm(g3(PS[7][:, 256:512], 4), tile(Whh, 2), s4)
        t0 = PE.do(f, t, t_b1)
        t1 = A.do(lambda bsum=bsum, gr=gr: act(gr, PS[6][:, 0:256], ACT.Sigmoid, bias=bsum[:, 0:1]), t0, t_bs)
        tz = A.do(lambda bsum=bsum, gz=gz: act(gz, PS[6][:, 256:512], ACT.Sigmoid, bias=bsum[:, 1:2]))
        t = V.do(lambda gr=gr, tn=tn: stt(tn, PS[7][:, 256:512], w("bhh")[:, 2:3], gr, ALU.add, ALU.mult), t1)
        t = V.do(lambda tn=tn: stt(tn, PS[7][:, 0:256], w("bih")[:, 2:3], tn, ALU.add, ALU.add), t)
        t = A.do(lambda gn=gn, tn=tn: act(gn, tn, ACT.Tanh), t)
        t = V.do(lambda gn=gn, s4=s4, tn=tn: tt(g3(tn, 4), s4, g3(gn, 4), ALU.subtract), t)
        t = V.do(lambda gz=gz, tn=tn: tt(tn, tn, gz, ALU.mult), t, tz)
        t_S = V.do(lambda Sn=Sn, gn=gn, tn=tn: tt(Sn, tn, gn, ALU.add), t)

        def f(Sn=Sn):
            mm(PS[0][0:32, 0:256], w("wq"), Sn)
            return mm(PS[0][0:32, 256:512], w("wk"), Sn)
        t = PE.do(f, t_S)
        tq = V.do(lambda qk=qk: ts(qk[:, 0:256], PS[0][0:32, 0:256], w("bq"), None, ALU.add), t)
        tq = V.do(lambda qk=qk: ts(qk[:, 256:512], PS[0][0:32, 256:512], w("bk"), None, ALU.add), t)

        def f(Sn=Sn):
            for b in range(NB):
                r = mm(PS[1][0:64, b * 128:(b + 1) * 128], Sn[:, b * 64:(b + 1) * 64], w("wv"))
            return r
        t = PE.do(f, t_S)
        tv = V.do(lambda vK=vK: tt(g3(vK, 4), g3(PS[1][0:64, :], 4), w("bvr").unsqueeze(1).to_broadcast([64, 4, 128]), ALU.add), t)

        def f(qk=qk):
            for b in range(NB):
                r = mm(PS[2][0:64, b * 64:(b + 1) * 64], qk[:, b * 64:(b + 1) * 64], qk[:, 256 + b * 64:256 + (b + 1) * 64])
            return r
        t = PE.do(f, tq, last_m)
        s3 = g3(sc, 4)
        p3 = g3(PS[2][0:64, 0:256], 4)
        tm = V.do(lambda mx=mx, p3=p3: nc.vector.tensor_reduce(mx, p3, AX, ALU.max), t)
        t = V.do(lambda mx=mx, p3=p3, s3=s3: tt(s3, p3, bin_(mx, 4, 64), ALU.subtract), tm)
        t = A.do(lambda sc=sc: act(sc, sc, ACT.Exp, scale=32 ** -0.5), t)
        t = V.do(lambda s3=s3, sm=sm: nc.vector.tensor_reduce(sm, s3, AX, ALU.add), t)
        t = V.do(lambda sm=sm: nc.vector.reciprocal(sm, sm), t)
        t = V.do(lambda s3=s3, sm=sm: tt(s3, s3, bin_(sm, 4, 64), ALU.mult), t)

        def f(sc=sc):
            for b in range(NB):
                r = nc.tensor.transpose(PS[3][0:64, b * 64:(b + 1) * 64], sc[:, b * 64:(b + 1) * 64], w("ident")[0:64, 0:64])
            return r
        t = PE.do(f, t, last_m)
        t = V.do(lambda sT=sT: nc.vector.tensor_copy(sT, PS[3][0:64, 0:256]), t)

        def f(sT=sT, vK=vK):
            for b in range(NB):
                r = mm(PS[0][:, b * 64:(b + 1) * 64], vK[:, b * 128:(b + 1) * 128], sT[:, b * 64:(b + 1) * 64])
            return r
        t = PE.do(f, t, tv)
        t = V.do(lambda Sn=Sn, yT=yT: tt(yT, PS[0][:, 0:256], Sn, ALU.add), t)

        def f(yT=yT):
            for b in range(NB):
                r = mm(PS[1][0:64, b * 128:(b + 1) * 128], yT[:, b * 64:(b + 1) * 64], w("cen"))
            return r
        t0 = PE.do(f, t)

        def f(jk=jk, ss=ss):
            for b in range(NB):
                r = act(jk[:, b * 128:(b + 1) * 128], PS[1][0:64, b * 128:(b + 1) * 128], ACT.Square, scale=128 ** -0.5, acc=ss[:, b:b + 1])
            return r
        t = A.do(f, t0)
        t = A.do(lambda eps=eps, sd=sd, ss=ss: act(sd, ss, ACT.Sqrt, bias=eps[0:64, :]), t, t_eps)
        t = V.do(lambda sd=sd: nc.vector.reciprocal(sd, sd), t)
        t = V.do(lambda sd=sd, yN=yN: tt(g3(yN, 4), g3(PS[1][0:64, :], 4), bin_(sd, 4, 128), ALU.mult), t)

        def f(yN=yN):
            for b in range(NB):
                r = nc.tensor.transpose(PS[0][:, b * 64:(b + 1) * 64], yN[:, b * 128:(b + 1) * 128], w("ident")[0:64, 0:64])
            return r
        t = PE.do(f, t)
        t = V.do(lambda yT=yT: ts(yT, PS[0][:, 0:256], w("lng"), w("lnb"), ALU.mult, ALU.add), t)
        t = PE.do(lambda yT=yT: mm(PS[1][:, 0:256], w("wvp"), yT), t)
        t = V.do(lambda siT=siT: ts(siT, PS[1][:, 0:256], w("bvp"), None, ALU.add), t)

        def f(siT=siT):
            for b in range(NB):
                r = mm(PS[0][0:64, b * 128:(b + 1) * 128], siT[:, b * 64:(b + 1) * 64], w("wo"))
            return r
        t = PE.do(f, t)
        t_Z = V.do(lambda Zt=Zt: nc.vector.tensor_copy(Zt, PS[0][0:64, :]), t)
        Rt, Ra, Ro = Ring([PS[4], PS[5]], [t_Z]), Ring(aT), Ring([PS[6], PS[7]], [t_S])
        for i in range(NCH):
            k, p, fr = Rt.take()

            def f(A3=A3, i=i, p=p):
                for j in range(4):
                    r = nc.tensor.transpose(p[0:64, j * 128:(j + 1) * 128], A3[:, 4 * i + j, :], w("ident"))
                return r
            t = PE.do(f, fr)
            ka, a, fa = Ra.take()
            t = A.do(lambda a=a, p=p: nc.scalar.copy(a, p[0:64, :]), t, fa)
            Rt.free[k] = [t]
            ko, o, fo = Ro.take()
            b = i // 2
            t = PE.do(lambda Zt=Zt, a=a, o=o, b=b: mm(o, Zt[:, b * 128:(b + 1) * 128], a), t, t_Z, fo)
            Ra.free[ka] = [t]
            t = V.do(lambda i=i, o=o: stt(ch(XT, i), o, w("bo"), ch(XT, i), ALU.add, ALU.add), t)
            Ro.free[ko] = [t]
        barrier()

    def stage3():
        ar = Arena()
        W2 = wtok(2)
        NU = 560
        SO = ar(280)
        sidx, sif = ar(35, dt=I32), ar(35)
        KTb = ar(1024)
        Kbk = [ar(576), ar(576)]
        ks = ar(35)
        MK = ar(512)
        MT = ar(1024, 64)
        cand = SM[0:64, 192:200]
        one64 = ar(1024, 64)
        posT = ar(1024, 64)
        PK = ar(512)
        xs = ar(35)
        rsum = SM[:, 93:94]
        t = G.do(None)if False else None
        G.dma(lambda sidx=sidx: nc.gpsimd.dma_start(sidx, sidx_d.partition_broadcast(128)), s_si, now())
        t = V.do(lambda sidx=sidx, sif=sif: nc.vector.tensor_copy(sif, sidx), (s_si, 16), W2)
        tid = w("tokid")
        t = V.do(lambda SO=SO, sif=sif, tid=tid: tt(g3(SO, 8), sif.unsqueeze(1).to_broadcast([128, 8, 35]), bin_(tid, 8, 35), ALU.is_equal), t)
        t_so = t
        Rq, Rk = Ring([ar(512) for _ in range(2)]), Ring(Kbk)
        Rp = Ring([PS[0], PS[1]])
        Rm = Ring([(PS[2], PS[3]), (PS[4], PS[5])])
        hm = w("hm")
        MK4 = MK.rearrange("p (c b h) -> p c b h", c=8, b=4)
        t_mk = None
        t_xs = t_kb = None
        for b in range(NB):
            def f(SO=SO, b=b):
                for c in range(8):
                    r = mm(PS[6][:, 0:35], tile(XK, b * 8 + c), SO[:, c * 35:(c + 1) * 35], c == 0, c == 7)
                return r
            t = PE.do(f, t_so, t_kb)
            t = V.do(lambda xs=xs: nc.vector.tensor_copy(xs, PS[6][:, 0:35]), t)
            t = PE.do(lambda xs=xs: mm(PS[7][:, 0:35], w("aWk"), xs), t, W2)
            t = V.do(lambda ks=ks: ts(ks, PS[7][:, 0:35], w("abk"), None, ALU.add), t)
            kk, kb, fk = Rk.take()
            kv = kb.rearrange("p (g c) -> p g c", g=2)
            ksum = SM[:, 94:95]
            t2 = V.do(lambda ks=ks, ksum=ksum: nc.vector.tensor_reduce(ksum, ks, AX, ALU.add), t)
            for g in range(2):
                mk = hm[:, g * 8:g * 8 + 8]
                t_kb = V.do(lambda ks=ks, kv=kv, g=g, mk=mk: tt(kv[:, g, 0:280].rearrange("p (h s) -> p h s", h=8),
                            ks.unsqueeze(1).to_broadcast([128, 8, 35]), bin_(mk, 8, 35), ALU.mult), t, fk)
                t_kb = V.do(lambda ksum=ksum, kv=kv, g=g, mk=mk: ts(kv[:, g, 280:288], mk, ksum, None, ALU.mult), t2)
            for i in range(2):
                k, p, fr = Rp.take()
                t = PE.do(lambda p=p, b=b, i=i: mm(p, w("aWq"), ch(XT, 2 * b + i)), fr)
                kq, q, fq = Rq.take()
                t = A.do(lambda p=p, q=q: act(q, p, ACT.Identity, bias=w("abq")), t, fq)
                Rp.free[k] = [t]
                for j in range(4):
                    km, pm, fm = Rm.take()

                    def f(q=q, j=j, pm=pm, kv=kv):
                        for g in range(2):
                            r = mm(pm[g][:, 0:288], tile(q, j), kv[:, g, :])
                        return r
                    tq = PE.do(f, t, t_kb, fm)
                    c = 4 * i + j
                    for g in range(2):
                        m = MK4[:, c, b, g * 8:g * 8 + 8]
                        t2 = V.do(lambda pm=pm, g=g, m=m: nc.vector.tensor_reduce(
                            m, pm[g][:, 0:280].rearrange("p (h s) -> p h s", h=8), AX, ALU.max), tq)
                        t_mk = V.do(lambda pm=pm, g=g, m=m: stt(m, pm[g][:, 280:288], -1.0 / 35, m, ALU.mult, ALU.add), t2)
                    Rm.free[km] = [t_mk]
                Rq.free[kq] = [tq]
            Rk.free[kk] = [tq]

        def f(MK=MK):
            for c in range(8):
                r = nc.tensor.transpose(PS[c // 4][0:64, (c % 4) * 128:(c % 4 + 1) * 128], MK[:, c * 64:(c + 1) * 64], w("ident"))
            return r
        t = PE.do(f, t_mk, now())
        for i in range(2):
            t = V.do(lambda MT=MT, i=i: nc.vector.tensor_scalar(ch(MT, i), PS[i][0:64, :], 8 ** -0.5, None, ALU.mult), t)
        for r in range(5):
            t = V.do(lambda MT=MT, cand=cand: nc.vector.max(cand, MT), t)
            if r == 4:
                t = V.do(lambda cand=cand: nc.vector.memset(cand[:, 3:8], FILL), t)
            t = V.do(lambda MT=MT, cand=cand: nc.vector.match_replace(MT, cand, MT, FILL), t)
        t1 = V.do(lambda one64=one64: nc.vector.memset(one64, 1.0))
        t = V.do(lambda MT=MT: ts(MT, MT, FILL, None, ALU.is_equal), t)
        t = V.do(lambda MT=MT, one64=one64, posT=posT: nc.vector.tensor_tensor_scan(posT, one64, MT, 0.0, ALU.mult, ALU.add), t, t1)
        t_pos = V.do(lambda MT=MT, posT=posT: tt(posT, posT, MT, ALU.mult), t)

        def f(posT=posT):
            for c in range(8):
                r = nc.tensor.transpose(PS[2][:, c * 64:(c + 1) * 64], tile(posT, c), w("ident")[0:64, 0:64])
            return r
        t = PE.do(f, t_pos)
        t_pk = V.do(lambda PK=PK: nc.vector.tensor_copy(PK, PS[2]), t)
        PK4 = PK.rearrange("p (c b h) -> p c b h", c=8, b=4)

        barrier()
        ar.o = 280 + 70 + 1024 + 1152 + 35 + 512 + 1024 + 1024 + 1024 + 512 + 35
        SO2 = SO
        Roh = Ring([ar(NU), ar(NU)])
        Xs, Qb, VK = ar(NU), ar(NU), ar(1024)
        PR = ar(1024, 112)
        PTt = ar(1024)[:, 0:896]
        Ob = ar(640, 112)
        vmc = SM[:, 95:96]
        vmr = ar(128, 112)
        posB = ar(1024, 112)
        OHT = [ar(512, 112), ar(512, 112)]
        outT = ar(512)
        hmT = w("hmT")
        nmx = SM[:, 200:201]
        iota3 = w("iotau").rearrange("p (u h) -> p u h", h=16)
        Xs3, Qb3 = Xs.rearrange("p (u h) -> p u h", h=16), Qb.rearrange("p (u h) -> p u h", h=16)
        Roo = Ring(OHT)
        for b in range(NB):
            def f(b=b):
                for i in range(2):
                    r = mm(PS[4 + i], w("aWk"), ch(XT, 2 * b + i))
                return r
            t = PE.do(f, now())
            for i in range(2):
                t_k = A.do(lambda KTb=KTb, i=i: act(ch(KTb, i), PS[4 + i], ACT.Identity, bias=w("abk")), t, now())
            for i in range(2):
                def f(b=b, i=i):
                    for j in range(4):
                        r = mm(PS[6 + i][:, j * 128:(j + 1) * 128], tile(XT, b * 8 + 4 * i + j), w("aWv"))
                    return r
                t = PE.do(f)
                t_v = V.do(lambda VK=VK, i=i: tt(g3(ch(VK, i), 4), g3(PS[6 + i], 4), w("abvr").unsqueeze(1).to_broadcast([128, 4, 128]), ALU.add), t)
            for c in range(8):
                ko, oh, fo = Roh.take()
                t = V.do(lambda PK4=PK4, iota3=iota3, oh=oh, c=c, b=b: tt(oh.rearrange("p (u h) -> p u h", h=16),
                         PK4[:, c, b, :].unsqueeze(1).to_broadcast([128, 35, 16]), iota3, ALU.is_equal), fo, t_k)

                def f(oh=oh, c=c, b=b):
                    for g in range(2):
                        r = mm(PS[g][:, 0:280], tile(XK, b * 8 + c), oh[:, g * 280:(g + 1) * 280], c == 0, c == 7)
                    return r
                t = PE.do(f, t)
                Roh.free[ko] = [t]
            for g in range(2):
                t2 = V.do(lambda Xs=Xs, g=g: nc.vector.tensor_copy(Xs[:, g * 280:(g + 1) * 280], PS[g][:, 0:280]), t)

            def f(Xs=Xs):
                for g in range(2):
                    r = mm(PS[2 + g][:, 0:280], w("aWq"), Xs[:, g * 280:(g + 1) * 280])
                return r
            t = PE.do(f, t2)
            for g in range(2):
                t2 = V.do(lambda Xs=Xs, g=g: ts(Xs[:, g * 280:(g + 1) * 280], PS[2 + g][:, 0:280], w("abq"), None, ALU.add), t)
            t_q = V.do(lambda Qb3=Qb3, Xs3=Xs3, hm=hm: tt(Qb3, Xs3, hm.unsqueeze(1).to_broadcast([128, 35, 16]), ALU.mult), t2)

            def f(VK=VK):
                for c in range(8):
                    mm(PS[6][:, 0:1], tile(VK, c), w("ones")[:, 0:1], c == 0, c == 7)
                for c in range(8):
                    r = mm(PS[7][0:112, 0:128], w("ones")[:, 0:112], tile(VK, c), c == 0, c == 7)
                return r
            t = PE.do(f, t_v)
            t = V.do(lambda vmc=vmc: ts(vmc, PS[6][:, 0:1], 1.0 / 1024, None, ALU.mult), t)
            t_vm = V.do(lambda vmr=vmr: ts(vmr, PS[7][0:112, 0:128], 1.0 / 1024, None, ALU.mult))
            for j in range(5):
                def f(KTb=KTb, Qb=Qb, j=j):
                    for i in range(2):
                        r = mm(PS[i][0:112, :], Qb[:, j * 112:(j + 1) * 112], ch(KTb, i))
                    return r
                t = PE.do(f, t_q, t_k, now())
                for i in range(2):
                    t1 = V.do(lambda i=i: nc.vector.tensor_reduce(SM[0:112, 201 + i:202 + i], PS[i][0:112, :], AX, ALU.max), t)
                t = V.do(lambda nmx=nmx: tt(nmx[0:112, :], SM[0:112, 201:202], SM[0:112, 202:203], ALU.max), t1)
                t = V.do(lambda nmx=nmx: ts(nmx[0:112, :], nmx[0:112, :], -8 ** -0.5, None, ALU.mult), t)
                for i in range(2):
                    t1 = A.do(lambda PR=PR, nmx=nmx, i=i: act(ch(PR, i), PS[i][0:112, :], ACT.Exp, bias=nmx[0:112, :], scale=8 ** -0.5,
                                              acc=SM[0:112, 204 + i:205 + i]), t)
                t = V.do(lambda rsum=rsum: tt(rsum[0:112, :], SM[0:112, 204:205], SM[0:112, 205:206], ALU.add), t1)
                t_r = V.do(lambda rsum=rsum: nc.vector.reciprocal(rsum[0:112, :], rsum[0:112, :]), t)

                def f(PR=PR):
                    for c in range(8):
                        r = nc.tensor.transpose(PS[2 + c // 4][:, (c % 4) * 112:(c % 4 + 1) * 112], tile(PR, c), w("ident")[0:112, 0:112])
                    return r
                t = PE.do(f, t1)
                t = A.do(lambda PTt=PTt: nc.scalar.copy(PTt[:, 0:448], PS[2][:, 0:448]), t)
                t = V.do(lambda PTt=PTt: nc.vector.tensor_copy(PTt[:, 448:896], PS[3][:, 0:448]), t)

                def f(PTt=PTt, VK=VK):
                    for c in range(8):
                        r = mm(PS[6][0:112, 0:128], PTt[:, c * 112:(c + 1) * 112], tile(VK, c), c == 0, c == 7)
                    return r
                t = PE.do(f, t, t_vm)
                ob = Ob[:, j * 128:(j + 1) * 128]
                t = V.do(lambda rsum=rsum, vmr=vmr, ob=ob: stt(ob, PS[6][0:112, 0:128], rsum[0:112, :], vmr, ALU.mult, ALU.subtract), t, t_r)
                t = V.do(lambda hmT=hmT, ob=ob: tt(ob, ob, hmT, ALU.mult), t)
            t_ob = t

            def f(posT=posT, b=b):
                for i in range(2):
                    r = mm(PS[i][0:112, :], w("E64")[:, b * 112:(b + 1) * 112], ch(posT, i))
                return r
            t = PE.do(f)
            for i in range(2):
                t_pb = A.do(lambda posB=posB, i=i: nc.scalar.copy(ch(posB, i), PS[i][0:112, :]), t)
            for i in range(2):
                for j in range(5):
                    ko, oh, fo = Roo.take()
                    t = V.do(lambda posB=posB, oh=oh, i=i, j=j: ts(oh, ch(posB, i), w("ucol")[:, j:j + 1], None, ALU.is_equal), t_pb, fo)
                    t = PE.do(lambda Ob=Ob, oh=oh, j=j, i=i: mm(PS[4 + i], Ob[:, j * 128:(j + 1) * 128], oh, j == 0, j == 4), t, t_ob)
                    Roo.free[ko] = [t]
                t = A.do(lambda outT=outT, vmc=vmc, i=i: act(outT, PS[4 + i], ACT.Identity, bias=vmc), t, now())
                t = PE.do(lambda outT=outT, i=i: mm(PS[6 + i], w("aWo"), outT), t)
                t = V.do(lambda i=i, b=b: stt(ch(XT, 2 * b + i), PS[6 + i], w("abo"), ch(XT, 2 * b + i), ALU.add, ALU.add), t)
        barrier()

    def stage4():
        ar = Arena()
        b2 = SM[:, 92:93]
        G = Ggate = ar(128)
        Rx, Rh = Ring([(ar(512), ar(512)) for _ in range(2)]), Ring([ar(512) for _ in range(4)])
        Rp, Ro, Rd = Ring(PS[0:4]), Ring(PS[4:6]), Ring(PS[6:8])
        W2 = wtok(2)
        tg = V.do(lambda Ggate=Ggate: tt(Ggate, w("gate1"), w("gate0"), ALU.subtract), W2)
        t = V.do(lambda b2=b2: tt(b2, w("fb2")[:, 0:1], w("fb2")[:, 1:2], ALU.add))
        tb = V.do(lambda b2=b2: tt(b2, b2, w("sb2"), ALU.add), t)
        fw1, fw2, sw1, sw2 = w("fw1"), w("fw2"), w("sw1"), w("sw2")
        for i in range(NCH):
            kd, d, fd = Rd.take()
            kx, (x0, x1), fx = Rx.take()
            x = ch(XT, i)
            t = PE.do(lambda Ggate=Ggate, d=d, x=x: mm(d, Ggate, x), tg, fd)
            t = V.do(lambda d=d, x=x, x1=x1: stt(x1, d, 0.0, x, ALU.is_gt, ALU.mult), t, fx)
            Rd.free[kd] = [t]
            tx = V.do(lambda x0=x0, x1=x1, x=x: tt(x0, x, x1, ALU.subtract), t)
            ko, o, fo = Ro.take()
            pend = []

            def down(h, kh, th, n, o=o, fo=fo):
                t = PE.do(lambda h=h, n=n, o=o: mm(o, fw2[:, n * 128:(n + 1) * 128] if n < 8 else sw2[:, (n - 8) * 128:(n - 7) * 128], h,
                                     n == 8, n == 7), th, fo)
                Rh.free[kh] = [t]
                return t
            for n in (8, 9, 10, 11, 0, 1, 2, 3, 4, 5, 6, 7):
                src = x if n >= 8 else (x0 if n < 4 else x1)
                wt = fw1[:, n * 128:(n + 1) * 128] if n < 8 else sw1[:, (n - 8) * 128:(n - 7) * 128]
                bb = w("fb1")[:, n:n + 1] if n < 8 else w("sb1")[:, n - 8:n - 7]
                k, p, fr = Rp.take()
                t = PE.do(lambda p=p, wt=wt, src=src: mm(p, wt, src), fr, W2, tx if n < 8 else None)
                kh, h, fh = Rh.take()
                if n % 2:
                    t = A.do(lambda h=h, p=p, bb=bb: act(h, p, ACT.Relu, bias=bb), t, fh)
                else:
                    t = V.do(lambda h=h, p=p, bb=bb: ts(h, p, bb, 0.0, ALU.add, ALU.max), t, fh)
                Rp.free[k] = [t]
                pend.append((h, kh, t, n))
                if len(pend) > 2:
                    down(*pend.pop(0))
            for q in pend:
                to = down(*q)
            Rx.free[kx] = [to]
            t = V.do(lambda b2=b2, o=o, x=x: stt(x, o, b2, x, ALU.add, ALU.add), to, tb)
            Ro.free[ko] = [t]
        barrier()

    def stage5():
        ar = Arena()
        W3 = wtok(3)
        CS, bvr = ar(1024), ar(1024)
        S.dma(lambda CS=CS: nc.sync.dma_start(CS, cs_d), s_cs2, now())
        S.dma(lambda bvr=bvr: nc.sync.dma_start(bvr, bkv_d[1:2, :].partition_broadcast(128)), s_kv)
        CSt, KVt = (s_cs2, 16), (s_kv, 16)
        sets = [tuple(ar(n) for n in (2048, 2048, 1024, 2048, 1040)) for _ in range(2)]
        AM = Ring([ar(512) for _ in range(2)])
        Sb = Ring([ar(260) for _ in range(2)])
        Ok, OT = ar(1024), ar(1024)
        WqD = ar(512)
        den = [SM[:, 208:212], SM[:, 332:336]]
        co = w("coss")
        v5 = lambda V_: V_.rearrange("p (c h d) -> p c h d", c=4, h=4)
        t_one = None
        for q in sets:
            t_one = V.do(lambda q=q, v5=v5: nc.vector.memset(v5(q[4])[:, :, :, 64:65], 1.0))
        k5 = lambda K_: K_.rearrange("p (c h s d) -> p c h s d", c=4, h=4, s=2)
        Rp, Ro = Ring([PS[0], PS[1]]), Ring([PS[5], PS[6]])
        Ra = Ring([PSALL[:, 1024:2048].rearrange("p (e q j t) -> p q e j t", e=2, q=2, j=2)[:, q] for q in range(2)])
        Sp, Rf = PS[4], Ring([PS[7]])
        cWq, cWk, cWv, cWo = w("cWq"), w("cWk"), w("cWv"), w("cWo")
        dm = w("dmask").unsqueeze(1).unsqueeze(1).to_broadcast([128, 2, 2, 128])
        a4 = lambda am: am.rearrange("p (e j t) -> p e j t", e=2, j=2)
        its = [(b, g, i) for b in range(NB) for g in range(4) for i in range(2)]
        tok, fin = {}, {"ok": None, "ot": None, "rq": None}

        def project(m):
            b, g, i = its[m]
            Qr, Qe, KT, Ke, Vv = sets[m % 2]
            old = tok[m - 2]["done"] if m >= 2 else None
            d = tok[m] = {}
            x = ch(XT, 2 * b + i)
            for h in range(2):
                k, p, fr = Rp.take()
                o = (4 * g + 2 * h) * 64
                t = PE.do(lambda o=o, p=p, x=x: mm(p, cWk[:, o:o + 128], x), fr, W3)
                d["kt"] = t = A.do(lambda KT=KT, g=g, h=h, p=p: act(KT[:, h * 512:(h + 1) * 512], p, ACT.Relu,
                                               bias=w("cbk")[:, 2 * g + h:2 * g + h + 1]), t, old)
                Rp.free[k] = [t]
                yield
            if i == 0:
                wq4 = cWq[:, g * 256:(g + 1) * 256].rearrange("p (h d) -> p h d", h=4).unsqueeze(2).to_broadcast([128, 4, 2, 64])
                fin["wq"] = V.do(lambda wq4=wq4: nc.vector.tensor_copy(WqD.rearrange("p (h s d) -> p h s d", h=4, s=2), wq4),
                                 fin["rq"], W3)
            for h in range(4):
                k, p, fr = Rp.take()
                t = PE.do(lambda h=h, p=p, x=x: mm(p, WqD[:, h * 128:(h + 1) * 128], x), fr, fin["wq"])
                fin["rq"] = t
                q = Qr[:, h * 512:(h + 1) * 512]
                d["qr"] = t = A.do(lambda g=g, h=h, p=p, q=q: act(q, p, ACT.Relu, bias=w("cbq2")[:, 4 * g + h:4 * g + h + 1]), t)
                Rp.free[k] = [t]
                d["qe"] = G.do(lambda Qe=Qe, h=h, i=i, q=q: nc.gpsimd.tensor_tensor(Qe[:, h * 512:(h + 1) * 512], q, ch(CS, i), ALU.mult), t, CSt, old)
                yield
            for c in range(4):
                k, p, fr = Rp.take()
                xt = tile(XT, b * 8 + 4 * i + c)
                o, n = g * 256, 4 * i + c

                def f(KT=KT, c=c, o=o, p=p, xt=xt):
                    for h in range(2):
                        nc.tensor.transpose(p[:, h * 128:(h + 1) * 128], KT[:, h * 512 + c * 128:h * 512 + (c + 1) * 128], w("ident"))
                    return mm(p[:, 256:512], xt, cWv[:, o:o + 256])
                t = PE.do(f, fr, d["kt"])
                d["v"] = t1 = V.do(lambda Vv=Vv, c=c, o=o, p=p: tt(v5(Vv)[:, c, :, 0:64], g3(p[:, 256:512], 4), g3(bvr[:, o:o + 256], 4), ALU.add),
                                   t, t_one, KVt, old)
                kk = g3(p[:, 0:256], 4)
                A.do(lambda Ke=Ke, c=c, kk=kk, n=n: act(k5(Ke)[:, c, :, 0, :], kk, ACT.Copy, scale=co[:, n:n + 1]), t1)
                d["ke"] = t = A.do(lambda Ke=Ke, c=c, kk=kk, n=n: act(k5(Ke)[:, c, :, 1, :], kk, ACT.Copy, scale=co[:, 8 + n:9 + n]))
                Rp.free[k] = [t]
                yield

        am_of, sb_of = {}, {}

        def scores(s):
            m, c = divmod(s, 4)
            Qr, Qe, KT, Ke, Vv = sets[m % 2]
            d = tok[m]
            k, pa, fr = Ra.take()

            def f(KT=KT, Qr=Qr, c=c, pa=pa):
                for h in range(4):
                    r0, o = 64 * (h % 2), (h // 2) * 512 + c * 128
                    r = mm(pa[:, h % 2, h // 2, :], KT[r0:r0 + 64, o:o + 128], Qr[r0:r0 + 64, h * 512 + c * 128:h * 512 + (c + 1) * 128])
                return r
            t = PE.do(f, fr, d["qr"], d["kt"])
            ka, am, fa = AM.take()
            t = V.do(lambda am=am, pa=pa: tt(a4(am), pa, dm, ALU.mult), t, fa)
            Ra.free = [[t], [t]]
            am_of[s] = (ka, am, t)

        def state(s):
            m, c = divmod(s, 4)
            n = 4 * its[m][2] + c
            if n == 7:
                return
            Ke, Vv = sets[m % 2][3:]
            d = tok[m]
            ks, sb, fs = Sb.take()
            prev = sb_of[s - 1][2] if s else None

            def f(Ke=Ke, Vv=Vv, c=c, n=n):
                for h in range(4):
                    r = mm(Sp[:, h * 65:(h + 1) * 65], k5(Ke)[:, c, h, :, :].rearrange("p s d -> p (s d)"),
                           v5(Vv)[:, c, h, :], n == 0 and h == 0, n == 6, skip_group_check=True)
                return r
            t = PE.do(f, d["ke"], d["v"], prev)
            t = A.do(lambda sb=sb: nc.scalar.copy(sb, Sp[:, 0:260]), t, fs)
            sb_of[s] = (ks, sb, t)
            if n == 6:
                sb_of[s + 1] = (ks, sb, t)

        def outputs(s):
            m, c = divmod(s, 4)
            b, g, i = its[m]
            n = 4 * i + c
            Qr, Qe, KT, Ke, Vv = sets[m % 2]
            d = tok[m]
            ka, am, t_am = am_of[s]
            ko, po, fo = Ro.take()
            ks, sb, t_sb = sb_of[s - 1] if n else (None, None, None)

            def f(Qe=Qe, Vv=Vv, am=am, c=c, n=n, po=po, sb=sb):
                for h in range(4):
                    r = mm(po[:, h * 65:(h + 1) * 65], a4(am)[:, h % 2, h // 2, :], v5(Vv)[:, c, h, :], True, n == 0)
                    if n > 0:
                        r = mm(po[:, h * 65:(h + 1) * 65], Qe[:, h * 512 + c * 128:h * 512 + (c + 1) * 128],
                               sb[:, h * 65:(h + 1) * 65], False, True)
                return r
            t = PE.do(f, t_am, d["v"], d["qe"], t_sb, fo)
            AM.free[ka] = [t]
            if n > 0:
                Sb.free[ks] = [t]
            d["done"] = t
            o4 = po[:, 0:260].rearrange("p (h d) -> p h d", h=4)
            dn = den[s % 2]
            t = V.do(lambda dn=dn, o4=o4: ts(dn, o4[:, :, 64], 1e-6, None, ALU.max), t)
            t = V.do(lambda dn=dn: nc.vector.reciprocal(dn, dn), t)
            t = V.do(lambda c=c, dn=dn, o4=o4: tt(g3(Ok[:, c * 256:(c + 1) * 256], 4), o4[:, :, 0:64], bin_(dn, 4, 64), ALU.mult), t, fin["ok"])
            Ro.free[ko] = [t]
            d["ok"] = t

        def finish(m):
            b, g, i = its[m]
            x = ch(XT, 2 * b + i)
            for h in range(2):
                k, p, fr = Rf.take()

                def f(h=h, p=p):
                    for c in range(4):
                        r = nc.tensor.transpose(p[:, c * 128:(c + 1) * 128], Ok[:, c * 256 + h * 128:c * 256 + (h + 1) * 128], w("ident"))
                    return r
                fin["ok"] = t = PE.do(f, tok[m]["ok"], fr)
                t = A.do(lambda h=h, p=p: nc.scalar.copy(ch(OT, h), p), t, fin["ot"])
                Rf.free[k] = [t]
                yield
            k, p, fr = Rf.take()

            def f(g=g, p=p):
                for h in range(2):
                    r = mm(p, cWo[:, (2 * g + h) * 128:(2 * g + h + 1) * 128], ch(OT, h), h == 0, h == 1)
                return r
            fin["ot"] = t = PE.do(f, fr, t)
            y = ch(XK, 2 * b + i)
            if g == 0:
                t = V.do(lambda p=p, x=x, y=y: stt(y, p, w("cbo"), x, ALU.add, ALU.add), t)
            else:
                t = V.do(lambda p=p, y=y: tt(y, p, y, ALU.add), t, tok[m]["y"])
            Rf.free[k] = [t]
            tok[m]["y1"] = t

        for _ in project(0):
            pass
        scores(0)
        last_y = {}
        nf = None
        for m in range(len(its)):
            b, g, i = its[m]
            tok[m]["y"] = None
            nx = project(m + 1) if m + 1 < len(its) else None
            for c in range(4):
                s = 4 * m + c
                for _ in range(3 if c < 2 else 2):
                    if nx is not None:
                        next(nx, None)
                state(s)
                if nf is not None:
                    next(nf, None)
                    next(nf, None)
                if c == 3 and nx is not None:
                    for _ in nx:
                        pass
                if s + 1 < 4 * len(its):
                    scores(s + 1)
                outputs(s)
            if nf is not None:
                for _ in nf:
                    pass
            tok[m]["y"] = last_y.get((b, i))
            nf = finish(m)
            key = (b, i)
            last_y[key] = (V.sem, V.n)
        for _ in nf:
            pass
        barrier()

    def softmax8(ar, lg, V8, pr):
        m, s = SM[:, 96:128], SM[:, 128:160]
        l3, p3 = g3(lg, NT), g3(pr, NT)
        t = V.do(lambda l3=l3, m=m: nc.vector.tensor_reduce(m, l3, AX, ALU.max), now())
        t = V.do(lambda l3=l3, m=m: tt(l3, l3, bin_(m, NT, 8), ALU.subtract), t)
        t = A.do(lambda lg=lg: act(lg, lg, ACT.Exp), t)
        t = V.do(lambda l3=l3, s=s: nc.vector.tensor_reduce(s, l3, AX, ALU.add), t)
        t = V.do(lambda s=s: nc.vector.reciprocal(s, s), t)
        t = V.do(lambda l3=l3, p3=p3, s=s: tt(p3[:, :, 0:8], l3, bin_(s, NT, 8), ALU.mult), t)

        def f(V8=V8, pr=pr):
            for c in range(NT):
                r = nc.vector.max(V8[:, c * 8:c * 8 + 8], pr[:, c * 16:c * 16 + 8])
            return r
        return V.do(f, t)

    def router(rw, lg, bias, wt):
        p = PS[0][:, 0:256]

        def f(p=p, rw=rw):
            for c in range(NT):
                r = mm(p[:, c * 8:c * 8 + 8], tile(XT, c), rw)
            return r
        t = PE.do(f, wt)
        if bias is None:
            return V.do(lambda lg=lg, p=p: nc.vector.tensor_copy(lg, p), t)
        return V.do(lambda bias=bias, lg=lg, p=p: tt(g3(lg, NT), g3(p, NT), bias.unsqueeze(1).to_broadcast([128, NT, 8]), ALU.add), t)

    def to_rows(WK, WT, tw):
        Rt = Ring(PS[1:3])
        for i in range(NCH):
            k, p, fr = Rt.take()

            def f(WK=WK, i=i, p=p):
                for j in range(4):
                    c = 4 * i + j
                    r = nc.tensor.transpose(p[0:8, j * 128:(j + 1) * 128], WK[:, c * 8:c * 8 + 8], w("ident"))
                return r
            t = PE.do(f, fr, tw)
            t = A.do(lambda WT=WT, i=i, p=p: nc.scalar.copy(ch(WT, i), p[0:8, :]), t)
            Rt.free[k] = [t]
        return t

    def stage6():
        ar = Arena()
        lg, V8, pr, R = ar(256), ar(256), ar(NT * 16), ar(NT * 16)
        WK, WT = ar(256), ar(T, 8)
        rp = ar(NT * 8)
        s2 = SM[:, 160:192]
        router(w("rwT"), lg, None, wtok(3))
        tp = V.do(lambda pr=pr: nc.vector.memset(pr, FILL))
        tv = softmax8(ar, lg, V8, pr)
        v3 = g3(V8, NT)
        t = V.do(lambda s2=s2, v3=v3: stt(s2, v3[:, :, 0], 1e-6, v3[:, :, 1], ALU.add, ALU.add), tv)
        t_s = V.do(lambda s2=s2: nc.vector.reciprocal(s2, s2), t)
        t = V.do(lambda rp=rp: nc.vector.memset(rp, FILL))
        t = V.do(lambda rp=rp, v3=v3: nc.vector.tensor_copy(g3(rp, NT)[:, :, 0:2], v3[:, :, 0:2]), t)

        def f(R=R, pr=pr, rp=rp):
            for c in range(NT):
                r = nc.vector.match_replace(R[:, c * 16:c * 16 + 16], rp[:, c * 8:c * 8 + 8], pr[:, c * 16:c * 16 + 16], FILL)
            return r
        t = V.do(f, t)
        r3, q3, w3 = g3(R, NT)[:, :, 0:8], g3(pr, NT)[:, :, 0:8], g3(WK, NT)
        t = V.do(lambda q3=q3, r3=r3, w3=w3: tt(w3, r3, q3, ALU.not_equal), t)
        t = V.do(lambda q3=q3, w3=w3: tt(w3, w3, q3, ALU.mult), t)
        t = V.do(lambda s2=s2, w3=w3: tt(w3, w3, bin_(s2, NT, 8), ALU.mult), t, t_s)
        t_w = to_rows(WK, WT, t)
        Rx, Rg, Rh = Ring([ar(512) for _ in range(2)]), Ring([ar(512) for _ in range(2)]), Ring([ar(512) for _ in range(3)])
        Rb, Rp, Ro = Ring(PS[0:2], [t_w]), Ring([(PS[2], PS[3]), (PS[4], PS[5])], [t_w]), Ring(PS[6:8])
        w13, w2e = w("w13"), w("w2e")
        W4 = wtok(4)
        for i in range(NCH):
            x = ch(XT, i)
            ko, o, fo = Ro.take()
            pend = []

            def down(h, kh, th, n, o=o, fo=fo):
                t = PE.do(lambda h=h, n=n, o=o: mm(o, w2e[:, n * 128:(n + 1) * 128], h, n == 0, n == 15), th, fo)
                Rh.free[kh] = [t]
                return t
            for e in range(8):
                kb, pb, fb = Rb.take()
                kx, xw, fx = Rx.take()
                t = PE.do(lambda WT=WT, e=e, pb=pb, i=i: mm(pb, w("sel8")[:, e * 128:(e + 1) * 128], ch(WT, i)), fb, t_w)
                tx = V.do(lambda pb=pb, xw=xw, x=x: tt(xw, pb, x, ALU.mult), t, fx)
                Rb.free[kb] = [tx]
                for c in range(2):
                    k, (pg, pu), fr = Rp.take()
                    o1 = e * 512 + c * 128
                    t1 = PE.do(lambda w13=w13, pg=pg, x=x, o1=o1: mm(pg, w13[:, o1:o1 + 128], x), fr, W4)
                    kg, g, fg = Rg.take()
                    t1 = A.do(lambda pg=pg, g=g: act(g, pg, ACT.Silu), t1, fg)
                    t2 = PE.do(lambda w13=w13, pu=pu, xw=xw, o1=o1: mm(pu, w13[:, o1 + 256:o1 + 384], xw), tx)
                    kh, h, fh = Rh.take()
                    t = V.do(lambda h=h, pu=pu, g=g: tt(h, pu, g, ALU.mult), t1, t2, fh)
                    Rp.free[k] = Rg.free[kg] = [t]
                    pend.append((h, kh, t, 2 * e + c))
                    if len(pend) > 1:
                        down(*pend.pop(0))
                Rx.free[kx] = [t2]
            for q in pend:
                to = down(*q)
            t = V.do(lambda o=o, x=x: tt(x, o, x, ALU.add), to)
            Ro.free[ko] = [t]
        barrier()

    def stage7():
        W5 = wtok(5)
        ss, rs, sd = SM[:, 0:32], SM[:, 32:64], SM[:, 212:244]
        negA, car, carx = SM[:, 244:276], SM[:, 276:308], SM[:, 308:314]
        eps = SM[:, 479:480]
        ar = Arena()
        Rj = Ring([ar(512) for _ in range(2)])
        Rt = Ring(PS[0:2])
        t_A = A.do(lambda negA=negA: act(negA, w("Alog"), ACT.Exp), W5)
        t_A = V.do(lambda negA=negA: ts(negA, negA, -1.0, None, ALU.mult), t_A)
        for i in range(NCH):
            kj, jk, fj = Rj.take()

            def f(ss=ss, i=i, jk=jk):
                for j in range(4):
                    c = 4 * i + j
                    r = act(jk[:, j * 128:(j + 1) * 128], tile(XK, c), ACT.Square, scale=128 ** -0.5, acc=ss[:, c:c + 1])
                return r
            t = A.do(f, fj)
            Rj.free[kj] = [t]
        t = A.do(lambda eps=eps, sd=sd, ss=ss: act(sd, ss, ACT.Sqrt, bias=eps), t, t_eps)
        t_rs = V.do(lambda rs=rs, sd=sd: nc.vector.reciprocal(rs, sd), t)
        for i in range(NCH):
            t = V.do(lambda rs=rs, i=i: tt(g3(ch(XK, i), 4), g3(ch(XK, i), 4), bin_(rs[:, 4 * i:4 * i + 4], 4, 128), ALU.mult), t_rs)
            k, p, fr = Rt.take()

            def f(i=i, p=p):
                for j in range(4):
                    r = nc.tensor.transpose(p[:, j * 128:(j + 1) * 128], tile(XK, 4 * i + j), w("ident"))
                return r
            t = PE.do(f, t, fr)
            t_xn = A.do(lambda i=i, p=p: act(ch(XK, i), p, ACT.Copy, scale=w("normw")), t)
            Rt.free[k] = [t_xn]
        barrier()
        ar = Arena()
        sets = [tuple(ar(1024) for _ in range(4)) for _ in range(2)]
        ev = ar(1024)
        xe = [ar(515), ar(515)]
        d1 = ar(512, 64)
        Rb, Ru, Ra, Rh, Rc = Ring([ar(512) for _ in range(3)]), Ring([ar(512) for _ in range(4)]), Ring([ar(512) for _ in range(4)]), \
            Ring([ar(512) for _ in range(4)]), Ring([ar(512) for _ in range(4)])
        Bp, Cp = Ring(PS[0:2]), Ring(PS[2:4])
        Yp = PS[4:6]
        Rp = Ring(PS[6:8])
        skT, inT, cw, cb = w("skT"), w("inT"), SM[:, 320:328], SM[:, 328:330]
        V.do(lambda cw=cw: ts(cw, w("convw"), 0.5, None, ALU.mult))
        t_ev = [V.do(lambda cb=cb: ts(cb, w("convb"), 0.5, None, ALU.mult))]
        BCs = [RT[0:64, 0:512], RT[0:64, 512:1024]]
        s2 = RT[0:64, 1024:1056]
        t_s2 = V.do(lambda s2=s2: nc.vector.tensor_copy(s2, w("ss2")))
        tok = {}

        def prepare(i):
            first = i % 2 == 0
            sk, xs, dl, dx = sets[i % 2]
            BC = BCs[i % 2]
            old = tok[i - 2]["done"] if i >= 2 else None
            xn = ch(XK, i)
            d = tok[i] = {}
            for e in range(2):
                k, p, fr = Rp.take()
                t = PE.do(lambda e=e, p=p, xn=xn: mm(p, tile(skT, e), xn), fr)
                t = A.do(lambda e=e, p=p, sk=sk: act(ch(sk, e), p, ACT.Tanh, scale=0.5), t, old)
                t_sk = V.do(lambda e=e, p=p, sk=sk: stt(ch(sk, e), ch(sk, e), 1.0, p, ALU.add, ALU.mult), t)
                Rp.free[k] = [t_sk]
                k, p2, fr = Rp.take()
                t = PE.do(lambda e=e, p2=p2, xn=xn: mm(p2, tile(inT, e), xn), fr)
                pc = tok[i - 1]["conv"] if i else None
                if first:
                    t2 = V.do(lambda e=e: nc.vector.memset(xe[e][:, 0:3], 0.0), pc)
                else:
                    t2 = V.do(lambda e=e: nc.vector.tensor_copy(xe[e][:, 0:3], carx[:, 3 * e:3 * e + 3]), pc)
                t = A.do(lambda e=e, p2=p2: nc.scalar.copy(xe[e][:, 3:515], p2), t, pc)
                Rp.free[k] = [t]
                yield
                t3 = V.do(lambda e=e: nc.vector.tensor_copy(carx[:, 3 * e:3 * e + 3], xe[e][:, 512:515]), t, t2)
                v = ch(ev, e)
                t = A.do(lambda e=e, v=v: act(v, xe[e][:, 0:512], ACT.Identity, scale=cw[:, 4 * e:4 * e + 1], bias=cb[:, e:e + 1]), t, t2, t_ev[0])
                for j in range(1, 4):
                    t = V.do(lambda e=e, j=j, v=v: stt(v, xe[e][:, j:j + 512], cw[:, 4 * e + j:4 * e + j + 1], v, ALU.mult, ALU.add), t)
                    if j == 2:
                        yield
                t_cv = [t, t3]
                t = A.do(lambda e=e, v=v, xs=xs: act(ch(xs, e), v, ACT.Tanh), t, old)
                t_xs = V.do(lambda e=e, v=v, xs=xs: stt(ch(xs, e), ch(xs, e), 1.0, v, ALU.add, ALU.mult), t)
                yield
            d["conv"] = t_cv
            k, p, fr = Rp.take()

            def f(p=p, xs=xs):
                for e in range(2):
                    r = mm(p[0:64, :], w("wd1T")[:, e * 64:(e + 1) * 64], ch(xs, e), e == 0, e == 1)
                return r
            t = PE.do(f, t_xs, fr)
            t_d1 = V.do(lambda p=p: nc.vector.tensor_copy(d1, p[0:64, :]), t, tok[i - 1]["d1"] if i else None)
            Rp.free[k] = [t_d1]
            yield
            k, p2, fr = Rp.take()

            def f(p2=p2, xs=xs):
                for e in range(2):
                    r = mm(p2[0:32, :], w("wbcT")[:, e * 32:(e + 1) * 32], ch(xs, e), e == 0, e == 1)
                return r
            t = PE.do(f, fr)
            t = V.do(lambda BC=BC, p2=p2: nc.vector.tensor_copy(BC[0:32, :], p2[0:32, :]), t, old)
            t_bc = V.do(lambda BC=BC, p2=p2: tt(BC[32:64, :], p2[0:32, :], BC[0:32, :].bitcast(F32), ALU.subtract), t)
            Rp.free[k] = [t_bc]
            d["bc"] = t_bc
            yield
            t12 = []
            for e in range(2):
                k, p, fr = Rp.take()
                t = d["d1"] = PE.do(lambda e=e, p=p: mm(p, w("wd2T")[:, e * 128:(e + 1) * 128], d1), t_d1, fr)
                t2 = V.do(lambda dl=dl, e=e, p=p: ts(ch(dl, e), p, w("wd2b")[:, e:e + 1], 0.0, ALU.add, ALU.max), t, old)
                t1 = A.do(lambda e=e, p=p: act(ch(ev, e), p, ACT.Abs, bias=w("wd2b")[:, e:e + 1]), t2)
                Rp.free[k] = [t1]
                yield
            t = A.do(lambda: act(ev, ev, ACT.Exp, scale=-1.0), t1)
            t = A.do(lambda: act(ev, ev, ACT.Ln, bias=1.0), t)
            yield
            t = V.do(lambda dl=dl: tt(dl, dl, ev, ALU.add), t, t2)
            t_ev[0] = t
            yield
            d["dl"] = t
            d["dx"] = V.do(lambda dl=dl, dx=dx, xs=xs: tt(dx, dl, xs, ALU.mult), t)

        st = {}

        def head(g):
            i, n = divmod(g, 16)
            sk, xs, dl, dx = sets[i % 2]
            BC = BCs[i % 2]
            d, s = tok[i], {}
            kb, pb, fb = Bp.take()
            kc, pc, fc = Cp.take()
            t = PE.do(lambda BC=BC, n=n, pb=pb: mm(pb, s2[:, n:n + 1].to_broadcast([64, 128]), BC), d["bc"], fb, t_s2)
            s["c"] = PE.do(lambda BC=BC, n=n, pc=pc: mm(pc, s2[:, 16 + n:17 + n].to_broadcast([64, 128]), BC), fc)
            kB, Bs, fB = Rb.take()
            t_b = A.do(lambda Bs=Bs, pb=pb: nc.scalar.copy(Bs, pb), t, fB)
            Bp.free[kb] = [t_b]
            s["pc"], s["kc"] = pc, kc
            for e in range(2):
                q = e * 16 + n
                ka, a, fa = Ra.take()
                t_a = A.do(lambda a=a, dl=dl, e=e, q=q: act(a, ch(dl, e), ACT.Exp, scale=negA[:, q:q + 1]), d["dl"], fa, t_A)
                ku, u, fu = Ru.take()
                t_u = G.do(lambda Bs=Bs, dx=dx, e=e, u=u: nc.gpsimd.tensor_tensor(u, ch(dx, e), Bs, ALU.mult), t_b, d["dx"], fu)
                s[e] = (ka, a, t_a, ku, u, t_u)
            Rb.free[kB] = [t_u]
            st[g] = s

        def body(g):
            i, n = divmod(g, 16)
            s = st[g]
            for e in range(2):
                q = e * 16 + n
                ka, a, t_a, ku, u, t_u = s[e]
                kh, h, fh = Rh.take()
                ini = 0.0 if i % 2 == 0 else car[:, q:q + 1]
                t_h = V.do(lambda a=a, h=h, ini=ini, u=u: nc.vector.tensor_tensor_scan(h, a, u, ini, ALU.mult, ALU.add), t_a, t_u, fh,
                           st[g - 16]["cr"] if i % 2 else None)
                Ra.free[ka] = Ru.free[ku] = [t_h]
                s[e] = (kh, h, t_h)
            for e in range(2):
                kh, h, t_h = s[e]
                kC, hc, fC = Rc.take()
                t_hc = V.do(lambda h=h, hc=hc, s=s: tt(hc, s["pc"], h, ALU.mult), t_h, s["c"], fC)
                q = e * 16 + n
                if i % 2 == 0:
                    s["cr"] = t_cr = G.do(lambda h=h, q=q: nc.gpsimd.tensor_copy(car[:, q:q + 1], h[:, 511:512]), t_h, t_A)
                    Rh.free[kh] = [t_hc, t_cr]
                else:
                    Rh.free[kh] = [t_hc]
                s[e] = (kC, hc, t_hc)
            Cp.free[s["kc"]] = [t_hc]

        t_z = [None]

        def tail(g):
            i, n = divmod(g, 16)
            s = st[g]
            for e in range(2):
                kC, hc, t_hc = s[e]
                t_y = PE.do(lambda e=e, hc=hc, n=n: mm(Yp[e], w("ident"), hc, n == 0, n == 15), t_hc, t_z[0] if n == 0 else None)
                Rc.free[kC] = [t_y]
            if n == 15:
                sk, xs, dl, dx = sets[i % 2]
                for e in range(2):
                    z = ch(dl, e)
                    t = t_z[0] = V.do(lambda e=e, xs=xs, z=z: stt(z, ch(xs, e), w("WD")[:, e:e + 1], Yp[e], ALU.mult, ALU.add), t_y, s["a"])
                    t = V.do(lambda e=e, sk=sk, z=z: stt(z, z, 0.5, ch(sk, e), ALU.mult, ALU.mult), t)
                k, p, fr = Rp.take()

                def f(dl=dl, p=p):
                    for e in range(2):
                        r = mm(p, w("outT")[:, e * 128:(e + 1) * 128], ch(dl, e), e == 0, e == 1)
                    return r
                t = PE.do(f, t, fr)
                t = V.do(lambda i=i, p=p: stt(ch(XT, i), ch(XT, i), 2.0, p, ALU.mult, ALU.add), t)
                Rp.free[k] = [t]
                tok[i]["done"] = t

        for _ in prepare(0):
            pass
        GN = NCH * 16
        nxt = None
        for g in range(-1, GN + 1):
            if 0 <= g + 1 < GN:
                head(g + 1)
                st[g + 1]["a"] = (A.sem, A.n)
            if 0 <= g < GN:
                body(g)
            if 0 <= g - 1 < GN:
                tail(g - 1)
            if g >= 0 and g % 16 == 1 and g // 16 + 1 < NCH:
                nxt = prepare(g // 16 + 1)
            if nxt is not None and g % 16 != 0:
                next(nxt, None)
        barrier()

    def stage8():
        ar = Arena()
        lg, V8, pr, R = ar(256), ar(256), ar(NT * 16), ar(NT * 16)
        WK, WT, rp, cum = ar(256), ar(T, 8), ar(256), ar(256)
        router(w("Wr"), lg, w("brr"), wtok(6))
        V.do(lambda pr=pr: nc.vector.memset(pr, FILL))
        tv = softmax8(ar, lg, V8, pr)
        v3, c3 = g3(V8, NT), g3(cum, NT)
        t = V.do(lambda c3=c3, v3=v3: nc.vector.tensor_copy(c3[:, :, 0], v3[:, :, 0]), tv)
        for j in range(1, 8):
            t = V.do(lambda c3=c3, v3=v3, j=j: tt(c3[:, :, j], c3[:, :, j - 1], v3[:, :, j], ALU.add), t)
        t = V.do(lambda cum=cum: ts(cum, cum, 0.8, None, ALU.is_lt), t)
        t = V.do(lambda c3=c3: nc.vector.memset(c3[:, :, 0:1], 1.0), t)
        t = V.do(lambda V8=V8, cum=cum, rp=rp: tt(rp, V8, cum, ALU.mult), t)
        t = V.do(lambda cum=cum: ts(cum, cum, -FILL, FILL, ALU.mult, ALU.add), t)
        t = V.do(lambda cum=cum, rp=rp: tt(rp, rp, cum, ALU.add), t)

        def f(R=R, pr=pr, rp=rp):
            for c in range(NT):
                r = nc.vector.match_replace(R[:, c * 16:c * 16 + 16], rp[:, c * 8:c * 8 + 8], pr[:, c * 16:c * 16 + 16], FILL)
            return r
        t = V.do(f, t)
        r3, q3, w3 = g3(R, NT)[:, :, 0:8], g3(pr, NT)[:, :, 0:8], g3(WK, NT)
        t = V.do(lambda q3=q3, r3=r3, w3=w3: tt(w3, r3, q3, ALU.not_equal), t)
        t = V.do(lambda q3=q3, w3=w3: tt(w3, w3, q3, ALU.mult), t)
        t_w = to_rows(WK, WT, t)
        Rh = Ring([ar(512) for _ in range(4)])
        Rw, Rv = Ring([ar(512) for _ in range(2)]), Ring([ar(512) for _ in range(2)])
        Rb, Rp, Ro = Ring(PS[0:2], [t_w]), Ring(PS[2:6], [t_w]), Ring(PS[6:8])
        W1, W2, B1, B2 = w("W1"), w("W2"), w("B1"), w("B2")
        W6 = wtok(6)
        t_acc = None
        for i in range(NCH):
            x = ch(XT, i)
            xr = ch(XK, i)
            tc = G.do(lambda x=x, xr=xr: nc.gpsimd.tensor_copy(xr, x))
            for e in range(8):
                kb, pb, fb = Rb.take()
                kw, wb, fw = Rw.take()
                t = PE.do(lambda WT=WT, e=e, pb=pb, i=i: mm(pb, w("sel8")[:, e * 128:(e + 1) * 128], ch(WT, i)), fb, t_w)
                t_wb = A.do(lambda wb=wb, pb=pb: nc.scalar.copy(wb, pb), t, fw)
                Rb.free[kb] = [t_wb]
                ko, o, fo = Ro.take()
                pend = []

                def down(h, kh, th, n, o=o, fo=fo):
                    t = PE.do(lambda h=h, n=n, o=o: mm(o, W2[:, n * 128:(n + 1) * 128], h, n % 4 == 0, n % 4 == 3), th, fo)
                    Rh.free[kh] = [t]
                    return t
                for c in range(4):
                    n = 4 * e + c
                    k, p, fr = Rp.take()
                    t = PE.do(lambda W1=W1, p=p, n=n, xr=xr: mm(p, W1[:, n * 128:(n + 1) * 128], xr), fr, W6, tc)
                    kh, h, fh = Rh.take()
                    if c % 2:
                        t = A.do(lambda B1=B1, h=h, p=p, n=n: act(h, p, ACT.Relu, bias=B1[:, n:n + 1]), t, fh)
                    else:
                        t = V.do(lambda B1=B1, h=h, p=p, n=n: ts(h, p, B1[:, n:n + 1], 0.0, ALU.add, ALU.max), t, fh)
                    Rp.free[k] = [t]
                    pend.append((h, kh, t, n))
                    if len(pend) > 2:
                        down(*pend.pop(0))
                for q in pend:
                    to = down(*q)
                kv, v, fv = Rv.take()
                t = V.do(lambda B2=B2, v=v, o=o, e=e, wb=wb: stt(v, o, B2[:, e:e + 1], wb, ALU.add, ALU.mult), to, t_wb, fv)
                Ro.free[ko] = Rw.free[kw] = [t]
                t_acc = G.do(lambda x=x, v=v: nc.gpsimd.tensor_tensor(x, x, v, ALU.add), t, tc, t_acc)
                Rv.free[kv] = [t_acc]
        barrier()


    stages = [stage1, stage2, stage3, stage4, stage5, stage6, stage7, stage8]
    late_at = (0, ())
    for k in range(START, STOP + 1):
        stages[k - 1]()
        if k == 5:
            late_at = (len(S.items), (now(),))
        layernorm(last=(k == STOP), src=XK if k == 5 else XT)

    src = 0
    for g, (a, b) in enumerate(spans):
        f = lambda a=a, b=b, c=src: nc.sync.dma_start(W[:, a:b], wp[:, c:c + b - a])
        src += b - a
        if g == LATE:
            S.items.insert(late_at[0] + g + 1, (f, late_at[1] + tuple((s_w[j], 16) for j in (1, 2, 3)), s_w[g], 16))
        else:
            S.items.insert(g + (1 if g > 0 else 0), (f, (), s_w[g], 16))
        if g == 0:
            S.items.insert(1, (lambda: nc.sync.dma_start(XT, xT_d), (), s_x, 16))
    pre = [(lambda: nc.scalar.dma_start(XK, xK_d), (), s_cs, 16)] if START > 1 else []
    A.items[:0] = pre
    if START > 1:
        for q in engines:
            k = 1 if q is A else 0
            q.items.insert(k, (None, [(s_cs, 16), (s_x, 16)] + [(s, 16) for j, s in enumerate(s_w) if j != LATE], None, 0))
    S.items.append((None, [(s_out, 16 * NCH)], None, 0))

    block = ctx.enter_context(nc.Block())

    @block.tensor
    def _(e):
        PE.emit(e)

    @block.vector
    def _(e):
        V.emit(e)

    @block.scalar
    def _(e):
        A.emit(e)

    @block.gpsimd
    def _(e):
        G.emit(e)

    @block.sync
    def _(e):
        S.emit(e)

    ctx.close()


def constants():
    p = np.arange(128)
    c = {}
    c["ss2"] = np.concatenate([np.eye(32), np.eye(32)], 0)
    c["ident"] = np.eye(128)
    c["cen"] = np.eye(128) - 1.0 / 128
    c["ones"] = np.ones((128, 128))
    c["one64"] = np.full((64, 1), 1.0 / 64)
    c["hm"] = (p[:, None] // 8 == np.arange(16)[None]) * 1.0
    r = np.arange(112)
    c["hmT"] = (r[:, None] % 16 == p[None] // 8) * 1.0
    e = np.zeros((64, 4, 112))
    for b in range(4):
        for j in range(112):
            e[b * 16 + j % 16, b, j] = 1
    c["E64"] = e.reshape(64, -1)
    c["ucol"] = r[:, None] // 16 + 7.0 * np.arange(5)[None] + 1
    c["tokid"] = p[:, None] + 128.0 * np.arange(8)[None]
    c["iotau"] = np.broadcast_to((np.arange(560) // 16 + 1.0)[None], (128, 560))
    s = np.zeros((8, 8, 128))
    for i in range(8):
        s[i, i] = 1
    c["sel8"] = s.reshape(8, -1)
    th = np.float32(np.pi / 2048) * np.arange(1024, dtype=np.float32)
    co, si = np.cos(th, dtype=np.float32), np.sin(th, dtype=np.float32)
    d = np.pi / 2048 * (p[None, :] - p[:, None])
    c["dmask"] = np.where(p[None, :] >= p[:, None], np.cos(d), 0.0)
    c["coss"] = np.concatenate([co.reshape(8, 128).T, si.reshape(8, 128).T], 1)
    c = {k: np.asarray(v, np.float32) for k, v in c.items()}
    cs = np.concatenate([np.broadcast_to(co, (64, 1024)), np.broadcast_to(si, (64, 1024))], 0).astype(np.float32)
    return c, np.ascontiguousarray(cs)


def kernel(**inputs):
    from concourse import bacc as _bacc
    from concourse.bass_utils import run_bass_kernel_spmd as _run
    I = {k: np.asarray(v) for k, v in inputs.items()}
    c, cs = constants()
    P = dict(c)
    col = lambda a: a.reshape(-1, 128).T
    rep = lambda a, n=128: np.broadcast_to(a.reshape(1, -1), (n, a.size))
    ck = lambda a: a.reshape(-1, 128, a.shape[-1]).transpose(1, 0, 2).reshape(128, -1)
    for l in range(2):
        P[f"Wz{l}"], P[f"Wh{l}"] = I[f"L0_attn_Wz{l}"].T, I[f"L0_attn_Wh{l}"].T
    P["b_l0a"] = np.stack([I["L0_attn_" + n] for n in ("bz0", "bh0", "bz1", "bh1")], 1)
    f = lambda n: I["L0_ffn_" + n]
    P["slot"], P["slotT"] = f("slot_init"), f("slot_init").T
    P["w1"] = ck(f("w1"))
    P["w2"], P["WihT"], P["WhhT"] = f("w2"), f("Wih").T, f("Whh").T
    for n in ("wq", "wk", "wv", "wvp", "wo"):
        P[n] = f(n)
    P["b1"], P["b2r"], P["tau"] = f("b1")[:, None], rep(f("b2")), rep(f("tau"))
    P["bih"], P["bhh"], P["bq"], P["bk"] = col(f("bih")), col(f("bhh")), f("bq")[:, None], f("bk")[:, None]
    P["bvr"], P["lng"], P["lnb"], P["bvp"], P["bo"] = rep(f("bv"), 64), col(f("ln_g")), col(f("ln_b")), col(f("bvp")), col(f("bo"))
    f = lambda n: I["L1_attn_" + n]
    for n in ("Wq", "Wk", "Wv", "Wo"):
        P["a" + n] = f(n)
    P["abq"], P["abk"], P["abvr"], P["abo"] = col(f("bq")), col(f("bk")), rep(f("bv")), col(f("bo"))
    f = lambda n: I["L1_ffn_" + n]
    P["gate0"], P["gate1"] = (np.broadcast_to(f("gate_w")[e][:, None], (128, 128)) for e in range(2))
    P["fw1"] = f("w1").transpose(1, 0, 2).reshape(128, -1)
    P["fb1"], P["fw2"] = col(f("b1")), ck(f("w2").reshape(1024, 128))
    P["fb2"], P["sw1"], P["sb1"], P["sw2"], P["sb2"] = col(f("b2")), f("sw1"), col(f("sb1")), ck(f("sw2")), col(f("sb2"))
    f = lambda n: I["L2_attn_" + n]
    P["cWq"], P["cWk"], P["cWv"], P["cWo"] = f("Wq"), f("Wk"), f("Wv"), ck(f("Wo"))
    bq = f("bq").reshape(16, 64).T
    P["cbq2"], P["cbk"], P["cbo"] = np.concatenate([bq, bq], 0), col(f("bk")), col(f("bo"))
    P["rwT"] = I["L2_ffn_router_w"].T
    P["w13"] = I["L2_ffn_w13"].transpose(1, 0, 2).reshape(128, -1)
    P["w2e"] = ck(I["L2_ffn_w2"].reshape(2048, 128))
    f = lambda n: I["L3_attn_" + n]
    P["normw"], P["skT"], P["inT"] = col(f("norm_w")), f("skip_w").T, f("in_w").T
    P["convw"], P["convb"] = ck(f("conv_w").reshape(256, 4)), col(f("conv_b"))
    P["wd1T"], P["wd2T"], P["wd2b"] = ck(f("wd1").T), f("wd2").T, col(f("wd2_b"))
    P["wbcT"] = ck(np.concatenate([f("wb"), f("wc")], 0).T)
    P["Alog"], P["WD"], P["outT"] = ck(f("A_log")), col(f("W_D")), ck(f("out_w").T)
    f = lambda n: I["L3_ffn_" + n]
    P["Wr"], P["brr"] = f("Wr"), rep(f("br"))
    P["W1"], P["B1"] = f("W1").transpose(1, 0, 2).reshape(128, -1), col(f("b1"))
    P["W2"], P["B2"] = ck(f("W2").reshape(4096, 128)), col(f("b2"))

    cols = []
    for g in GROUPS:
        for name, r, n in g:
            a = P[name]
            assert a.shape == (r, n) and a.dtype == np.float32, (name, a.shape, a.dtype)
            if r < 128:
                a = np.concatenate([a, np.zeros((128 - r, n), np.float32)], 0)
            cols.append(a)
    x = I["L0_attn_x"]
    arrays = {
        "wp": np.ascontiguousarray(np.concatenate(cols, 1)),
        "xT": np.ascontiguousarray(x.reshape(T, D).T),
        "sidx": np.ascontiguousarray(I["L1_attn_sample_idx"].reshape(1, 35)),
        "cs": cs,
        "bkv": np.ascontiguousarray(np.stack([I["L2_attn_bk"], I["L2_attn_bv"]], 0)),
    }
    if START > 1:
        arrays["xK"] = np.ascontiguousarray(x.reshape(NT, 128, D).transpose(1, 0, 2).reshape(128, T))
    nc = _bacc.Bacc("TRN2", target_bir_lowering=False, num_devices=1)
    h = {}
    for k, a in arrays.items():
        h[k] = nc.dram_tensor(k, a.shape, mybir.dt.from_np(a.dtype), kind="ExternalInput").ap()
    out = nc.dram_tensor("out", (NB, L, D), F32, kind="ExternalOutput").ap()
    build(nc, h["wp"], h["xT"], h.get("xK"), h["sidx"], h["cs"], h["bkv"], out)
    r = _run(nc, [arrays], core_ids=[0])
    return r.results[0]["out"]
```

```python
import numpy as np
import concourse.bass as bass
from concourse import mybir
from contextlib import ExitStack

F32 = mybir.dt.float32
BF16 = mybir.dt.bfloat16
I32 = mybir.dt.int32
ALU = mybir.AluOpType
ACT = mybir.ActivationFunctionType
AX = mybir.AxisListType.X
FILL = -3.0e38

NB, L, D = 4, 1024, 128
T = NB * L
NT = T // 128


class Queue:

    def __init__(self, name, sem):
        self.name, self.sem, self.n, self.items = name, sem, 0, []

    def do(self, fn, *deps):
        self.n += 1
        self.items.append((fn, deps, self.sem, 1))
        return (self.sem, self.n)

    def dma(self, fn, sem, *deps):
        self.items.append((fn, deps, sem, 16))

    def emit(self, eng):
        seen = {}

        def wait(d):
            if d is None:
                return
            if isinstance(d, list):
                for x in d:
                    wait(x)
                return
            sem, v = d
            if v > 0 and seen.get(id(sem), 0) < v:
                eng.wait_ge(sem, v)
                seen[id(sem)] = v

        for fn, deps, sem, k in self.items:
            for d in deps:
                wait(d)
            if fn is not None:
                fn().then_inc(sem, k)


class Ring:

    def __init__(self, bufs, first=None):
        self.bufs, self.i = bufs, -1
        self.free = [first or [] for _ in bufs]

    def take(self):
        self.i = (self.i + 1) % len(self.bufs)
        return self.i, self.bufs[self.i], self.free[self.i]


GROUPS = [
    [("ident", 128, 128), ("cen", 128, 128), ("Wz0", 128, 128), ("Wh0", 128, 128), ("Wz1", 128, 128), ("Wh1", 128, 128), ("b_l0a", 128, 4)],
    [("slotT", 128, 64), ("slot", 64, 128), ("w1", 128, 128), ("w2", 64, 64), ("WihT", 128, 384), ("WhhT", 128, 384),
     ("wq", 128, 32), ("wk", 128, 32), ("wv", 128, 128), ("wvp", 128, 128), ("wo", 128, 128),
     ("b1", 64, 1), ("b2r", 128, 64), ("tau", 128, 1), ("bih", 128, 3), ("bhh", 128, 3), ("bq", 32, 1), ("bk", 32, 1),
     ("bvr", 64, 128), ("lng", 128, 1), ("lnb", 128, 1), ("bvp", 128, 1), ("bo", 128, 1)],
    [("aWq", 128, 128), ("aWk", 128, 128), ("aWv", 128, 128), ("aWo", 128, 128), ("abq", 128, 1), ("abk", 128, 1),
     ("abvr", 128, 128), ("abo", 128, 1),
     ("gate0", 128, 128), ("gate1", 128, 128), ("fw1", 128, 1024), ("fb1", 128, 8), ("fw2", 128, 1024), ("fb2", 128, 2),
     ("sw1", 128, 512), ("sb1", 128, 4), ("sw2", 128, 512), ("sb2", 128, 1)],
    [("cWq", 128, 1024), ("cWk", 128, 1024), ("cWv", 128, 1024), ("cWo", 128, 1024),
     ("cbq2", 128, 16), ("cbk", 128, 8), ("cbo", 128, 1), ("dmask", 128, 128), ("coss", 128, 16),
     ("rwT", 128, 8)],
    [("w13", 128, 4096), ("w2e", 128, 2048)],
    [("normw", 128, 1), ("skT", 128, 256), ("inT", 128, 256), ("convw", 128, 8), ("convb", 128, 2), ("wd1T", 128, 128),
     ("wd2T", 64, 256), ("wd2b", 128, 2), ("wbcT", 128, 64), ("Alog", 128, 32), ("WD", 128, 2), ("outT", 128, 256)],
    [("Wr", 128, 8), ("brr", 128, 8), ("W1", 128, 4096), ("B1", 128, 32), ("W2", 128, 4096), ("B2", 128, 8)],
    [("ss2", 64, 32), ("sel16r", 40, 8), ("ones", 128, 128), ("one64", 64, 1), ("hm", 128, 16),
     ("hmT", 112, 128), ("E64", 64, 4 * 112), ("ucol", 112, 5), ("tokid", 128, 8), ("iotau", 128, 560)],
]
ORDER = (0, 7, 1, 2, 3, 4, 5)


LATE = 6


def place():
    off, at, spans = 0, {}, []
    for k, g in enumerate(GROUPS):
        if k == LATE:
            keep, off = off, spans[1][0]
        a = off
        for name, r, c in g:
            at[name] = (r, off, c)
            off += c
        spans.append((a, off))
        if k == LATE:
            assert off <= spans[3][1]
            off = keep
    return at, spans, off


def build(nc, wp, xT_d, sidx_d, cs_d, bkv_d, out_d):
    at, spans, WN = place()
    names = ["pe", "dve", "act", "pool", "sp"]
    ctx = ExitStack()
    sem = lambda n: ctx.enter_context(nc.semaphore(n))
    PE, V, A, G, S = (Queue(n, sem("q_" + n)) for n in names)
    engines = (PE, V, A, G)
    s_w = [sem(f"s_w{i}") for i in range(len(GROUPS))]
    s_si, s_kv, s_out, s_cs2 = (sem(n) for n in ("s_si", "s_kv", "s_out", "s_cs2"))
    s_x = [sem(f"s_x{b}") for b in range(NB)]

    FR = mybir.dt.float32r
    base = (nc.sbuf_base + 63) // 64 * 64
    SMN = 512
    TN = (nc.sbuf_usable_end - base) // 4 - WN - 2 * T - SMN - 64
    at_ = {}
    for name, n in (("W", WN), ("XT", T), ("XK", T), ("SM", SMN), ("TMP", TN)):
        at_[name] = nc.alloc_sbuf_tensor_at(name, [128, n], F32, offset=base)
        if name in ("W", "XK", "TMP"):
            at_[name + "r"] = nc.alloc_sbuf_tensor_at(name + "r", [128, n], FR, offset=base)
        base += (4 * n + 63) // 64 * 64
    W, XTt, XKt, SMt, TMP, TMPr, XKr, Wr = (at_[n] for n in ("W", "XT", "XK", "SM", "TMP", "TMPr", "XKr", "Wr"))
    XT, XK, SM = XTt[:, :], XKt[:, :], SMt[:, :]
    PSALL = nc.alloc_psum_tensor("ps", [128, 4096], F32)[:, :]
    PS = [PSALL[:, i * 512:(i + 1) * 512] for i in range(8)]

    def w(name):
        r, o, c = at[name]
        return W[0:r, o:o + c]

    wtok = lambda g: (s_w[g], 16)

    class Arena:
        def __init__(self, mem=TMP, memr=TMPr, size=TN):
            self.o, self.mem, self.memr, self.size = 0, mem, memr, size

        def __call__(self, cols, rows=128, dt=F32):
            assert self.o + cols <= self.size, ("arena", self.o + cols, self.size)
            v = (self.memr if dt == FR else self.mem)[0:rows, self.o:self.o + cols]
            self.o += cols
            return v.bitcast(dt) if dt == I32 else v

    def now():
        return [(q.sem, q.n) for q in engines]

    def barrier():
        t = now()
        for q in engines:
            q.items.append((None, t, None, 0))

    def mm(out, lhsT, rhs, start=True, stop=True, **k):
        return nc.tensor.matmul(out, lhsT, rhs, start=start, stop=stop, **k)

    def act(out, in_, f, bias=0.0, scale=1.0, acc=None):
        if acc is None:
            return nc.scalar.activation(out, in_, f, bias=bias, scale=scale)
        return nc.scalar.activation(out, in_, f, bias=bias, scale=scale, accum_out=acc)

    tt = lambda o, a, b, op: nc.vector.tensor_tensor(o, a, b, op)
    ts = lambda o, a, s1, s2, op0, op1=None: (nc.vector.tensor_scalar(o, a, s1, s2, op0, op1) if op1 is not None
                                             else nc.vector.tensor_scalar(o, a, s1, None, op0))
    stt = lambda o, a, s, b, op0, op1: nc.vector.scalar_tensor_tensor(out=o, in0=a, scalar=s, in1=b, op0=op0, op1=op1)

    def g3(ap, n):
        return ap.rearrange("p (n k) -> p n k", n=n)

    def split(src, h, l, *deps):
        t = V.do(lambda h=h, src=src: nc.vector.tensor_copy(h, src), *deps)
        return V.do(lambda h=h, l=l, src=src: tt(l, src, h.bitcast(F32), ALU.subtract), t)

    def mm3(out, a, b, start=True, stop=True):
        mm(out, a[0], b[0], start, False)
        mm(out, a[0], b[1], False, False)
        return mm(out, a[1], b[0], False, stop)

    def bin_(ap, n, k):
        return ap.unsqueeze(2).to_broadcast([ap.shape[0], n, k])

    def bout(ap, n):
        return ap.unsqueeze(1).to_broadcast([ap.shape[0], n, ap.shape[1]])

    CH = 512
    NCH = T // CH
    ch = lambda ap, i, k=CH: ap[:, i * k:(i + 1) * k]
    tile = lambda ap, i: ap[:, i * 128:(i + 1) * 128]

    t_eps = V.do(lambda: nc.vector.memset(SM[:, 479:480], 1e-5))

    XP = 4096 + 256
    ready = {}

    def layernorm(last=False, src=None, route=None, wt=None):
        src = XT if src is None else src
        ar = Arena()
        Rj = Ring([ar(512) for _ in range(2)])
        ss, rs, sd, eps = SM[:, 0:32], SM[:, 32:64], SM[:, 480:512], SM[:, 479:480]
        Rp, Rt = Ring([PS[0], PS[1], PS[2], PS[3]]), Ring([PS[4], PS[5], PS[6]])
        pend, routed = [], []
        if route is not None:
            ready.update(x=(TMPr[:, XP:XP + T], TMPr[:, XP + T:XP + 2 * T]), t_x={})

        def logits(i, t):
            def f(i=i):
                for c in range(4 * i, 4 * i + 4):
                    r = mm(PS[7][:, c * 8:c * 8 + 8], tile(XT, c), route)
                return r
            ready["lg"] = PE.do(f, t, wt)

        def back(i, t_xk):
            k, pt, fr = Rt.take()

            def f(i=i, pt=pt):
                for j in range(4):
                    r = nc.tensor.transpose(pt[:, j * 128:(j + 1) * 128], tile(XK, 4 * i + j), w("ident"))
                return r
            t = PE.do(f, fr, t_xk)
            if route is not None:
                t = A.do(lambda i=i, pt=pt: nc.scalar.copy(ch(XT, i), pt), t)
            else:
                t = V.do(lambda i=i, pt=pt: nc.vector.tensor_copy(ch(XT, i), pt), t)
            Rt.free[k] = [t]
            if route is not None:
                h, l = ready["x"]
                ready["t_x"][i] = split(ch(XT, i), ch(h, i), ch(l, i), t)
                routed.append((i, t))
                if len(routed) > 1:
                    logits(*routed.pop(0))

        centred = {}

        def centre(i):
            k, p, fr = Rp.take()

            def f(i=i, p=p):
                for j in range(4):
                    r = mm(p[:, j * 128:(j + 1) * 128], tile(src, 4 * i + j), w("cen"))
                return r
            centred[i] = (k, p, PE.do(f, fr))

        centre(0)
        centre(1)
        for i in range(NCH):
            if i + 2 < NCH:
                centre(i + 2)
            k, p, t0 = centred[i]
            kj, jk, fj = Rj.take()

            def f(ss=ss, i=i, p=p, jk=jk):
                for j in range(4):
                    c = 4 * i + j
                    r = act(jk[:, j * 128:(j + 1) * 128], p[:, j * 128:(j + 1) * 128], ACT.Square, scale=128 ** -0.5, acc=ss[:, c:c + 1])
                return r
            t1 = A.do(f, t0, fj)
            Rj.free[kj] = [t1]
            t2 = A.do(lambda eps=eps, sd=sd, ss=ss, i=i: act(sd[:, 4 * i:4 * i + 4], ss[:, 4 * i:4 * i + 4], ACT.Sqrt, bias=eps), t1, t_eps)
            t2 = V.do(lambda rs=rs, sd=sd, i=i: nc.vector.reciprocal(rs[:, 4 * i:4 * i + 4], sd[:, 4 * i:4 * i + 4]), t2)
            t3 = V.do(lambda rs=rs, i=i, p=p: tt(g3(ch(XK, i), 4), g3(p, 4), bin_(rs[:, 4 * i:4 * i + 4], 4, 128), ALU.mult), t2)
            Rp.free[k] = [t3]
            if last:
                S.dma(lambda i=i: nc.sync.dma_start(
                    out_d.rearrange("b (n p) d -> p (b n) d", p=128)[:, 4 * i:4 * i + 4, :], g3(ch(XK, i), 4)), s_out, t3)
            else:
                pend.append((i, t3))
                if len(pend) > 1:
                    back(*pend.pop(0))
        for x in pend:
            back(*x)
        for x in routed:
            logits(*x)
        barrier()

    def stage1():
        ar = Arena()
        H1 = ar(T)
        bufs = [[ar(512) for _ in range(3)] for _ in range(5)]
        Ra, Rz, Rs, Rg, Rh = (Ring(b) for b in bufs)
        Rp = Ring([(PS[2 * i], PS[2 * i + 1]) for i in range(4)])
        nb, bh5 = SM[:, 64:66], SM[:, 66:68]
        b = w("b_l0a")
        t_b = V.do(lambda b=b, nb=nb: ts(nb, b.rearrange("p (l k) -> p k l", k=2)[:, 0, :], -1.0, None, ALU.mult), wtok(0))
        t_b = V.do(lambda b=b, bh5=bh5: ts(bh5, b.rearrange("p (l k) -> p k l", k=2)[:, 1, :], 0.5, None, ALU.add), wtok(0))
        tH = {}

        def part(l, i):
            src = XT if l == 0 else H1
            k, (pz, ph), fr = Rp.take()

            def f(i=i, l=l, ph=ph, pz=pz, src=src):
                mm(pz, w(f"Wz{l}"), ch(src, i))
                return mm(ph, w(f"Wh{l}"), ch(src, i))
            t0 = PE.do(f, fr, wtok(0), (s_x[i // 2], 16) if l == 0 else tH[(0, i)])
            ka, a, fa = Ra.take()
            kz, z, fz = Rz.take()
            ks, s, fs = Rs.take()
            kg, g, fg = Rg.take()
            t1 = A.do(lambda a=a, l=l, pz=pz: act(a, pz, ACT.Sigmoid, bias=nb[:, l:l + 1], scale=-1.0), t0, t_b, fa)
            t1 = A.do(lambda l=l, pz=pz, z=z: act(z, pz, ACT.Sigmoid, bias=b[:, 2 * l:2 * l + 1]), fz)
            t1 = A.do(lambda l=l, ph=ph, s=s: act(s, ph, ACT.Sigmoid, bias=b[:, 2 * l + 1:2 * l + 2]), fs)
            t2 = V.do(lambda g=g, l=l, ph=ph, s=s: stt(g, ph, bh5[:, l:l + 1], s, ALU.add, ALU.max), t1, fg)
            Rp.free[k] = [t1, t2]
            t3 = V.do(lambda g=g, z=z: tt(g, g, z, ALU.mult), t2)
            if l == 0:
                h = ch(H1, i)
                hprev = H1[:, i * 512 - 1:i * 512] if i % 2 else 0.5
                fh = None
            else:
                kh, h, fh = Rh.take()
                hprev = Rh.bufs[(kh - 1) % 3][:, 511:512] if i % 2 else 0.5
            t4 = V.do(lambda a=a, g=g, h=h, hprev=hprev: nc.vector.tensor_tensor_scan(h, a, g, hprev, ALU.mult, ALU.add), t3, fh, tH.get((l, i - 1)))
            tH[(l, i)] = t4
            Ra.free[ka] = Rz.free[kz] = Rs.free[ks] = Rg.free[kg] = [t4]
            if l == 1:
                t5 = G.do(lambda h=h, i=i: nc.gpsimd.tensor_tensor(ch(XT, i), ch(XT, i), h, ALU.add), t4, (s_x[i // 2], 16))
                Rh.free[kh] = [t5]

        for i in range(NCH + 1):
            if i < NCH:
                part(0, i)
            if i > 0:
                part(1, i - 1)
        for q in engines:
            q.items.append((None, [wtok(7)], None, 0))
        barrier()

    def stage2():
        ar = Arena()
        hb = [ar(512, 64) for _ in range(NCH)]
        Lg, R, E, AL = ar(NT * 64), ar(NT * 64), ar(NT * 64), ar(NT * 64)
        V8, den, rden = ar(NT * 8), ar(NT), ar(NT)
        aT, asum = ar(T, 64), ar(256)
        sm1, b1p, itau = SM[:, 68:69], SM[0:64, 69:70], SM[:, 70:71]
        bsum = SM[:, 71:74]
        siT, rd, gr, gz, gn, tn, Sn = (ar(256) for _ in range(7))
        qk, vK = ar(512, 32), ar(512, 64)
        sc, mx, sm = ar(256, 64), SM[0:64, 74:78], SM[0:64, 78:82]
        sT, yT, yN = ar(256, 64), ar(256), ar(512, 64)
        ss, sd = SM[0:64, 82:86], SM[0:64, 86:90]
        eps = SM[:, 479:480]
        jk = hb[0]
        Zt = hb[1]
        w1, w2, slotT, slot = w("w1"), w("w2"), w("slotT"), w("slot")
        W1 = wtok(1)
        t = PE.do(lambda slot=slot: mm(PS[7][:, 0:1], slot, w("one64")), W1)
        t = V.do(lambda sm1=sm1: nc.vector.tensor_copy(sm1, PS[7][:, 0:1]), t, W1)
        t = PE.do(lambda sm1=sm1, w1=w1: mm(PS[7][0:64, 8:9], w1[:, 64:128], sm1), t)
        t_b1 = V.do(lambda b1p=b1p: tt(b1p, PS[7][0:64, 8:9], w("b1"), ALU.add), t)
        t = V.do(lambda itau=itau: ts(itau, w("tau"), 0.0, None, ALU.max))
        t2 = V.do(lambda: ts(SM[:, 90:91], w("tau"), -1.0, 0.0, ALU.mult, ALU.max))
        t = V.do(lambda itau=itau: stt(itau, itau, 0.1, SM[:, 90:91], ALU.add, ALU.add), t2)
        t_tau = V.do(lambda itau=itau: nc.vector.reciprocal(itau, itau), t)
        t_bs = V.do(lambda bsum=bsum: tt(bsum, w("bih"), w("bhh"), ALU.add))
        Rp, Rl, Rh = Ring([PS[0], PS[1], PS[5], PS[6]]), Ring([PS[2][:, 0:256], PS[3][:, 0:256]]), Ring(hb)
        Lg3, R3, E3, A3 = g3(Lg, NT), g3(R, NT), g3(E, NT), g3(AL, NT)
        v8 = g3(V8, NT)
        hs, first = {}, {}

        def hidden(i):
            k, p, fr = Rp.take()
            t = PE.do(lambda i=i, p=p: mm(p[0:64, :], w1[:, 0:64], ch(XT, i)), fr)
            kh, h, fh = Rh.take()
            t = A.do(lambda h=h, p=p: act(h, p[0:64, :], ACT.Gelu, bias=b1p), t, t_b1, fh)
            Rp.free[k] = [t]
            hs[i] = (kh, h, t)

        def logits(i):
            kh, h, t = hs[i]
            kl, pl, fl = Rl.take()

            def f(h=h, pl=pl):
                for j in range(4):
                    r = mm(pl[:, j * 64:(j + 1) * 64], tile(h, j), w2)
                return r
            t = PE.do(f, t, fl)
            Rh.free[kh] = [t]
            lg = Lg[:, i * 256:(i + 1) * 256]
            b2 = w("b2r").unsqueeze(1).to_broadcast([128, 4, 64])
            t = V.do(lambda b2=b2, lg=lg, pl=pl: tt(g3(lg, 4), g3(pl, 4), b2, ALU.add), t)
            Rl.free[kl] = [t]
            t = V.do(lambda lg=lg: ts(lg, lg, itau, None, ALU.mult), t, t_tau)

            def f(i=i):
                for c in range(4 * i, 4 * i + 4):
                    r = nc.vector.max(V8[:, c * 8:c * 8 + 8], Lg[:, c * 64:c * 64 + 64])
                return r
            t = V.do(f, t)
            q = slice(4 * i, 4 * i + 4)
            te = V.do(lambda q=q: tt(E3[:, q, :], Lg3[:, q, :], v8[:, q, 0:1].to_broadcast([128, 4, 64]), ALU.subtract), t)
            e = E[:, i * 256:(i + 1) * 256]
            te = A.do(lambda e=e: act(e, e, ACT.Exp), te)

            def f(i=i):
                for c in range(4 * i, 4 * i + 4):
                    r = nc.vector.match_replace(R[:, c * 64:c * 64 + 64], V8[:, c * 8:c * 8 + 8], Lg[:, c * 64:c * 64 + 64], FILL)
                return r
            t = V.do(f, t)
            r_ = R[:, i * 256:(i + 1) * 256]
            t = V.do(lambda lg=lg, r_=r_: tt(r_, r_, lg, ALU.not_equal), t)
            first[i] = G.do(lambda e=e, r_=r_: nc.gpsimd.tensor_tensor(e, e, r_, ALU.mult), te, t)

        def weigh(i):
            q = slice(4 * i, 4 * i + 4)
            t = V.do(lambda q=q: nc.vector.tensor_reduce(den[:, q], E3[:, q, :], AX, ALU.add), first[i])
            t = V.do(lambda q=q: nc.vector.reciprocal(rden[:, q], den[:, q]), t)
            return V.do(lambda q=q: tt(A3[:, q, :], E3[:, q, :], bin_(rden[:, q], 4, 64), ALU.mult), t)

        def inputs(b, t):
            def f(b=b):
                for c in range(8):
                    r = mm(PS[4][:, b * 64:(b + 1) * 64], tile(XK, b * 8 + c), A3[:, b * 8 + c, :], c == 0, c == 7)
                return r
            return PE.do(f, t)

        for i in range(NCH):
            hidden(i)
        whole = []
        for i in range(NCH + 1):
            if i < NCH:
                logits(i)
            if whole:
                inputs(*whole.pop(0))
            if i > 0:
                t_al = weigh(i - 1)
            if i > 0 and i % 2 == 0:
                b = i // 2 - 1
                whole.append((b, t_al))
                t_as = V.do(lambda A3=A3, asum=asum, b=b: nc.vector.tensor_reduce(asum[:, b * 64:(b + 1) * 64],
                            A3[:, b * 8:b * 8 + 8, :].rearrange("p c s -> p s c"), AX, ALU.add), t_al)
        t_si = inputs(*whole.pop(0))
        last_m = t_al
        t0 = PE.do(lambda asum=asum: mm(PS[5][:, 0:256], w("ones"), asum), t_as, Rp.free)
        t_aT = {}

        def turn(i):
            p, fr = tb[i % 2]

            def f(i=i, p=p):
                for j in range(4):
                    r = nc.tensor.transpose(p[0:64, j * 128:(j + 1) * 128], A3[:, 4 * i + j, :], w("ident"))
                return r
            t = PE.do(f, fr)
            t_aT[i] = t = A.do(lambda i=i, p=p: nc.scalar.copy(ch(aT, i), p[0:64, :]), t)
            tb[i % 2] = (p, [t])

        t = V.do(lambda rd=rd: ts(rd, PS[5][:, 0:256], 1e-8, None, ALU.add), t0)
        tb = [(PS[5], [t]), (PS[4], None)]
        t = V.do(lambda rd=rd: nc.vector.reciprocal(rd, rd), t)
        t = V.do(lambda rd=rd, siT=siT: tt(siT, PS[4][:, 0:256], rd, ALU.mult), t, t_si)
        tb[1] = (PS[4], [t])
        s4 = slotT.unsqueeze(1).to_broadcast([128, 4, 64])
        Wih, Whh = w("WihT"), w("WhhT")

        def f(Whh=Whh, Wih=Wih, s4=s4, siT=siT):
            for g in range(2):
                mm(PS[6][:, g * 256:(g + 1) * 256], tile(Wih, g), siT, True, False)
                mm(g3(PS[6][:, g * 256:(g + 1) * 256], 4), tile(Whh, g), s4, False, True)
            mm(PS[7][:, 0:256], tile(Wih, 2), siT)
            return mm(g3(PS[7][:, 256:512], 4), tile(Whh, 2), s4)
        t0 = PE.do(f, t, t_b1)
        t1 = A.do(lambda bsum=bsum, gr=gr: act(gr, PS[6][:, 0:256], ACT.Sigmoid, bias=bsum[:, 0:1]), t0, t_bs)
        tz = A.do(lambda bsum=bsum, gz=gz: act(gz, PS[6][:, 256:512], ACT.Sigmoid, bias=bsum[:, 1:2]))
        turn(0)
        t = V.do(lambda gr=gr, tn=tn: stt(tn, PS[7][:, 256:512], w("bhh")[:, 2:3], gr, ALU.add, ALU.mult), t1)
        t = V.do(lambda tn=tn: stt(tn, PS[7][:, 0:256], w("bih")[:, 2:3], tn, ALU.add, ALU.add), t)
        t = A.do(lambda gn=gn, tn=tn: act(gn, tn, ACT.Tanh), t)
        turn(1)
        t = V.do(lambda gn=gn, s4=s4, tn=tn: tt(g3(tn, 4), s4, g3(gn, 4), ALU.subtract), t)
        t = V.do(lambda gz=gz, tn=tn: tt(tn, tn, gz, ALU.mult), t, tz)
        t_S = V.do(lambda Sn=Sn, gn=gn, tn=tn: tt(Sn, tn, gn, ALU.add), t)

        def f(Sn=Sn):
            mm(PS[0][0:32, 0:256], w("wq"), Sn)
            return mm(PS[0][0:32, 256:512], w("wk"), Sn)
        t = PE.do(f, t_S)
        tq = V.do(lambda qk=qk: ts(qk[:, 0:256], PS[0][0:32, 0:256], w("bq"), None, ALU.add), t)
        tq = V.do(lambda qk=qk: ts(qk[:, 256:512], PS[0][0:32, 256:512], w("bk"), None, ALU.add), t)

        def f(Sn=Sn):
            for b in range(NB):
                r = mm(PS[1][0:64, b * 128:(b + 1) * 128], Sn[:, b * 64:(b + 1) * 64], w("wv"))
            return r
        t = PE.do(f, t_S)
        tv = V.do(lambda vK=vK: tt(g3(vK, 4), g3(PS[1][0:64, :], 4), w("bvr").unsqueeze(1).to_broadcast([64, 4, 128]), ALU.add), t)

        def f(qk=qk):
            for b in range(NB):
                r = mm(PS[2][0:64, b * 64:(b + 1) * 64], qk[:, b * 64:(b + 1) * 64], qk[:, 256 + b * 64:256 + (b + 1) * 64])
            return r
        t = PE.do(f, tq, last_m)
        s3 = g3(sc, 4)
        p3 = g3(PS[2][0:64, 0:256], 4)
        tm = V.do(lambda mx=mx, p3=p3: nc.vector.tensor_reduce(mx, p3, AX, ALU.max), t)
        t = V.do(lambda mx=mx, p3=p3, s3=s3: tt(s3, p3, bin_(mx, 4, 64), ALU.subtract), tm)
        t = A.do(lambda sc=sc: act(sc, sc, ACT.Exp, scale=32 ** -0.5), t)
        turn(2)
        turn(3)
        t = V.do(lambda s3=s3, sm=sm: nc.vector.tensor_reduce(sm, s3, AX, ALU.add), t)
        t = V.do(lambda sm=sm: nc.vector.reciprocal(sm, sm), t)
        t = V.do(lambda s3=s3, sm=sm: tt(s3, s3, bin_(sm, 4, 64), ALU.mult), t)

        def f(sc=sc):
            for b in range(NB):
                r = nc.tensor.transpose(PS[3][0:64, b * 64:(b + 1) * 64], sc[:, b * 64:(b + 1) * 64], w("ident")[0:64, 0:64])
            return r
        t = PE.do(f, t, last_m)
        t = V.do(lambda sT=sT: nc.vector.tensor_copy(sT, PS[3][0:64, 0:256]), t)

        def f(sT=sT, vK=vK):
            for b in range(NB):
                r = mm(PS[0][:, b * 64:(b + 1) * 64], vK[:, b * 128:(b + 1) * 128], sT[:, b * 64:(b + 1) * 64])
            return r
        t = PE.do(f, t, tv)
        t = V.do(lambda Sn=Sn, yT=yT: tt(yT, PS[0][:, 0:256], Sn, ALU.add), t)

        def f(yT=yT):
            for b in range(NB):
                r = mm(PS[1][0:64, b * 128:(b + 1) * 128], yT[:, b * 64:(b + 1) * 64], w("cen"))
            return r
        t0 = PE.do(f, t)

        def f(jk=jk, ss=ss):
            for b in range(NB):
                r = act(jk[:, b * 128:(b + 1) * 128], PS[1][0:64, b * 128:(b + 1) * 128], ACT.Square, scale=128 ** -0.5, acc=ss[:, b:b + 1])
            return r
        t = A.do(f, t0)
        t = A.do(lambda eps=eps, sd=sd, ss=ss: act(sd, ss, ACT.Sqrt, bias=eps[0:64, :]), t, t_eps)
        turn(4)
        turn(5)
        t = V.do(lambda sd=sd: nc.vector.reciprocal(sd, sd), t)
        t = V.do(lambda sd=sd, yN=yN: tt(g3(yN, 4), g3(PS[1][0:64, :], 4), bin_(sd, 4, 128), ALU.mult), t)

        def f(yN=yN):
            for b in range(NB):
                r = nc.tensor.transpose(PS[0][:, b * 64:(b + 1) * 64], yN[:, b * 128:(b + 1) * 128], w("ident")[0:64, 0:64])
            return r
        t = PE.do(f, t)
        t = V.do(lambda yT=yT: ts(yT, PS[0][:, 0:256], w("lng"), w("lnb"), ALU.mult, ALU.add), t)
        t = PE.do(lambda yT=yT: mm(PS[1][:, 0:256], w("wvp"), yT), t)
        t = V.do(lambda siT=siT: ts(siT, PS[1][:, 0:256], w("bvp"), None, ALU.add), t)

        def f(siT=siT):
            for b in range(NB):
                r = mm(PS[0][0:64, b * 128:(b + 1) * 128], siT[:, b * 64:(b + 1) * 64], w("wo"))
            return r
        t = PE.do(f, t)
        t_Z = V.do(lambda Zt=Zt: nc.vector.tensor_copy(Zt, PS[0][0:64, :]), t)
        turn(6)
        turn(7)
        Ro = Ring([PS[6], PS[7], PS[2], PS[3]], [t_S])
        for i in range(NCH):
            ko, o, fo = Ro.take()
            b = i // 2
            t = PE.do(lambda Zt=Zt, aT=aT, b=b, i=i, o=o: mm(o, Zt[:, b * 128:(b + 1) * 128], ch(aT, i)), t_aT[i], t_Z, fo)
            t = V.do(lambda i=i, o=o: stt(ch(XT, i), o, w("bo"), ch(XT, i), ALU.add, ALU.add), t)
            Ro.free[ko] = [t]
        barrier()
    def stage3():
        ar = Arena()
        W2 = wtok(2)
        NU = 560
        hm, hmT, ident, ones = w("hm"), w("hmT"), w("ident"), w("ones")
        posT, PK = ar(1024, 64, dt=FR), ar(512, dt=FR)
        E64 = ar(448, 64, dt=FR)
        XKs = (ar(1024, dt=FR), ar(1024, dt=FR))
        KTb, KTs = ar(1024), [(ar(1024, dt=FR), ar(1024, dt=FR)) for _ in range(2)]
        VKs = [ar(1024) for _ in range(2)]
        VM = [ar(128, 112) for _ in range(2)]
        mark = ar.o

        SO, sidx, sif = ar(280), ar(35, dt=I32), ar(35)
        xs, ks = ar(140), ar(140)
        KB = [ar(576) for _ in range(NB)]
        MK, MT, one64 = ar(512), ar(1024, 64), ar(1024, 64)
        Rq = Ring([ar(512) for _ in range(3)])
        cand, ksum = SM[0:64, 192:200], SM[:, 216:220]
        G.dma(lambda sidx=sidx: nc.gpsimd.dma_start(sidx, sidx_d.partition_broadcast(128)), s_si, now())
        t = V.do(lambda sidx=sidx, sif=sif: nc.vector.tensor_copy(sif, sidx), (s_si, 16), W2)
        t_so = V.do(lambda SO=SO, sif=sif: tt(g3(SO, 8), sif.unsqueeze(1).to_broadcast([128, 8, 35]), bin_(w("tokid"), 8, 35), ALU.is_equal), t)
        t_e = V.do(lambda E64=E64: nc.vector.tensor_copy(E64, w("E64")))
        t_one = V.do(lambda one64=one64: nc.vector.memset(one64, 1.0))
        Rp = Ring([PS[0], PS[1]])
        Rm = Ring([PSALL[:, 1024 * (1 + i):1024 * (2 + i)].rearrange("p (g k) -> p g k", g=2) for i in range(2)])
        MK4 = MK.rearrange("p (c b h) -> p c b h", c=8, b=4)

        def f(SO=SO):
            for b in range(NB):
                for c in range(8):
                    r = mm(PS[6][:, b * 35:(b + 1) * 35], tile(XK, b * 8 + c), SO[:, c * 35:(c + 1) * 35], c == 0, c == 7)
            return r
        t = PE.do(f, t_so)
        t = V.do(lambda xs=xs: nc.vector.tensor_copy(xs, PS[6][:, 0:140]), t)
        t = PE.do(lambda xs=xs: mm(PS[7][:, 0:140], w("aWk"), xs), t)
        t_ks = V.do(lambda ks=ks: ts(ks, PS[7][:, 0:140], w("abk"), None, ALU.add), t)
        t_sum = V.do(lambda ks=ks, ksum=ksum: nc.vector.tensor_reduce(ksum, g3(ks, 4), AX, ALU.add), t_ks)
        hm2 = g3(hm, 2)
        qs, t_kb = {}, {}

        def keys(b):
            kv = g3(KB[b], 2)
            V.do(lambda b=b, kv=kv: tt(kv[:, :, 0:280].rearrange("p g (h s) -> p g h s", h=8),
                            ks[:, b * 35:(b + 1) * 35].unsqueeze(1).unsqueeze(1).to_broadcast([128, 2, 8, 35]),
                            hm2.unsqueeze(3).to_broadcast([128, 2, 8, 35]), ALU.mult), t_ks)
            t_kb[b] = V.do(lambda b=b, kv=kv: ts(kv[:, :, 280:288], hm2, ksum[:, b:b + 1], None, ALU.mult), t_sum)

        def query(n):
            k, p, fr = Rp.take()
            t = PE.do(lambda n=n, p=p: mm(p, w("aWq"), ch(XT, n)), fr)
            kq, q, fq = Rq.take()
            t = A.do(lambda p=p, q=q: act(q, p, ACT.Identity, bias=w("abq")), t, fq)
            Rp.free[k] = [t]
            qs[n] = (kq, q, t)

        t_mk = None
        query(0)
        keys(0)
        for n in range(NCH):
            b, i = divmod(n, 2)
            if n + 1 < NCH:
                query(n + 1)
            kq, q, t_q = qs[n]
            kv = g3(KB[b], 2)
            for j in range(4):
                km, pm, fm = Rm.take()

                def f(j=j, kv=kv, pm=pm, q=q):
                    for g in range(2):
                        r = mm(pm[:, g, 0:288], tile(q, j), kv[:, g, :])
                    return r
                t = PE.do(f, t_q, t_kb[b], fm)
                m = g3(MK4[:, 4 * i + j, b, :], 2)
                t1 = V.do(lambda m=m, pm=pm: nc.vector.tensor_reduce(m, pm[:, :, 0:280].rearrange("p g (h s) -> p g h s", h=8), AX, ALU.max), t)
                t_mk = V.do(lambda m=m, pm=pm: stt(m, pm[:, :, 280:288], -1.0 / 35, m, ALU.mult, ALU.add), t1)
                Rm.free[km] = [t_mk]
                if i == 1 and j == 1 and b + 1 < NB:
                    keys(b + 1)
            Rq.free[kq] = [t]

        def f(MK=MK, ident=ident):
            for c in range(8):
                r = nc.tensor.transpose(PS[c // 4][0:64, (c % 4) * 128:(c % 4 + 1) * 128], MK[:, c * 64:(c + 1) * 64], ident)
            return r
        t = PE.do(f, t_mk, Rp.free)
        t_mt = V.do(lambda MT=MT: nc.vector.tensor_scalar(MT, PSALL[0:64, 0:1024], 8 ** -0.5, None, ALU.mult), t)
        end1 = now()

        Rg = Ring([PS[5], PS[6], PS[7]], [t_ks])
        small = {}
        ar.o = mark
        Xs, Qb = ar(NU), ar(NU)
        Qs = [(ar(NU, dt=FR), ar(NU, dt=FR)) for _ in range(2)]
        PR, PTt = ar(1024, 112), ar(896)
        Oh = [(ar(640, 112, dt=FR), ar(640, 112, dt=FR)) for _ in range(2)]
        Ro = Ring([ar(512, dt=FR) for _ in range(4)])
        posB = Ring([ar(512, 112) for _ in range(2)])
        ot_ = Ring([ar(512) for _ in range(2)])
        ob_ = Ring([ar(128, 112) for _ in range(2)])

        def keys_values(b):
            d = small[b] = {}
            kt, vk = KTs[b % 2], VKs[b % 2]
            old = small[b - 2]["read"] if b > 1 else None
            xm = SM[:, 220 + b:221 + b]
            d["xm"] = A.do(lambda b=b, xm=xm: act(KTb, XT[:, b * 1024:(b + 1) * 1024], ACT.Copy, scale=1.0 / 1024, acc=xm),
                           small[b - 1]["kt"] if b else None)
            xk = XK[:, b * 1024:(b + 1) * 1024]
            t = A.do(lambda xk=xk: nc.scalar.copy(XKs[0], xk), small[b - 1]["gather"] if b else None)
            d["xk"] = G.do(lambda xk=xk: nc.gpsimd.tensor_tensor(XKs[1], xk, XKs[0].bitcast(F32), ALU.subtract), t)
            yield
            d["kt"] = []
            for i in range(2):
                k, p, fr = Rg.take()
                t = PE.do(lambda b=b, i=i, p=p: mm(p, w("aWk"), ch(XT, 2 * b + i)), fr)
                t = A.do(lambda i=i, p=p: act(ch(KTb, i), p, ACT.Identity, bias=w("abk")), t, d["xm"])
                Rg.free[k] = [t]
                t = A.do(lambda i=i, kt=kt: nc.scalar.copy(ch(kt[0], i), ch(KTb, i)), t, old)
                d["kt"].append(G.do(lambda i=i, kt=kt: nc.gpsimd.tensor_tensor(ch(kt[1], i), ch(KTb, i), ch(kt[0], i).bitcast(F32), ALU.subtract), t))
                yield
            k, p, fr = Rg.take()

            def f(p=p, xm=xm):
                mm(p[:, 0:1], w("aWv"), xm, True, False)
                mm(p[:, 0:1], w("abvr")[0:1, :], ones[0:1, 0:1], False, True)
                mm(p[0:112, 128:256], xm.to_broadcast([128, 112]), w("aWv"), True, False)
                return mm(p[0:112, 128:256], ones[0:1, 0:112], w("abvr")[0:1, :], False, True)
            t = PE.do(f, fr, d["xm"])
            d["vmc"] = SM[:, 224 + b:225 + b]
            d["vmr"] = VM[b % 2]
            V.do(lambda d=d, p=p: nc.vector.tensor_copy(d["vmc"], p[:, 0:1]), t)
            d["vm"] = V.do(lambda d=d, p=p: nc.vector.tensor_copy(d["vmr"], p[0:112, 128:256]), small[b - 2]["done"] if b > 1 else None)
            Rg.free[k] = [d["vm"]]
            yield
            for i in range(2):
                k, p, fr = Rg.take()

                def f(b=b, i=i, p=p):
                    for j in range(4):
                        r = mm(p[:, j * 128:(j + 1) * 128], tile(XT, b * 8 + 4 * i + j), w("aWv"))
                    return r
                t = PE.do(f, fr)
                d["v"] = V.do(lambda i=i, p=p, vk=vk: tt(g3(ch(vk, i), 4), g3(p, 4), w("abvr").unsqueeze(1).to_broadcast([128, 4, 128]), ALU.add), t, old)
                Rg.free[k] = [d["v"]]
                yield

        def stream(args, make):
            made = []
            for k in range(len(args)):
                while len(made) < min(k + 3, len(args)):
                    made.append(make(args[len(made)]))
                yield made[k]

        def queries(b):
            d = small[b]
            d["q"] = []

            def hot(a):
                c, u0, u1 = a
                n, o = (u1 - u0) * 16, u0 * 16
                ko, oh, fo = Ro.take()
                oh = oh[:, 0:n]
                t = V.do(lambda c=c, n=n, o=o, oh=oh, u0=u0, u1=u1: tt(oh.rearrange("p (u h) -> p u h", h=16),
                                    PK4[:, c, b, :].unsqueeze(1).to_broadcast([128, u1 - u0, 16]),
                                    w("iotau")[:, o:o + n].rearrange("p (u h) -> p u h", h=16), ALU.is_equal), fo, t_pk)
                return ko, oh, t
            cuts = ((0, 18), (18, 35))
            hots = stream([(c, u0, u1) for u0, u1 in cuts for c in range(8)], hot)
            for g, (u0, u1) in enumerate(cuts):
                n, o = (u1 - u0) * 16, u0 * 16
                k, p, fr = Rg.take()
                for c in range(8):
                    ko, oh, t = next(hots)

                    def f(c=c, n=n, oh=oh, p=p):
                        mm(p[:, 0:n], tile(XKs[0], c), oh, c == 0, False)
                        return mm(p[:, 0:n], tile(XKs[1], c), oh, False, c == 7)
                    t = PE.do(f, t, d["xk"], fr)
                    Ro.free[ko] = [t]
                    if c % 2:
                        yield
                d["gather"] = t
                x = Xs[:, o:o + n]
                t = A.do(lambda n=n, p=p, x=x: nc.scalar.copy(x, p[:, 0:n]), t, small[b - 1]["xs"] if b else None)
                Rg.free[k] = [t]
                yield
                k, p, fr = Rg.take()
                d["xs"] = t = PE.do(lambda n=n, p=p, x=x: mm(p[:, 0:n], w("aWq"), x), t, fr)
                qb = Qb[:, o:o + n]
                t = V.do(lambda n=n, p=p, qb=qb, u0=u0, u1=u1: stt(qb.rearrange("p (u h) -> p u h", h=16), p[:, 0:n].rearrange("p (u h) -> p u h", h=16),
                                     w("abq"), hm.unsqueeze(1).to_broadcast([128, u1 - u0, 16]), ALU.add, ALU.mult), t)
                Rg.free[k] = [t]
                d["q"].append(split(qb, Qs[b % 2][0][:, o:o + n], Qs[b % 2][1][:, o:o + n], t))
                yield

        def put(b):
            d = small[b]
            obh, obl = Oh[b % 2]
            pbs = []
            for i in range(2):
                k, p, fr = Rg.take()
                t = PE.do(lambda b=b, i=i, p=p: mm(p[0:112, :], E64[:, b * 112:(b + 1) * 112], ch(posT, i)), fr, t_pos, t_e)
                kp, pb, fp = posB.take()
                t_pb = A.do(lambda p=p, pb=pb: nc.scalar.copy(pb, p[0:112, :]), t, fp)
                Rg.free[k] = [t_pb]
                pbs.append((pb, t_pb))
                posB.free[kp] = []
            yield

            def hot(a):
                i, j = a
                ko, oh, fo = Ro.take()
                oh = oh[0:112, :]
                t_o = V.do(lambda i=i, j=j, oh=oh: ts(oh, pbs[i][0], w("ucol")[:, j:j + 1], None, ALU.is_equal), pbs[i][1], fo)
                posB.free[i] = [t_o]
                return ko, oh, t_o
            hots = stream([(i, j) for i in range(2) for j in range(5)], hot)
            for i in range(2):
                k, p, fr = Rg.take()
                for j in range(5):
                    ko, oh, t_o = next(hots)

                    def f(j=j, obh=obh, obl=obl, oh=oh, p=p):
                        mm(p, obh[:, j * 128:(j + 1) * 128], oh, j == 0, False)
                        return mm(p, obl[:, j * 128:(j + 1) * 128], oh, False, j == 4)
                    t = PE.do(f, t_o, d["ob"], fr)
                    Ro.free[ko] = [t]
                    if j % 2:
                        yield
                d["put"] = t
                kt, o, fo = ot_.take()
                t = A.do(lambda d=d, o=o, p=p: act(o, p, ACT.Identity, bias=d["vmc"]), t, fo, d["vm"])
                Rg.free[k] = [t]
                yield
                k, p, fr = Rg.take()
                t = PE.do(lambda o=o, p=p: mm(p, w("aWo"), o), t, fr)
                ot_.free[kt] = [t]
                x = ch(XT, 2 * b + i)
                Rg.free[k] = [V.do(lambda p=p, x=x: stt(x, p, w("abo"), x, ALU.add, ALU.add), t, d["v"], d["kt"])]
                yield

        kv0 = keys_values(0)
        for _ in range(4):
            next(kv0)
        t = t_mt
        for r in range(5):
            t = V.do(lambda MT=MT, cand=cand: nc.vector.max(cand, MT), t)
            if r == 4:
                t = V.do(lambda cand=cand: nc.vector.memset(cand[:, 3:8], FILL), t)
            t = V.do(lambda MT=MT, cand=cand: nc.vector.match_replace(MT, cand, MT, FILL), t)
        t = V.do(lambda MT=MT: ts(MT, MT, FILL, None, ALU.is_equal), t)
        t = V.do(lambda MT=MT, one64=one64: nc.vector.tensor_tensor_scan(one64, one64, MT, 0.0, ALU.mult, ALU.add), t, t_one)
        t_pos = V.do(lambda MT=MT, one64=one64, posT=posT: tt(posT, one64, MT, ALU.mult), t)

        def f(ident=ident, posT=posT):
            for c in range(8):
                r = nc.tensor.transpose(PS[2][:, c * 64:(c + 1) * 64], tile(posT.bitcast(F32), c), ident[0:64, 0:64])
            return r
        t = PE.do(f, t_pos, end1)
        t_pk = V.do(lambda PK=PK: nc.vector.tensor_copy(PK, PS[2]), t)
        PK4 = PK.bitcast(F32).rearrange("p (c b h) -> p c b h", c=8, b=4)
        for _ in kv0:
            pass

        barrier()

        def run(gen, n):
            for _ in range(n):
                if gen is None or next(gen, gen) is gen:
                    return

        def chain(*gens):
            for g in gens:
                yield from g

        un = {}

        def sm(u):
            return [SM[0:112, 228 + 4 * (u % 2) + i:229 + 4 * (u % 2) + i] for i in range(4)]

        def scores(u):
            b, j = divmod(u, 5)
            d = small[b]
            kh, kl = KTs[b % 2]
            qh, ql = (x[:, j * 112:(j + 1) * 112] for x in Qs[b % 2])

            def f(kh=kh, kl=kl, qh=qh, ql=ql):
                for i in range(2):
                    r = mm3(PS[i][0:112, :], (qh, ql), (ch(kh, i), ch(kl, i)))
                return r
            t = PE.do(f, d["q"], d["kt"], un[u - 1]["exp"] if u else None)
            mx, nmx, sm_, rs = sm(u)
            t = V.do(lambda mx=mx: nc.vector.tensor_reduce(mx, PSALL[0:112, 0:1024], AX, ALU.max), t, un[u - 2]["done"] if u > 1 else None)
            t = V.do(lambda mx=mx, nmx=nmx: ts(nmx, mx, -8 ** -0.5, None, ALU.mult), t)
            t = A.do(lambda nmx=nmx, sm_=sm_: act(PR, PSALL[0:112, 0:1024], ACT.Exp, bias=nmx, scale=8 ** -0.5, acc=sm_), t)
            un[u] = {"exp": t}

        def turned(u):
            def f():
                for c in range(8):
                    r = nc.tensor.transpose(PS[2 + c // 4][:, (c % 4) * 112:(c % 4 + 1) * 112], tile(PR, c), ident[0:112, 0:112])
                return r
            t = PE.do(f, un[u]["exp"], un[u - 1]["pt"] if u else None)
            old = un[u - 1]["pv"] if u else None
            t1 = A.do(lambda: nc.scalar.copy(PTt[:, 0:448], PS[2][:, 0:448]), t, old)
            t2 = V.do(lambda: nc.vector.tensor_copy(PTt[:, 448:896], PS[3][:, 0:448]), t, old)
            un[u]["pt"] = [t1, t2]

        def values(u):
            b, j = divmod(u, 5)
            d = small[b]
            vk = VKs[b % 2]

            def f(vk=vk):
                for c in range(8):
                    r = mm(PS[4][0:112, 0:128], PTt[:, c * 112:(c + 1) * 112], tile(vk, c), c == 0, c == 7)
                return r
            un[u]["pv"] = d["read"] = t = PE.do(f, un[u]["pt"], d["v"], un[u - 1]["out"] if u else None)
            mx, nmx, sm_, rs = sm(u)
            t1 = V.do(lambda rs=rs, sm_=sm_: nc.vector.reciprocal(rs, sm_), un[u]["exp"])
            ko, ob, fo = ob_.take()
            t = V.do(lambda d=d, ob=ob, rs=rs: stt(ob, PS[4][0:112, 0:128], rs, d["vmr"], ALU.mult, ALU.subtract), t, t1, d["vm"], fo)
            un[u]["out"] = un[u]["done"] = d["done"] = t
            t = V.do(lambda ob=ob: tt(ob, ob, hmT, ALU.mult), t)
            obh, obl = (x[:, j * 128:(j + 1) * 128] for x in Oh[b % 2])
            d["ob"] = t = split(ob, obh, obl, t, small[b - 2]["put"] if b > 1 else None)
            ob_.free[ko] = [t]

        run(queries(0), 99)
        scores(0)
        work = chain(keys_values(1), queries(1))
        for u in range(5 * NB):
            b, j = divmod(u, 5)
            if j == 0:
                per = (5, 7, 7, 2)[b]
            turned(u)
            if u + 1 < 5 * NB:
                if j == 4:
                    run(work, 99)
                scores(u + 1)
            run(work, per // 2)
            values(u)
            run(work, per - per // 2)
            if j == 4:
                work = chain(put(b), *((keys_values(b + 2), queries(b + 2)) if b + 2 < NB else ()))
        run(work, 99)
        barrier()

    def stage4():
        ar, ax = Arena(), Arena(XKt, XKr, T)
        b2 = SM[:, 92:93]
        Gg, Gs = ar(128), (ar(128, dt=FR), ar(128, dt=FR))
        W2 = wtok(2)
        t = V.do(lambda Gg=Gg: tt(Gg, w("gate1"), w("gate0"), ALU.subtract), W2)
        tg = split(Gg, Gs[0], Gs[1], t)
        t = V.do(lambda b2=b2: tt(b2, w("fb2")[:, 0:1], w("fb2")[:, 1:2], ALU.add))
        tb = V.do(lambda b2=b2: tt(b2, b2, w("sb2"), ALU.add), t)
        ups = {}
        for n in (8, 9, 10, 11, 0, 1, 2, 3, 4, 5, 6, 7):
            q = n * 128 if n < 8 else (n - 8) * 128
            for s, nm in ((0, "fw1" if n < 8 else "sw1"), (1, "fw2" if n < 8 else "sw2")):
                h, l = ar(128, dt=FR), ar(128, dt=FR)
                src = w(nm)[:, q:q + 128]
                ups[(n, s)] = (h, l, split(src, h, l, W2))
        x_ = Ring([(ar(512, dt=FR), ar(512, dt=FR)) for _ in range(2)])
        m_ = Ring([tuple(a(512, dt=FR) for _ in range(4)) for a in (ar, ax)])
        Rm = Ring([ax(512)])
        Rr = Ring([ar(512) for _ in range(4)])
        Rh = Ring([(ar(512, dt=FR), ar(512, dt=FR)) for _ in range(6)])
        Rp, Ro, Rd = Ring(PS[0:5]), Ring(PS[5:7]), Ring(PS[7:8])
        second, pend = [], []

        xs_ = {}

        def part_x(i):
            kx, (xh, xl), fx = x_.take()
            xs_[i] = (kx, xh, xl, split(ch(XT, i), xh, xl, fx))

        def prepare(i):
            kx, xh, xl, t_x = xs_[i]
            kd, d, fd = Rd.take()
            t = PE.do(lambda d=d, xh=xh, xl=xl: mm3(d, Gs, (xh, xl)), tg, t_x, fd)
            km, (h0, l0, h1, l1), fm = m_.take()
            kq, m, fq = Rm.take()
            t = V.do(lambda d=d, m=m: ts(m, d, 0.0, None, ALU.is_gt), t, fq)
            Rd.free[kd] = [t]
            t1 = V.do(lambda h1=h1, m=m, xh=xh: tt(h1, xh.bitcast(F32), m, ALU.mult), t, fm)
            t2 = G.do(lambda l1=l1, m=m, xl=xl: nc.gpsimd.tensor_tensor(l1, xl.bitcast(F32), m, ALU.mult), t, fm, t_x)
            t1 = V.do(lambda h0=h0, h1=h1, xh=xh: tt(h0, xh.bitcast(F32), h1.bitcast(F32), ALU.subtract), t1)
            t2 = G.do(lambda l0=l0, l1=l1, xl=xl: nc.gpsimd.tensor_tensor(l0, xl.bitcast(F32), l1.bitcast(F32), ALU.subtract), t2)
            Rm.free[kq] = [t1, t2]
            return dict(kx=kx, km=km, x=(xh, xl), x0=(h0, l0), x1=(h1, l1), tx=t_x, tm=[t1, t2])

        def parts(n, i, rest):
            kh, h, fh = Rh.take()
            pend.append((n, i, kh, h, rest(h, fh)))

        outs = {}

        def down(n, i, kh, h, th):
            if n == 8:
                outs[i] = Ro.take()
            ko, o, fo = outs[i]
            wh, wl, tw = ups[(n, 1)]
            t = PE.do(lambda h=h, n=n, o=o, wh=wh, wl=wl: mm3(o, (wh, wl), h, n == 8, n == 7), th, tw, fo if n == 8 else None)
            Rh.free[kh] = [t]
            if n == 7:
                x = ch(XT, i)
                t = V.do(lambda o=o, x=x: stt(x, o, b2, x, ALU.add, ALU.add), t, tb, P_[i]["tx"])
                Ro.free[ko] = [t]

        part_x(0)
        P_ = {0: prepare(0)}
        for i in range(NCH):
            d = P_[i]
            for n in (8, 9, 10, 11, 0, 1, 2, 3, 4, 5, 6, 7):
                src = d["x"] if n >= 8 else (d["x0"] if n < 4 else d["x1"])
                bb = w("fb1")[:, n:n + 1] if n < 8 else w("sb1")[:, n - 8:n - 7]
                wh, wl, tw = ups[(n, 0)]
                k, p, fr = Rp.take()
                t = PE.do(lambda p=p, src=src, wh=wh, wl=wl: mm3(p, (wh, wl), src), fr, tw, d["tm"] if n < 8 else d["tx"])
                if n == 7:
                    x_.free[d["kx"]] = m_.free[d["km"]] = [t]
                kr, r, fe = Rr.take()
                if n % 2:
                    t = V.do(lambda bb=bb, p=p, r=r: ts(r, p, bb, 0.0, ALU.add, ALU.max), t, fe)
                else:
                    t = A.do(lambda bb=bb, p=p, r=r: act(r, p, ACT.Relu, bias=bb), t, fe)
                Rp.free[k] = [t]

                def rest(h, fh, n=n, t=t, r=r, kr=kr):
                    if n % 2:
                        t2 = A.do(lambda h=h, r=r: nc.scalar.copy(h[0], r), t, fh)
                    else:
                        t2 = V.do(lambda h=h, r=r: nc.vector.tensor_copy(h[0], r), t, fh)
                    if n % 4 == 3:
                        t2 = G.do(lambda h=h, r=r: nc.gpsimd.tensor_tensor(h[1], r, h[0].bitcast(F32), ALU.subtract), t2)
                    else:
                        t2 = V.do(lambda h=h, r=r: tt(h[1], r, h[0].bitcast(F32), ALU.subtract), t2)
                    Rr.free[kr] = [t2]
                    return t2
                second.append((n, i, rest))
                if len(second) > 1:
                    parts(*second.pop(0))
                if len(pend) > 3:
                    down(*pend.pop(0))
                if n == 10 and i + 1 < NCH:
                    part_x(i + 1)
                if n == 1 and i + 1 < NCH:
                    P_[i + 1] = prepare(i + 1)
        parts(*second.pop(0))
        for q in pend:
            down(*q)
        barrier()

    def stage5():
        ar = Arena()
        W3 = wtok(3)
        CS, bvr = ar(1024), ar(1024)
        S.dma(lambda CS=CS: nc.sync.dma_start(CS, cs_d), s_cs2, now())
        S.dma(lambda bvr=bvr: nc.sync.dma_start(bvr, bkv_d[1:2, :].partition_broadcast(128)), s_kv)
        CSt, KVt = (s_cs2, 16), (s_kv, 16)
        sets = [tuple(ar(n) for n in (2048, 2048, 1024, 2048, 1040)) for _ in range(2)]
        AM = Ring([ar(512) for _ in range(2)])
        Sb = Ring([ar(260) for _ in range(2)])
        Ok, OT, Wo = ar(1024), (ar(1024, dt=FR), ar(1024, dt=FR)), (ar(256, dt=FR), ar(256, dt=FR))
        aw = Arena(W, Wr, spans[2][1])
        aw.o = spans[1][0]
        xp = [(aw(512, dt=FR), aw(512, dt=FR)) for _ in range(2)]
        wp_ = [(aw(768, dt=FR), aw(768, dt=FR)) for _ in range(2)]
        den = [SM[:, 208:212], SM[:, 332:336]]
        co = w("coss")
        v5 = lambda V_: V_.rearrange("p (c h d) -> p c h d", c=4, h=4)
        t_one = None
        for q in sets:
            t_one = V.do(lambda q=q, v5=v5: nc.vector.memset(v5(q[4])[:, :, :, 64:65], 1.0))
        k5 = lambda K_: K_.rearrange("p (c h s d) -> p c h s d", c=4, h=4, s=2)
        Rp, Ro = Ring([PS[0], PS[1]]), Ring([PS[5], PS[6]])
        Ra = Ring([PSALL[:, 1024:2048].rearrange("p (e q j t) -> p q e j t", e=2, q=2, j=2)[:, q] for q in range(2)])
        Sp, Rf = PS[4], Ring([PS[7]])
        cWq, cWk, cWv, cWo = w("cWq"), w("cWk"), w("cWv"), w("cWo")
        dm = w("dmask").unsqueeze(1).unsqueeze(1).to_broadcast([128, 2, 2, 128])
        a4 = lambda am: am.rearrange("p (e j t) -> p e j t", e=2, j=2)
        its = [(b, g, i) for b in range(NB) for g in range(4) for i in range(2)]
        tok, fin = {}, {"ok": None, "ot": None}
        w_of, x_of, before = {}, {}, now()

        def weights(n):
            g = n % 4
            wh, wl = wp_[n % 2]
            old = tok[2 * n - 3]["proj"] if n > 1 else before
            for j, c in enumerate((cWq, cWk, cWv)):
                o = j * 256
                t = split(c[:, g * 256:(g + 1) * 256], wh[:, o:o + 256], wl[:, o:o + 256], old, W3)
            w_of[n] = t

        def parts_of_x(b, i):
            x = ch(XT, 2 * b + i)
            x_of[(b, i)] = split(x, xp[i][0], xp[i][1], tok[8 * b + i - 2]["proj"] if b else before)

        def project(m):
            b, g, i = its[m]
            Qr, Qe, KT, Ke, Vv = sets[m % 2]
            old = tok[m - 2]["done"] if m >= 2 else None
            d = tok[m] = {}
            (xh, xl), (wh, wl) = xp[i], wp_[(m // 2) % 2]
            ready = [w_of[m // 2], x_of[(b, i)]]
            wt = lambda o: (wh[:, o:o + 128], wl[:, o:o + 128])
            for h in range(2):
                k, p, fr = Rp.take()
                t = PE.do(lambda h=h, p=p, wt=wt, xh=xh, xl=xl: mm3(p, wt(256 + 128 * h), (xh, xl)), fr, ready)
                d["kt"] = t = A.do(lambda KT=KT, g=g, h=h, p=p: act(KT[:, h * 512:(h + 1) * 512], p, ACT.Relu,
                                               bias=w("cbk")[:, 2 * g + h:2 * g + h + 1]), t, old)
                Rp.free[k] = [t]
                yield
            for h in range(4):
                r0 = 64 * (h % 2)
                if h % 2 == 0:
                    k, p, fr = Rp.take()
                    t0 = PE.do(lambda h=h, p=p, wt=wt, xh=xh, xl=xl: mm3(p, wt(64 * h), (xh, xl)), fr)
                q = Qr[:, h * 512:(h + 1) * 512]
                bb = w("cbq2")[:, 4 * g + h:4 * g + h + 1]
                for r in (0, 64):
                    if h < 2:
                        t = A.do(lambda bb=bb, p=p, q=q, r=r, r0=r0: act(q[r:r + 64, :], p[r0:r0 + 64, :], ACT.Relu, bias=bb[r0:r0 + 64, :]), t0, old)
                    else:
                        t = V.do(lambda bb=bb, p=p, q=q, r=r, r0=r0: ts(q[r:r + 64, :], p[r0:r0 + 64, :], bb[r0:r0 + 64, :], 0.0, ALU.add, ALU.max), t0, old)
                d.setdefault("qr", []).append(t)
                Rp.free[k] = [t]
                d["qe"] = G.do(lambda Qe=Qe, h=h, i=i, q=q: nc.gpsimd.tensor_tensor(Qe[:, h * 512:(h + 1) * 512], q, ch(CS, i), ALU.mult), t, CSt, old)
                yield
            for c in range(4):
                k, p, fr = Rp.take()
                o, n = g * 256, 4 * i + c

                def f(KT=KT, c=c, p=p, wh=wh, wl=wl, xh=xh, xl=xl):
                    for h in range(2):
                        nc.tensor.transpose(p[:, h * 128:(h + 1) * 128], KT[:, h * 512 + c * 128:h * 512 + (c + 1) * 128], w("ident"))
                    return mm3(p[:, 256:512], (tile(xh, c), tile(xl, c)), (wh[:, 512:768], wl[:, 512:768]))
                d["proj"] = t = PE.do(f, fr, d["kt"])
                d["v"] = t1 = V.do(lambda Vv=Vv, c=c, o=o, p=p: tt(v5(Vv)[:, c, :, 0:64], g3(p[:, 256:512], 4), g3(bvr[:, o:o + 256], 4), ALU.add),
                                   t, t_one, KVt, old)
                kk = g3(p[:, 0:256], 4)
                A.do(lambda Ke=Ke, c=c, kk=kk, n=n: act(k5(Ke)[:, c, :, 0, :], kk, ACT.Copy, scale=co[:, n:n + 1]), t1)
                d["ke"] = t = A.do(lambda Ke=Ke, c=c, kk=kk, n=n: act(k5(Ke)[:, c, :, 1, :], kk, ACT.Copy, scale=co[:, 8 + n:9 + n]))
                Rp.free[k] = [t]
                yield
            if i == 0:
                weights(m // 2 + 1) if m // 2 < 15 else None
            if g == 3 and b < 3:
                parts_of_x(b + 1, i)

        am_of, sb_of = {}, {}

        def scores(s):
            m, c = divmod(s, 4)
            Qr, Qe, KT, Ke, Vv = sets[m % 2]
            d = tok[m]
            k, pa, fr = Ra.take()

            def f(KT=KT, Qr=Qr, c=c, pa=pa):
                for h in range(4):
                    r0, o = 64 * (h % 2), (h // 2) * 512 + c * 128
                    r = mm(pa[:, h % 2, h // 2, :], KT[r0:r0 + 64, o:o + 128], Qr[r0:r0 + 64, h * 512 + c * 128:h * 512 + (c + 1) * 128])
                return r
            t = PE.do(f, fr, d["qr"], d["kt"])
            ka, am, fa = AM.take()
            t = V.do(lambda am=am, pa=pa: tt(a4(am), pa, dm, ALU.mult), t, fa)
            Ra.free = [[t], [t]]
            am_of[s] = (ka, am, t)

        def state(s):
            m, c = divmod(s, 4)
            n = 4 * its[m][2] + c
            if n == 7:
                return
            Ke, Vv = sets[m % 2][3:]
            d = tok[m]
            ks, sb, fs = Sb.take()
            prev = sb_of[s - 1][2] if s else None

            def f(Ke=Ke, Vv=Vv, c=c, n=n):
                for h in range(4):
                    r = mm(Sp[:, h * 65:(h + 1) * 65], k5(Ke)[:, c, h, :, :].rearrange("p s d -> p (s d)"),
                           v5(Vv)[:, c, h, :], n == 0 and h == 0, n == 6, skip_group_check=True)
                return r
            t = PE.do(f, d["ke"], d["v"], prev)
            t = A.do(lambda sb=sb: nc.scalar.copy(sb, Sp[:, 0:260]), t, fs)
            sb_of[s] = (ks, sb, t)
            if n == 6:
                sb_of[s + 1] = (ks, sb, t)

        def outputs(s):
            m, c = divmod(s, 4)
            b, g, i = its[m]
            n = 4 * i + c
            Qr, Qe, KT, Ke, Vv = sets[m % 2]
            d = tok[m]
            ka, am, t_am = am_of[s]
            ko, po, fo = Ro.take()
            ks, sb, t_sb = sb_of[s - 1] if n else (None, None, None)

            def f(Qe=Qe, Vv=Vv, am=am, c=c, n=n, po=po, sb=sb):
                for h in range(4):
                    r = mm(po[:, h * 65:(h + 1) * 65], a4(am)[:, h % 2, h // 2, :], v5(Vv)[:, c, h, :], True, n == 0)
                    if n > 0:
                        r = mm(po[:, h * 65:(h + 1) * 65], Qe[:, h * 512 + c * 128:h * 512 + (c + 1) * 128],
                               sb[:, h * 65:(h + 1) * 65], False, True)
                return r
            t = PE.do(f, t_am, d["v"], d["qe"], t_sb, fo)
            AM.free[ka] = [t]
            if n > 0:
                Sb.free[ks] = [t]
            d["done"] = t
            o4 = po[:, 0:260].rearrange("p (h d) -> p h d", h=4)
            dn = den[s % 2]
            t = V.do(lambda dn=dn, o4=o4: ts(dn, o4[:, :, 64], 1e-6, None, ALU.max), t)
            t = V.do(lambda dn=dn: nc.vector.reciprocal(dn, dn), t)
            t = V.do(lambda c=c, dn=dn, o4=o4: tt(g3(Ok[:, c * 256:(c + 1) * 256], 4), o4[:, :, 0:64], bin_(dn, 4, 64), ALU.mult), t, fin["ok"])
            Ro.free[ko] = [t]
            d["ok"] = t

        def finish(m):
            b, g, i = its[m]
            x = ch(XT, 2 * b + i)
            for h in range(2):
                k, p, fr = Rf.take()

                def f(h=h, p=p):
                    for c in range(4):
                        r = nc.tensor.transpose(p[:, c * 128:(c + 1) * 128], Ok[:, c * 256 + h * 128:c * 256 + (h + 1) * 128], w("ident"))
                    return r
                fin["ok"] = t = PE.do(f, tok[m]["ok"], fr)
                t = A.do(lambda h=h, p=p: nc.scalar.copy(ch(OT[0], h), p), t, fin["ot"])
                t = V.do(lambda h=h, p=p: tt(ch(OT[1], h), p, ch(OT[0], h).bitcast(F32), ALU.subtract), t)
                Rf.free[k] = [t]
                yield
            k, p, fr = Rf.take()

            def f(p=p):
                for h in range(2):
                    r = mm3(p, (tile(Wo[0], h), tile(Wo[1], h)), (ch(OT[0], h), ch(OT[1], h)), h == 0, h == 1)
                return r
            fin["ot"] = t = PE.do(f, fr, t, fin["wo"])
            y = ch(XK, 2 * b + i)
            if g == 0:
                t = V.do(lambda p=p, x=x, y=y: stt(y, p, w("cbo"), x, ALU.add, ALU.add), t)
            else:
                t = V.do(lambda p=p, y=y: tt(y, p, y, ALU.add), t, tok[m]["y"])
            Rf.free[k] = [t]
            tok[m]["y1"] = t

        weights(0)
        parts_of_x(0, 0)
        parts_of_x(0, 1)
        for _ in project(0):
            pass
        scores(0)
        nf = None
        for m in range(len(its)):
            b, g, i = its[m]
            tok[m]["y"] = None
            nx = project(m + 1) if m + 1 < len(its) else None
            for c in range(4):
                s = 4 * m + c
                for j in range(3 if c < 2 else 2):
                    if nx is not None:
                        next(nx, None)
                    if j == 0 and c < 2 and nf is not None:
                        next(nf, None)
                state(s)
                if c == 0 and nf is not None:
                    next(nf, None)
                if c == 3 and nx is not None:
                    for _ in nx:
                        pass
                if s + 1 < 4 * len(its):
                    scores(s + 1)
                outputs(s)
            if nf is not None:
                for _ in nf:
                    pass
            if i == 0:
                fin["wo"] = split(cWo[:, g * 256:(g + 1) * 256], Wo[0], Wo[1], fin["ot"], W3)
            tok[m]["y"] = tok[m - 2]["y1"] if g else None
            nf = finish(m)
        for _ in nf:
            pass
        barrier()

    def softmax8(ar, lg, V8, pr):
        m, s = SM[:, 96:128], SM[:, 128:160]
        l3, p3 = g3(lg, NT), g3(pr, NT)
        t = V.do(lambda l3=l3, m=m: nc.vector.tensor_reduce(m, l3, AX, ALU.max), now())
        t = V.do(lambda l3=l3, m=m: tt(l3, l3, bin_(m, NT, 8), ALU.subtract), t)
        t = A.do(lambda lg=lg: act(lg, lg, ACT.Exp), t)
        t = V.do(lambda l3=l3, s=s: nc.vector.tensor_reduce(s, l3, AX, ALU.add), t)
        t = V.do(lambda s=s: nc.vector.reciprocal(s, s), t)
        t = V.do(lambda l3=l3, p3=p3, s=s: tt(p3[:, :, 0:8], l3, bin_(s, NT, 8), ALU.mult), t)

        def f(V8=V8, pr=pr):
            for c in range(NT):
                r = nc.vector.max(V8[:, c * 8:c * 8 + 8], pr[:, c * 16:c * 16 + 8])
            return r
        return V.do(f, t)

    def router(lg, bias):
        p = PS[7][:, 0:256]
        if bias is None:
            return V.do(lambda lg=lg, p=p: nc.vector.tensor_copy(lg, p), ready["lg"])
        return V.do(lambda bias=bias, lg=lg, p=p: tt(g3(lg, NT), g3(p, NT), bias.unsqueeze(1).to_broadcast([128, NT, 8]), ALU.add), ready["lg"], wtok(6))

    def to_rows(WK, WT, Rt, i, tw):
        k, p, fr = Rt.take()

        def f(WK=WK, i=i, p=p):
            for j in range(4):
                c = 4 * i + j
                r = nc.tensor.transpose(p[0:8, j * 128:(j + 1) * 128], WK[:, c * 8:c * 8 + 8], w("ident"))
            return r
        t = PE.do(f, fr, tw)
        t = A.do(lambda WT=WT, i=i, p=p: nc.scalar.copy(ch(WT, i)[0:8, :], p[0:8, :]), t, tw)
        t = V.do(lambda WT=WT, i=i, p=p: tt(ch(WT, i)[32:40, :], p[0:8, :], ch(WT, i)[0:8, :].bitcast(F32), ALU.subtract), t)
        Rt.free[k] = [t]
        return t

    def split_weights(ar, nu, nd, Wup, Wdn, wsem):
        assert ar.o == XP
        ar.o += 2 * T
        E = dict(x=ready["x"], t_x=ready["t_x"], wts={})
        nw = nu + nd
        E["Rw"] = Rw = Ring([(ar(nw * 128, dt=FR), ar(nw * 128, dt=FR)) for _ in range(2)])
        E["s8"] = s8r = ar(8, 40, FR)
        E["t_s8"] = V.do(lambda s8r=s8r: nc.vector.tensor_copy(s8r, w("sel16r")))

        def weights(e):
            k, (wh, wl), fr = Rw.take()
            V.do(lambda e=e, wh=wh: nc.vector.tensor_copy(wh[:, 0:nu * 128], Wup(e)), fr, wsem)
            t = V.do(lambda e=e, wh=wh: nc.vector.tensor_copy(wh[:, nu * 128:], Wdn(e)))
            t = V.do(lambda e=e, wh=wh, wl=wl: tt(wl[:, 0:nu * 128], Wup(e), wh[:, 0:nu * 128].bitcast(F32), ALU.subtract), t)
            t = V.do(lambda e=e, wh=wh, wl=wl: tt(wl[:, nu * 128:], Wdn(e), wh[:, nu * 128:].bitcast(F32), ALU.subtract))
            E["wts"][e] = (k, wh, wl, t)

        E["weights"] = weights
        weights(0)
        return E

    def experts(E, ar, ax, WK, WT, t_w, b2, up, nu, nd, banks, ahead):
        (xh, xl), t_x, wts, Rw, s8r, t_s8 = (E[n] for n in ("x", "t_x", "wts", "Rw", "s8", "t_s8"))
        Rh = Ring([(ar(512, dt=FR), ar(512, dt=FR)) for _ in range(ahead + 2)])
        Rb, Ro = Ring(PS[0:1]), Ring(banks)
        Rg = Ring([ax(512) for _ in range(2)])
        Rv = Ring([ax(512) for _ in range(2)])
        t_acc, pend, o_of = {}, [], {}

        def down(e, i, c, kh, h, th):
            kw, wh, wl, tw = wts[e]
            if c == 0:
                t = rows[i]
                k, pb, fb = Rb.take()
                kg, gb, fg = Rg.take()
                t = PE.do(lambda e=e, i=i, pb=pb: mm(pb, s8r[:, e:e + 1].to_broadcast([40, 128]), ch(WT, i)[0:40, :]), fb, t, t_s8)
                t = A.do(lambda gb=gb, pb=pb: nc.scalar.copy(gb, pb), t, fg)
                Rb.free[k] = [t]
                gates[(e, i)] = (kg, gb, t)
                if e == 0 and i + 1 < NCH:
                    rows.append(to_rows(WK, WT, Rb, i + 1, t_w))
                o_of[(e, i)] = Ro.take()
            ko, o, fo = o_of[(e, i)]
            cc = (nu + c) * 128
            t = PE.do(lambda c=c, cc=cc, h=h, o=o, wh=wh, wl=wl: mm3(o, (wh[:, cc:cc + 128], wl[:, cc:cc + 128]), h, c == 0, c == nd - 1), th, fo if c == 0 else None)
            Rh.free[kh] = [t]
            if c == nd - 1:
                Rw.free[kw] = [t]
                kg, gb, tg = gates[(e, i)]
                kv, v, fv = Rv.take()
                if b2 is None:
                    t = V.do(lambda gb=gb, o=o, v=v: tt(v, o, gb, ALU.mult), t, tg, fv)
                else:
                    t = V.do(lambda e=e, gb=gb, o=o, v=v: stt(v, o, b2[:, e:e + 1], gb, ALU.add, ALU.mult), t, tg, fv)
                Ro.free[ko] = Rg.free[kg] = [t]
                x = ch(XT, i)
                t_acc[i] = t = G.do(lambda v=v, x=x: nc.gpsimd.tensor_tensor(x, x, v, ALU.add), t, t_x[i], t_acc.get(i))
                Rv.free[kv] = [t]

        def parts(e, i, c, rest):
            kh, h, fh = Rh.take()
            pend.append((e, i, c, kh, h, rest(h, fh)))

        gates, second = {}, []
        rows = [to_rows(WK, WT, Rb, 0, t_w)]
        for e in range(8):
            for i in range(NCH):
                for c in range(nd):
                    kw, wh, wl, tw = wts[e]
                    second.append((e, i, c, up(e, i, c, (ch(xh, i), ch(xl, i)), (wh, wl), [tw, t_x[i]])))
                    if len(second) > 1:
                        parts(*second.pop(0))
                    if len(pend) > ahead - 1:
                        down(*pend.pop(0))
                if i == 1 and e + 1 < 8:
                    E["weights"](e + 1)
        parts(*second.pop(0))
        for q in pend:
            down(*q)
        barrier()

    def stage6():
        ar, ax = Arena(), Arena(XKt, XKr, T)
        lg, V8, pr, R = ax(256), ax(256), ax(NT * 16), ax(NT * 16)
        rp = ax(256)
        WT, WK = ar(T, 40, FR), ar(256)
        s2 = SM[:, 160:192]
        w13, w2e = w("w13"), w("w2e")
        E = split_weights(ar, 4, 2, lambda e: w13[:, e * 512:(e + 1) * 512], lambda e: w2e[:, e * 256:(e + 1) * 256], wtok(4))
        t_z = G.do(lambda WT=WT: nc.gpsimd.memset(WT.bitcast(F32), 0.0))
        router(lg, None)
        tp = V.do(lambda pr=pr: nc.vector.memset(pr, FILL))
        tv = softmax8(ax, lg, V8, pr)
        v3 = g3(V8, NT)
        t = V.do(lambda s2=s2, v3=v3: stt(s2, v3[:, :, 0], 1e-6, v3[:, :, 1], ALU.add, ALU.add), tv)
        t_s = V.do(lambda s2=s2: nc.vector.reciprocal(s2, s2), t)
        t = V.do(lambda rp=rp: nc.vector.memset(rp, FILL))
        t = V.do(lambda rp=rp, v3=v3: nc.vector.tensor_copy(g3(rp, NT)[:, :, 0:2], v3[:, :, 0:2]), t)

        def f(R=R, pr=pr, rp=rp):
            for c in range(NT):
                r = nc.vector.match_replace(R[:, c * 16:c * 16 + 16], rp[:, c * 8:c * 8 + 8], pr[:, c * 16:c * 16 + 16], FILL)
            return r
        t = V.do(f, t)
        r3, q3, w3 = g3(R, NT)[:, :, 0:8], g3(pr, NT)[:, :, 0:8], g3(WK, NT)
        t = V.do(lambda q3=q3, r3=r3, w3=w3: tt(w3, r3, q3, ALU.not_equal), t)
        t = V.do(lambda q3=q3, w3=w3: tt(w3, w3, q3, ALU.mult), t)
        t = V.do(lambda s2=s2, w3=w3: tt(w3, w3, bin_(s2, NT, 8), ALU.mult), t, t_s)
        t_w = [t, t_z]
        barrier()
        ax = Arena(XKt, XKr, T)
        Rs, Rf = Ring([ar(512) for _ in range(2)]), Ring([ar(512) for _ in range(3)])
        Rp = Ring([(PS[1], PS[2]), (PS[3], PS[4]), (PS[5], PS[6])])

        def up(e, i, c, x, wt, deps):
            k, (pg, pu), fr = Rp.take()
            a, b = c * 128, (2 + c) * 128
            t1 = PE.do(lambda a=a, pg=pg, wt=wt, x=x: mm3(pg, (wt[0][:, a:a + 128], wt[1][:, a:a + 128]), x), fr, deps)
            t2 = PE.do(lambda b=b, pu=pu, wt=wt, x=x: mm3(pu, (wt[0][:, b:b + 128], wt[1][:, b:b + 128]), x))
            ks, s, fs = Rs.take()
            kf, q, ff = Rf.take()
            t1 = A.do(lambda pg=pg, s=s: act(s, pg, ACT.Silu), t1, fs)
            t = V.do(lambda pu=pu, q=q, s=s: tt(q, pu, s, ALU.mult), t1, t2, ff)
            Rp.free[k] = Rs.free[ks] = [t]

            def rest(h, fh):
                t2 = A.do(lambda h=h: nc.scalar.copy(h[0], q), t, fh)
                t2 = (G.do(lambda h=h: nc.gpsimd.tensor_tensor(h[1], q, h[0].bitcast(F32), ALU.subtract), t2) if c % 2 else
                      V.do(lambda h=h: tt(h[1], q, h[0].bitcast(F32), ALU.subtract), t2))
                Rf.free[kf] = [t2]
                return t2
            return rest
        experts(E, ar, ax, WK, WT, t_w, None, up, 4, 2, PS[7:8], 3)

    def stage7():
        W5 = wtok(5)
        ss, rs, sd = SM[:, 0:32], SM[:, 32:64], SM[:, 212:244]
        negA, car, carx = SM[:, 244:276], SM[:, 276:308], SM[:, 308:314]
        eps = SM[:, 479:480]
        ar = Arena()
        Rj = Ring([ar(512) for _ in range(2)])
        Rt = Ring(PS[0:2])
        t_A = A.do(lambda negA=negA: act(negA, w("Alog"), ACT.Exp), W5)
        t_A = V.do(lambda negA=negA: ts(negA, negA, -1.0, None, ALU.mult), t_A)
        pend = []

        def normed(i, k, p, t):
            t = V.do(lambda i=i, p=p: ts(ch(XK, i), p, w("normw"), None, ALU.mult), t)
            Rt.free[k] = [t]

        for i in range(NCH):
            kj, jk, fj = Rj.take()
            o = slice(4 * i, 4 * i + 4)

            def f(i=i, jk=jk, ss=ss):
                for j in range(4):
                    c = 4 * i + j
                    r = act(jk[:, j * 128:(j + 1) * 128], tile(XK, c), ACT.Square, scale=128 ** -0.5, acc=ss[:, c:c + 1])
                return r
            t = A.do(f, fj)
            Rj.free[kj] = [t]
            t = A.do(lambda eps=eps, o=o, sd=sd, ss=ss: act(sd[:, o], ss[:, o], ACT.Sqrt, bias=eps), t, t_eps)
            t = V.do(lambda o=o, rs=rs, sd=sd: nc.vector.reciprocal(rs[:, o], sd[:, o]), t)
            t = V.do(lambda i=i, o=o, rs=rs: tt(g3(ch(XK, i), 4), g3(ch(XK, i), 4), bin_(rs[:, o], 4, 128), ALU.mult), t)
            k, p, fr = Rt.take()

            def f(i=i, p=p):
                for j in range(4):
                    r = nc.tensor.transpose(p[:, j * 128:(j + 1) * 128], tile(XK, 4 * i + j), w("ident"))
                return r
            t = PE.do(f, t, fr)
            Rt.free[k] = []
            pend.append((i, k, p, t))
            if len(pend) > 1:
                normed(*pend.pop(0))
        normed(*pend.pop(0))
        barrier()
        ar = Arena()
        sets = [tuple(ar(1024) for _ in range(4)) for _ in range(2)]
        ev = ar(1024)
        xe = [ar(515), ar(515)]
        d1 = ar(512, 64)
        Rb, Ru, Ra, Rh, Rc = Ring([ar(512) for _ in range(3)]), Ring([ar(512) for _ in range(6)]), Ring([ar(512) for _ in range(6)]), \
            Ring([ar(512) for _ in range(4)]), Ring([ar(512) for _ in range(4)])
        Bp, Cp = Ring(PS[0:1]), Ring(PS[1:4])
        Yp = PS[4:6]
        Rp = Ring(PS[6:8])
        skT, inT, cw, cb = w("skT"), w("inT"), SM[:, 320:328], SM[:, 328:330]
        V.do(lambda cw=cw: ts(cw, w("convw"), 0.5, None, ALU.mult))
        zero = SM[:, 330:333]
        t_zero = V.do(lambda zero=zero: nc.vector.memset(zero, 0.0))
        t_ev = [V.do(lambda cb=cb: ts(cb, w("convb"), 0.5, None, ALU.mult))]
        BCs = [ar(512, 64, FR), ar(512, 64, FR)]
        s2 = ar(32, 64, FR)
        t_s2 = V.do(lambda s2=s2: nc.vector.tensor_copy(s2, w("ss2")))
        tok = {}

        def prepare(i):
            first = i % 2 == 0
            sk, xs, dl, dx = sets[i % 2]
            BC = BCs[i % 2]
            old = tok[i - 2]["done"] if i >= 2 else None
            xn = ch(XK, i)
            d = tok[i] = {}
            c_ = {}

            def open_(e):
                k, p, fr = Rp.take()
                t = PE.do(lambda e=e, p=p: mm(p, tile(skT, e), xn), fr)
                t_sk = A.do(lambda e=e, p=p: act(ch(sk, e), p, ACT.Tanh, scale=0.5), t, old)
                k2, p2, fr = Rp.take()
                t = PE.do(lambda e=e, p2=p2: mm(p2, tile(inT, e), xn), fr)
                pc = tok[i - 1]["conv"] if i else None
                t2 = A.do(lambda e=e: nc.scalar.copy(xe[e][:, 0:3], zero if first else carx[:, 3 * e:3 * e + 3]), pc, c_.get("car"), t_zero)
                t = A.do(lambda e=e, p2=p2: nc.scalar.copy(xe[e][:, 3:515], p2), t, pc)
                Rp.free[k2] = [t]
                t3 = A.do(lambda e=e: nc.scalar.copy(carx[:, 3 * e:3 * e + 3], xe[e][:, 512:515]), t, t2)
                v = ch(ev, e)
                t = A.do(lambda e=e, v=v: act(v, xe[e][:, 0:512], ACT.Identity, scale=cw[:, 4 * e:4 * e + 1], bias=cb[:, e:e + 1]), t, t2, t_ev[0])
                c_[e] = (k, p, t_sk, v, t, t3)

            def taps(e, j, t):
                v = c_[e][3]
                return V.do(lambda e=e, j=j, v=v: stt(v, xe[e][:, j:j + 512], cw[:, 4 * e + j:4 * e + j + 1], v, ALU.mult, ALU.add), t)

            def gate(e):
                k, p, t_sk, v, t_v, t3 = c_[e]
                t = V.do(lambda e=e, p=p: stt(ch(sk, e), ch(sk, e), 1.0, p, ALU.add, ALU.mult), t_sk)
                Rp.free[k] = [t]
                c_[e, "t"] = taps(e, 2, taps(e, 1, t_v))

            def last(e):
                v = c_[e][3]
                t = taps(e, 3, c_[e, "t"])
                d.setdefault("conv", []).extend([t, c_[e][5]])
                c_[e, "t"] = A.do(lambda e=e, v=v: act(ch(xs, e), v, ACT.Tanh), t, old)

            def shut(e):
                v = c_[e][3]
                c_[e, "x"] = V.do(lambda e=e, v=v: stt(ch(xs, e), ch(xs, e), 1.0, v, ALU.add, ALU.mult), c_[e, "t"])

            open_(0)
            yield
            gate(0)
            yield
            open_(1)
            last(0)
            yield
            shut(0)
            gate(1)
            yield
            last(1)
            yield
            shut(1)
            k, p, fr = Rp.take()

            def f(p=p, xs=xs):
                for e in range(2):
                    r = mm(p[0:64, :], w("wd1T")[:, e * 64:(e + 1) * 64], ch(xs, e), e == 0, e == 1)
                return r
            t = PE.do(f, c_[0, "x"], c_[1, "x"], fr)
            yield
            t_d1 = V.do(lambda p=p: nc.vector.tensor_copy(d1, p[0:64, :]), t, tok[i - 1]["d1"] if i else None)
            Rp.free[k] = [t_d1]
            k, p2, fr = Rp.take()

            def f(p2=p2, xs=xs):
                for e in range(2):
                    r = mm(p2[0:32, :], w("wbcT")[:, e * 32:(e + 1) * 32], ch(xs, e), e == 0, e == 1)
                return r
            t = PE.do(f, fr)
            yield
            k3, p3, fr = Rp.take()
            t_p = PE.do(lambda p3=p3: mm(p3, w("wd2T")[:, 0:128], d1), t_d1, fr)
            t = V.do(lambda BC=BC, p2=p2: nc.vector.tensor_copy(BC[0:32, :], p2[0:32, :]), t, old)
            t_bc = V.do(lambda BC=BC, p2=p2: tt(BC[32:64, :], p2[0:32, :], BC[0:32, :].bitcast(F32), ALU.subtract), t)
            Rp.free[k] = [t_bc]
            d["bc"] = t_bc
            yield
            for e in range(2):
                t2 = V.do(lambda dl=dl, e=e, p3=p3: ts(ch(dl, e), p3, w("wd2b")[:, e:e + 1], 0.0, ALU.add, ALU.max), t_p, old)
                t1 = A.do(lambda e=e, p3=p3: act(ch(ev, e), p3, ACT.Abs, bias=w("wd2b")[:, e:e + 1]), t2, c_[e, "x"])
                Rp.free[k3] = [t1]
                if e == 0:
                    k3, p3, fr = Rp.take()
                    t_p = d["d1"] = PE.do(lambda p3=p3: mm(p3, w("wd2T")[:, 128:256], d1), fr)
                yield
            t = A.do(lambda: act(ev, ev, ACT.Exp, scale=-1.0), t1)
            t = A.do(lambda: act(ev, ev, ACT.Ln, bias=1.0), t)
            yield
            d["dl"] = t_ev[0] = t = V.do(lambda dl=dl: tt(dl, dl, ev, ALU.add), t, t2)
            d["dx"] = G.do(lambda dl=dl, dx=dx, xs=xs: nc.gpsimd.tensor_tensor(dx, dl, xs, ALU.mult), t)

        st = {}

        def head(g):
            i, n = divmod(g, 16)
            sk, xs, dl, dx = sets[i % 2]
            BC = BCs[i % 2]
            d, s = tok[i], {}
            kb, pb, fb = Bp.take()
            kc, pc, fc = Cp.take()
            t = PE.do(lambda BC=BC, n=n, pb=pb: mm(pb, s2[:, n:n + 1].to_broadcast([64, 128]), BC), d["bc"], fb, t_s2)
            s["c"] = PE.do(lambda BC=BC, n=n, pc=pc: mm(pc, s2[:, 16 + n:17 + n].to_broadcast([64, 128]), BC), fc)
            kB, Bs, fB = Rb.take()
            t_b = A.do(lambda Bs=Bs, pb=pb: nc.scalar.copy(Bs, pb), t, fB)
            Bp.free[kb] = [t_b]
            s["pc"], s["kc"] = pc, kc
            for e in range(2):
                q = e * 16 + n
                ka, a, fa = Ra.take()
                t_a = A.do(lambda a=a, dl=dl, e=e, q=q: act(a, ch(dl, e), ACT.Exp, scale=negA[:, q:q + 1]), d["dl"], fa, t_A)
                ku, u, fu = Ru.take()
                t_u = G.do(lambda Bs=Bs, dx=dx, e=e, u=u: nc.gpsimd.tensor_tensor(u, ch(dx, e), Bs, ALU.mult), t_b, d["dx"], fu)
                s[e] = (ka, a, t_a, ku, u, t_u)
            Rb.free[kB] = [t_u]
            st[g] = s

        def body(g):
            i, n = divmod(g, 16)
            s = st[g]
            for e in range(2):
                q = e * 16 + n
                ka, a, t_a, ku, u, t_u = s[e]
                kh, h, fh = Rh.take()
                ini = 0.0 if i % 2 == 0 else car[:, q:q + 1]
                t_h = V.do(lambda a=a, h=h, ini=ini, u=u: nc.vector.tensor_tensor_scan(h, a, u, ini, ALU.mult, ALU.add), t_a, t_u, fh,
                           st[g - 16]["cr"] if i % 2 else None)
                Ra.free[ka] = Ru.free[ku] = [t_h]
                s[e] = (kh, h, t_h)
            for e in range(2):
                kh, h, t_h = s[e]
                kC, hc, fC = Rc.take()
                t_hc = V.do(lambda h=h, hc=hc, s=s: tt(hc, s["pc"], h, ALU.mult), t_h, s["c"], fC)
                q = e * 16 + n
                if i % 2 == 0:
                    s["cr"] = t_cr = G.do(lambda h=h, q=q: nc.gpsimd.tensor_copy(car[:, q:q + 1], h[:, 511:512]), t_h, t_A)
                    Rh.free[kh] = [t_hc, t_cr]
                else:
                    Rh.free[kh] = [t_hc]
                s[e] = (kC, hc, t_hc)
            Cp.free[s["kc"]] = [t_hc]

        t_z = [None]

        def tail(g):
            i, n = divmod(g, 16)
            s = st[g]
            for e in range(2):
                kC, hc, t_hc = s[e]
                t_y = PE.do(lambda e=e, hc=hc, n=n: mm(Yp[e], w("ident"), hc, n == 0, n == 15), t_hc, t_z[0] if n == 0 else None)
                Rc.free[kC] = [t_y]
            if n == 15:
                sk, xs, dl, dx = sets[i % 2]
                for e in range(2):
                    z = ch(dl, e)
                    t = t_z[0] = V.do(lambda e=e, xs=xs, z=z: stt(z, ch(xs, e), w("WD")[:, e:e + 1], Yp[e], ALU.mult, ALU.add), t_y, s["a"])
                    t = V.do(lambda e=e, sk=sk, z=z: stt(z, z, 0.5, ch(sk, e), ALU.mult, ALU.mult), t)
                k, p, fr = Rp.take()

                def f(dl=dl, p=p):
                    for e in range(2):
                        r = mm(p, w("outT")[:, e * 128:(e + 1) * 128], ch(dl, e), e == 0, e == 1)
                    return r
                tok[i]["done"] = t = PE.do(f, t, fr)
                out_[0] = (i, k, p, t)

        out_ = [None]

        def result():
            i, k, p, t = out_[0]
            t = V.do(lambda i=i, p=p: stt(ch(XT, i), ch(XT, i), 2.0, p, ALU.mult, ALU.add), t)
            Rp.free[k] = [t]
            out_[0] = None

        for _ in prepare(0):
            pass
        GN = NCH * 16
        nxt = None
        for g in range(-2, GN + 1):
            if g + 2 < GN:
                head(g + 2)
                st[g + 2]["a"] = (A.sem, A.n)
            if 0 <= g < GN:
                body(g)
            if out_[0]:
                result()
            if 0 <= g - 1 < GN:
                tail(g - 1)
            if g >= 0 and g % 16 == 1 and g // 16 + 1 < NCH:
                nxt = prepare(g // 16 + 1)
            if nxt is not None and g % 16 != 0:
                next(nxt, None)
        result()
        barrier()

    def stage8():
        ar, ax = Arena(), Arena(XKt, XKr, T)
        lg, V8, pr, R = ax(256), ax(256), ax(NT * 16), ax(NT * 16)
        rp, cum = ax(256), ax(256)
        WT, WK = ar(T, 40, FR), ar(256)
        W1, W2, B1, B2 = w("W1"), w("W2"), w("B1"), w("B2")
        E = split_weights(ar, 4, 4, lambda e: W1[:, e * 512:(e + 1) * 512], lambda e: W2[:, e * 512:(e + 1) * 512], wtok(6))
        t_z = G.do(lambda WT=WT: nc.gpsimd.memset(WT.bitcast(F32), 0.0))
        router(lg, w("brr"))
        V.do(lambda pr=pr: nc.vector.memset(pr, FILL))
        tv = softmax8(ax, lg, V8, pr)
        v3, c3 = g3(V8, NT), g3(cum, NT)
        t = V.do(lambda c3=c3, v3=v3: nc.vector.tensor_copy(c3[:, :, 0], v3[:, :, 0]), tv)
        for j in range(1, 8):
            t = V.do(lambda c3=c3, v3=v3, j=j: tt(c3[:, :, j], c3[:, :, j - 1], v3[:, :, j], ALU.add), t)
        t = V.do(lambda cum=cum: ts(cum, cum, 0.8, None, ALU.is_lt), t)
        t = V.do(lambda c3=c3: nc.vector.memset(c3[:, :, 0:1], 1.0), t)
        t = V.do(lambda V8=V8, cum=cum, rp=rp: tt(rp, V8, cum, ALU.mult), t)
        t = V.do(lambda cum=cum: ts(cum, cum, -FILL, FILL, ALU.mult, ALU.add), t)
        t = V.do(lambda cum=cum, rp=rp: tt(rp, rp, cum, ALU.add), t)

        def f(R=R, pr=pr, rp=rp):
            for c in range(NT):
                r = nc.vector.match_replace(R[:, c * 16:c * 16 + 16], rp[:, c * 8:c * 8 + 8], pr[:, c * 16:c * 16 + 16], FILL)
            return r
        t = V.do(f, t)
        r3, q3, w3 = g3(R, NT)[:, :, 0:8], g3(pr, NT)[:, :, 0:8], g3(WK, NT)
        t = V.do(lambda q3=q3, r3=r3, w3=w3: tt(w3, r3, q3, ALU.not_equal), t)
        t = V.do(lambda q3=q3, w3=w3: tt(w3, w3, q3, ALU.mult), t)
        t_w = [t, t_z]
        barrier()
        ax = Arena(XKt, XKr, T)
        Rr = Ring([ax(512) for _ in range(4)])
        Rp = Ring(PS[1:6])

        def up(e, i, c, x, wt, deps):
            k, p, fr = Rp.take()
            n, a = 4 * e + c, c * 128
            t = PE.do(lambda a=a, p=p, wt=wt, x=x: mm3(p, (wt[0][:, a:a + 128], wt[1][:, a:a + 128]), x), fr, deps)
            kr, r, fe = Rr.take()
            if c % 2:
                t = V.do(lambda n=n, p=p, r=r: ts(r, p, B1[:, n:n + 1], 0.0, ALU.add, ALU.max), t, fe)
            else:
                t = A.do(lambda n=n, p=p, r=r: act(r, p, ACT.Relu, bias=B1[:, n:n + 1]), t, fe)
            Rp.free[k] = [t]

            def rest(h, fh):
                if c % 2:
                    t2 = A.do(lambda h=h: nc.scalar.copy(h[0], r), t, fh)
                else:
                    t2 = V.do(lambda h=h: nc.vector.tensor_copy(h[0], r), t, fh)
                if c % 2:
                    t2 = G.do(lambda h=h: nc.gpsimd.tensor_tensor(h[1], r, h[0].bitcast(F32), ALU.subtract), t2)
                else:
                    t2 = V.do(lambda h=h: tt(h[1], r, h[0].bitcast(F32), ALU.subtract), t2)
                Rr.free[kr] = [t2]
                return t2
            return rest
        experts(E, ar, ax, WK, WT, t_w, B2, up, 4, 4, PS[6:8], 4)

    stages = [stage1, stage2, stage3, stage4, stage5, stage6, stage7, stage8]
    late_at = (0, ())
    route = {5: (w("rwT"), wtok(3)), 7: (w("Wr"), wtok(6))}
    for k in range(1, 9):
        stages[k - 1]()
        if k == 5:
            late_at = (len(S.items), (now(),))
        r, wt = route.get(k, (None, None)) if k < 8 else (None, None)
        layernorm(last=(k == 8), src=XK if k == 5 else XT, route=r, wt=wt)

    loads, late, src = [], None, 0
    for g, (a, b) in enumerate(spans):
        f = lambda a=a, b=b, c=src: nc.sync.dma_start(W[:, a:b], wp[:, c:c + b - a])
        src += b - a
        if g == LATE:
            late = (f, late_at[1] + tuple((s_w[j], 16) for j in (1, 2, 3)), s_w[g], 16)
        loads.append((f, (), s_w[g], 16))
    S.items.insert(late_at[0], late)
    xs = [(lambda b=b: nc.sync.dma_start(ch(XT, b, L), xT_d[:, b * L:(b + 1) * L]), (), s_x[b], 16) for b in range(NB)]
    S.items[:0] = [loads[0]] + xs + [loads[g] for g in ORDER[1:]]
    S.items.append((None, [(s_out, 16 * NCH)], None, 0))

    block = ctx.enter_context(nc.Block())

    @block.tensor
    def _(e):
        PE.emit(e)

    @block.vector
    def _(e):
        V.emit(e)

    @block.scalar
    def _(e):
        A.emit(e)

    @block.gpsimd
    def _(e):
        G.emit(e)

    @block.sync
    def _(e):
        S.emit(e)

    ctx.close()


def constants():
    p = np.arange(128)
    c = {}
    c["ss2"] = np.concatenate([np.eye(32), np.eye(32)], 0)
    c["sel16r"] = np.concatenate([np.eye(8), np.zeros((24, 8)), np.eye(8)], 0)
    c["ident"] = np.eye(128)
    c["cen"] = np.eye(128) - 1.0 / 128
    c["ones"] = np.ones((128, 128))
    c["one64"] = np.full((64, 1), 1.0 / 64)
    c["hm"] = (p[:, None] // 8 == np.arange(16)[None]) * 1.0
    r = np.arange(112)
    c["hmT"] = (r[:, None] % 16 == p[None] // 8) * 1.0
    e = np.zeros((64, 4, 112))
    for b in range(4):
        for j in range(112):
            e[b * 16 + j % 16, b, j] = 1
    c["E64"] = e.reshape(64, -1)
    c["ucol"] = r[:, None] // 16 + 7.0 * np.arange(5)[None] + 1
    c["tokid"] = p[:, None] + 128.0 * np.arange(8)[None]
    c["iotau"] = np.broadcast_to((np.arange(560) // 16 + 1.0)[None], (128, 560))
    th = np.float32(np.pi / 2048) * np.arange(1024, dtype=np.float32)
    co, si = np.cos(th, dtype=np.float32), np.sin(th, dtype=np.float32)
    d = np.pi / 2048 * (p[None, :] - p[:, None])
    c["dmask"] = np.where(p[None, :] >= p[:, None], np.cos(d), 0.0)
    c["coss"] = np.concatenate([co.reshape(8, 128).T, si.reshape(8, 128).T], 1)
    c = {k: np.asarray(v, np.float32) for k, v in c.items()}
    cs = np.concatenate([np.broadcast_to(co, (64, 1024)), np.broadcast_to(si, (64, 1024))], 0).astype(np.float32)
    return c, np.ascontiguousarray(cs)


def kernel(**inputs):
    from concourse import bacc as _bacc
    from concourse.bass_utils import run_bass_kernel_spmd as _run
    I = {k: np.asarray(v) for k, v in inputs.items()}
    c, cs = constants()
    P = dict(c)
    col = lambda a: a.reshape(-1, 128).T
    rep = lambda a, n=128: np.broadcast_to(a.reshape(1, -1), (n, a.size))
    ck = lambda a: a.reshape(-1, 128, a.shape[-1]).transpose(1, 0, 2).reshape(128, -1)
    for l in range(2):
        P[f"Wz{l}"], P[f"Wh{l}"] = I[f"L0_attn_Wz{l}"].T, I[f"L0_attn_Wh{l}"].T
    P["b_l0a"] = np.stack([I["L0_attn_" + n] for n in ("bz0", "bh0", "bz1", "bh1")], 1)
    f = lambda n: I["L0_ffn_" + n]
    P["slot"], P["slotT"] = f("slot_init"), f("slot_init").T
    P["w1"] = ck(f("w1"))
    P["w2"], P["WihT"], P["WhhT"] = f("w2"), f("Wih").T, f("Whh").T
    for n in ("wq", "wk", "wv", "wvp", "wo"):
        P[n] = f(n)
    P["b1"], P["b2r"], P["tau"] = f("b1")[:, None], rep(f("b2")), rep(f("tau"))
    P["bih"], P["bhh"], P["bq"], P["bk"] = col(f("bih")), col(f("bhh")), f("bq")[:, None], f("bk")[:, None]
    P["bvr"], P["lng"], P["lnb"], P["bvp"], P["bo"] = rep(f("bv"), 64), col(f("ln_g")), col(f("ln_b")), col(f("bvp")), col(f("bo"))
    f = lambda n: I["L1_attn_" + n]
    for n in ("Wq", "Wk", "Wv", "Wo"):
        P["a" + n] = f(n)
    P["abq"], P["abk"], P["abvr"], P["abo"] = col(f("bq")), col(f("bk")), rep(f("bv")), col(f("bo"))
    f = lambda n: I["L1_ffn_" + n]
    P["gate0"], P["gate1"] = (np.broadcast_to(f("gate_w")[e][:, None], (128, 128)) for e in range(2))
    P["fw1"] = f("w1").transpose(1, 0, 2).reshape(128, -1)
    P["fb1"], P["fw2"] = col(f("b1")), ck(f("w2").reshape(1024, 128))
    P["fb2"], P["sw1"], P["sb1"], P["sw2"], P["sb2"] = col(f("b2")), f("sw1"), col(f("sb1")), ck(f("sw2")), col(f("sb2"))
    f = lambda n: I["L2_attn_" + n]
    P["cWq"], P["cWk"], P["cWv"], P["cWo"] = f("Wq"), f("Wk"), f("Wv"), ck(f("Wo"))
    bq = f("bq").reshape(16, 64).T
    P["cbq2"], P["cbk"], P["cbo"] = np.concatenate([bq, bq], 0), col(f("bk")), col(f("bo"))
    P["rwT"] = I["L2_ffn_router_w"].T
    P["w13"] = I["L2_ffn_w13"].transpose(1, 0, 2).reshape(128, -1)
    P["w2e"] = ck(I["L2_ffn_w2"].reshape(2048, 128))
    f = lambda n: I["L3_attn_" + n]
    P["normw"], P["skT"], P["inT"] = col(f("norm_w")), f("skip_w").T, f("in_w").T
    P["convw"], P["convb"] = ck(f("conv_w").reshape(256, 4)), col(f("conv_b"))
    P["wd1T"], P["wd2T"], P["wd2b"] = ck(f("wd1").T), f("wd2").T, col(f("wd2_b"))
    P["wbcT"] = ck(np.concatenate([f("wb"), f("wc")], 0).T)
    P["Alog"], P["WD"], P["outT"] = ck(f("A_log")), col(f("W_D")), ck(f("out_w").T)
    f = lambda n: I["L3_ffn_" + n]
    P["Wr"], P["brr"] = f("Wr"), rep(f("br"))
    P["W1"], P["B1"] = f("W1").transpose(1, 0, 2).reshape(128, -1), col(f("b1"))
    P["W2"], P["B2"] = ck(f("W2").reshape(4096, 128)), col(f("b2"))

    cols = []
    for g in GROUPS:
        for name, r, n in g:
            a = P[name]
            assert a.shape == (r, n) and a.dtype == np.float32, (name, a.shape, a.dtype)
            if r < 128:
                a = np.concatenate([a, np.zeros((128 - r, n), np.float32)], 0)
            cols.append(a)
    x = I["L0_attn_x"]
    arrays = {
        "wp": np.ascontiguousarray(np.concatenate(cols, 1)),
        "xT": np.ascontiguousarray(x.reshape(T, D).T),
        "sidx": np.ascontiguousarray(I["L1_attn_sample_idx"].reshape(1, 35)),
        "cs": cs,
        "bkv": np.ascontiguousarray(np.stack([I["L2_attn_bk"], I["L2_attn_bv"]], 0)),
    }
    nc = _bacc.Bacc("TRN2", target_bir_lowering=False, num_devices=1)
    h = {}
    for k, a in arrays.items():
        h[k] = nc.dram_tensor(k, a.shape, mybir.dt.from_np(a.dtype), kind="ExternalInput").ap()
    out = nc.dram_tensor("out", (NB, L, D), F32, kind="ExternalOutput").ap()
    build(nc, h["wp"], h["xT"], h["sidx"], h["cs"], h["bkv"], out)
    r = _run(nc, [arrays], core_ids=[0])
    return r.results[0]["out"]
```
